# Optimizing a Trainium2 kernel written in Bass

```python
import numpy as np
import jax
import jax.numpy as jnp

def _softmax(x, axis=-1):
    return jax.nn.softmax(x, axis=axis)

def _gelu(x):
    return jax.nn.gelu(x, approximate=True)

def _silu(x):
    return jax.nn.silu(x)

def _sigmoid(x):
    return jax.nn.sigmoid(x)

def _layernorm(x, axis=-1, eps=1e-05):
    m = jnp.mean(x, axis=axis, keepdims=True)
    v = jnp.var(x, axis=axis, keepdims=True)
    return (x - m) / jnp.sqrt(v + eps)

def _scatter_add(tgt, idx, src, axis=0):
    return tgt.at[idx].add(src)

def _segment_sum(src, seg, n):
    return jax.ops.segment_sum(src, seg, n)
kernel_name = 'mk_adaln_d1_jaxref_r8_3d2d8e'

def setup_inputs(seed: int=0):
    np.random.seed(seed)
    _w = jnp.asarray

    def _L0_attn_setup():
        import jax, jax.numpy as jnp
        import numpy as np
        B_, S_, E_ = (1, 256, 256)
        NH, P_, N_, G_, K_, CS = (64, 64, 128, 1, 4, 32)
        INTER = NH * P_
        CONV_DIM = INTER + 2 * G_ * N_
        PROJ = INTER + CONV_DIM + NH
        EPS = 1e-05

        def segsum(x):
            L = x.shape[-1]
            i = jnp.arange(L)
            strict = i[:, None] > i[None, :]
            X = jnp.where(strict, x[..., :, None], 0.0)
            S = jnp.cumsum(X, axis=-2)
            return jnp.where(i[:, None] >= i[None, :], S, -jnp.inf)
        key = jax.random.key(seed)
        ks = jax.random.split(key, 6)
        return {'input_states': jax.random.normal(ks[0], (B_, S_, E_), dtype=jnp.float32), 'mask': jnp.ones((B_, 1, S_), dtype=jnp.int32), 'W_in': jax.random.normal(ks[1], (PROJ, E_), dtype=jnp.float32) * 0.02, 'conv_w': jax.random.normal(ks[2], (CONV_DIM, K_), dtype=jnp.float32) * 0.2, 'conv_b': jnp.zeros((CONV_DIM,), dtype=jnp.float32), 'dt_bias': jnp.ones((NH,), dtype=jnp.float32), 'A_log': jnp.log(jnp.arange(1, NH + 1, dtype=jnp.float32)), 'D': jnp.ones((NH,), dtype=jnp.float32), 'norm_w': jnp.ones((INTER,), dtype=jnp.float32), 'W_out': jax.random.normal(ks[3], (E_, INTER), dtype=jnp.float32) * 0.02}
    _L0_attn_in = _L0_attn_setup()

    def _L0_ffn_setup():
        import jax, jax.numpy as jnp
        import numpy as np
        B, S, H = (2, 64, 256)
        E, I, K = (64, 176, 6)
        NS = 2
        SH_I = I * NS
        key = jax.random.key(seed)
        ks = jax.random.split(key, 6)
        s = 0.02
        return {'hidden_states': jax.random.normal(ks[0], (B, S, H), jnp.float32), 'gate_w': jax.random.normal(ks[1], (E, H), jnp.float32) * s, 'experts_w1': jax.random.normal(ks[2], (E, I, H), jnp.float32) * s, 'experts_w2': jax.random.normal(ks[3], (E, H, I), jnp.float32) * s, 'shared_gate_up': jax.random.normal(ks[4], (2 * SH_I, H), jnp.float32) * s, 'shared_down': jax.random.normal(ks[5], (H, SH_I), jnp.float32) * s}
    _L0_ffn_in = _L0_ffn_setup()
    _L0_c = _w((lambda *s: np.random.randn(*s).astype(np.float32) * 0.05)(4, 256))
    _L0_wmod = _w((lambda *s: np.random.randn(*s).astype(np.float32) * 0.05)(256, 6 * 256) * 256 ** (-0.5))
    _d = {'L0_attn_input_states': _L0_attn_in['input_states'], 'L0_attn_mask': _L0_attn_in['mask'], 'L0_attn_W_in': _L0_attn_in['W_in'], 'L0_attn_conv_w': _L0_attn_in['conv_w'], 'L0_attn_conv_b': _L0_attn_in['conv_b'], 'L0_attn_dt_bias': _L0_attn_in['dt_bias'], 'L0_attn_A_log': _L0_attn_in['A_log'], 'L0_attn_D': _L0_attn_in['D'], 'L0_attn_norm_w': _L0_attn_in['norm_w'], 'L0_attn_W_out': _L0_attn_in['W_out'], 'L0_ffn_gate_w': _L0_ffn_in['gate_w'], 'L0_ffn_experts_w1': _L0_ffn_in['experts_w1'], 'L0_ffn_experts_w2': _L0_ffn_in['experts_w2'], 'L0_ffn_shared_gate_up': _L0_ffn_in['shared_gate_up'], 'L0_ffn_shared_down': _L0_ffn_in['shared_down'], 'L0_c': _L0_c, 'L0_wmod': _L0_wmod}
    _x0 = _d['L0_attn_input_states']
    _d['L0_attn_input_states'] = jax.random.normal(jax.random.fold_in(jax.random.key(seed), 1), (4, 512, 256), dtype=_x0.dtype)
    del _x0
    return _d

def reference(L0_attn_input_states, L0_attn_mask, L0_attn_W_in, L0_attn_conv_w, L0_attn_conv_b, L0_attn_dt_bias, L0_attn_A_log, L0_attn_D, L0_attn_norm_w, L0_attn_W_out, L0_ffn_gate_w, L0_ffn_experts_w1, L0_ffn_experts_w2, L0_ffn_shared_gate_up, L0_ffn_shared_down, L0_c, L0_wmod):

    def _L0_attn_ref(input_states, mask, W_in, conv_w, conv_b, dt_bias, A_log, D, norm_w, W_out):
        import jax, jax.numpy as jnp
        import numpy as np
        B_, S_, E_ = (1, 256, 256)
        NH, P_, N_, G_, K_, CS = (64, 64, 128, 1, 4, 32)
        INTER = NH * P_
        CONV_DIM = INTER + 2 * G_ * N_
        PROJ = INTER + CONV_DIM + NH
        EPS = 1e-05

        def segsum(x):
            L = x.shape[-1]
            i = jnp.arange(L)
            strict = i[:, None] > i[None, :]
            X = jnp.where(strict, x[..., :, None], 0.0)
            S = jnp.cumsum(X, axis=-2)
            return jnp.where(i[:, None] >= i[None, :], S, -jnp.inf)
        B, S, E = input_states.shape
        proj = input_states @ W_in.T
        gate = proj[..., :INTER]
        h_BC = proj[..., INTER:INTER + CONV_DIM]
        dt = proj[..., INTER + CONV_DIM:]
        xpad = jnp.pad(h_BC, ((0, 0), (K_ - 1, 0), (0, 0)))
        conv = conv_b
        for i in range(K_):
            conv = conv + xpad[:, i:i + S, :] * conv_w[:, i]
        h_BC = jax.nn.silu(conv)
        hidden = h_BC[..., :INTER]
        Bm = h_BC[..., INTER:INTER + G_ * N_]
        Cm = h_BC[..., INTER + G_ * N_:]
        A = -jnp.exp(A_log)
        dt = jnp.clip(jax.nn.softplus(dt + dt_bias), 0.0)
        Hs = hidden.reshape(B, S, NH, P_).astype(jnp.float32)
        Bm = jnp.tile(Bm.reshape(B, S, G_, N_).astype(jnp.float32), (1, 1, NH // G_, 1))
        Cm = jnp.tile(Cm.reshape(B, S, G_, N_).astype(jnp.float32), (1, 1, NH // G_, 1))
        D_resid = D[None, None, :, None] * Hs
        Hdt = Hs * dt[..., None]
        At = A * dt
        C_ = S // CS
        Hc = Hdt.reshape(B, C_, CS, NH, P_)
        Ac = At.reshape(B, C_, CS, NH)
        Bc = Bm.reshape(B, C_, CS, NH, N_)
        Cc = Cm.reshape(B, C_, CS, NH, N_)
        Ap = jnp.transpose(Ac, (0, 3, 1, 2))
        A_cum = jnp.cumsum(Ap, axis=-1)
        L_tri = jnp.exp(segsum(Ap))
        Gm = jnp.einsum('bclhn,bcshn->bclsh', Cc, Bc)
        M = Gm * jnp.transpose(L_tri, (0, 2, 3, 4, 1))
        Yd = jnp.einsum('bclsh,bcshp->bclhp', M, Hc)
        decay = jnp.exp(A_cum[..., -1:] - A_cum)
        Bd = Bc * jnp.transpose(decay, (0, 2, 3, 1))[..., None]
        states = jnp.einsum('bclhn,bclhp->bchpn', Bd, Hc)
        Sd = jnp.transpose(jnp.exp(A_cum), (0, 2, 3, 1))
        Yoff = jnp.einsum('bclhn,bchpn->bclhp', Cc, states) * Sd[..., None]
        y = (Yd + Yoff).reshape(B, S, NH, P_) + D_resid
        y = y.reshape(B, S, INTER)
        yf = y.astype(jnp.float32) * jax.nn.silu(gate.astype(jnp.float32))
        var = jnp.mean(yf * yf, axis=-1, keepdims=True)
        yn = norm_w * (yf * jax.lax.rsqrt(var + EPS))
        return yn @ W_out.T

    def _L0_ffn_ref(hidden_states, gate_w, experts_w1, experts_w2, shared_gate_up, shared_down):
        import jax, jax.numpy as jnp
        import numpy as np
        B, S, H = (2, 64, 256)
        E, I, K = (64, 176, 6)
        NS = 2
        SH_I = I * NS
        orig_shape = hidden_states.shape
        x = hidden_states.reshape(-1, orig_shape[-1])
        router_logits = x @ gate_w.T
        probs = jax.nn.softmax(router_logits, axis=-1)
        topk_w, topk_idx = jax.lax.top_k(probs, K)
        topk_w = topk_w / jnp.sum(topk_w, axis=-1, keepdims=True)
        combine = jnp.sum(jax.nn.one_hot(topk_idx, E, dtype=x.dtype) * topk_w[..., None], axis=1)
        h = jax.nn.silu(jnp.einsum('th,eih->tei', x, experts_w1))
        y = jnp.einsum('tei,ehi->teh', h, experts_w2)
        routed_out = jnp.einsum('teh,te->th', y, combine)
        gu = x @ shared_gate_up.T
        g, u = jnp.split(gu, 2, axis=-1)
        shared_out = jax.nn.silu(g) * u @ shared_down.T
        return (routed_out + shared_out).reshape(orig_shape)
    x = L0_attn_input_states
    mod = (_silu(L0_c) @ L0_wmod).reshape(L0_c.shape[0], 6, 1, -1)
    sa, ca, ga, sb, cb, gb = (mod[:, 0], mod[:, 1], mod[:, 2], mod[:, 3], mod[:, 4], mod[:, 5])
    ga = (2 * (ga >= 0) - 1) * jnp.maximum(jnp.abs(ga), 0.25)
    gb = (2 * (gb >= 0) - 1) * jnp.maximum(jnp.abs(gb), 0.25)
    h = _layernorm(x, axis=-1) * (1 + ca) + sa
    x = x + ga * _L0_attn_ref(h, L0_attn_mask, L0_attn_W_in, L0_attn_conv_w, L0_attn_conv_b, L0_attn_dt_bias, L0_attn_A_log, L0_attn_D, L0_attn_norm_w, L0_attn_W_out)
    h = _layernorm(x, axis=-1) * (1 + cb) + sb
    x = x + gb * _L0_ffn_ref(h, L0_ffn_gate_w, L0_ffn_experts_w1, L0_ffn_experts_w2, L0_ffn_shared_gate_up, L0_ffn_shared_down)
    return x

_drawn_inputs = setup_inputs


def setup_inputs(seed=0):
    import zlib

    import numpy as np

    out = dict(_drawn_inputs(seed))
    spreads = {'L0_attn_conv_b': (0.0, 0.1),
     'L0_attn_dt_bias': (1.0, 0.6),
     'L0_attn_D': (1.0, 0.2),
     'L0_attn_norm_w': (1.0, 0.2)}
    factors = {'L0_attn_A_log': 8.0,
     'L0_ffn_gate_w': 8.0,
     'L0_ffn_experts_w1': 8.0,
     'L0_ffn_experts_w2': 8.0,
     'L0_ffn_shared_gate_up': 8.0,
     'L0_ffn_shared_down': 8.0}
    for name, (base, spread) in spreads.items():
        noise = np.random.default_rng([zlib.crc32(name.encode()), seed]).standard_normal(out[name].shape)
        drawn = base * np.exp(spread * noise) if base else spread * noise
        out[name] = jnp.asarray(drawn.astype(out[name].dtype))
    for name, factor in factors.items():
        out[name] = (out[name] * factor).astype(out[name].dtype)
    return out
```

```python
from contextlib import ExitStack

import numpy as np

import concourse.bass as bass
from concourse import mybir

P = 128
F32 = mybir.dt.float32
ALU = mybir.AluOpType
ACT = mybir.ActivationFunctionType
AX_X = mybir.AxisListType.X

BATCH, SEQ, EMB = 4, 512, 256
HEADS, HEAD_DIM, STATE, TAPS, CHUNK = 64, 64, 128, 4, 32
INTER = HEADS * HEAD_DIM
EXPERTS, EXP_INNER, TOP_K = 64, 176, 6
SHARED_INNER = 2 * EXP_INNER
EPS = 1e-5

TOKENS = BATCH * SEQ
KE = EMB // P
TILES = SEQ // P
PAIRS = INTER // P
CPT = P // CHUNK
SEG = HEADS * CHUNK
SEG_MM = SEG // SEQ
WO_AT, SC_AT = 4 * P, 4 * P + EMB
NW_AT, D_AT, TAP_AT = SC_AT, SC_AT + 1, SC_AT + 2
PAIR_COLS = SC_AT + 2 + TAPS + 1
EXP_ROWS = EXPERTS * EXP_INNER
ECHUNKS = EXP_ROWS // P
E2_AT, SEL_AT = KE * P, KE * P + EMB
ECOLS = SEL_AT + P
HALVES = 2
BPH = BATCH // HALVES
SH_CHUNKS = -(-SHARED_INNER // P)
UNITS = (SH_CHUNKS + ECHUNKS) * BPH
TINY = -1.0


def constants():
    k = np.arange(P)
    same = (k[:, None] // CHUNK) == (k[None, :] // CHUNK)
    ident = np.eye(P)
    later = same & (k[:, None] > k[None, :])
    upto = (k[:, None] % CHUNK) <= np.arange(CHUNK)
    return np.concatenate([ident, later, same, upto, np.ones((P, P))], 1).astype(np.float32)


def selectors():
    row = np.arange(EXP_ROWS).reshape(ECHUNKS, 1, P) // EXP_INNER
    sel = (row == np.arange(EXPERTS)[None, :, None]).astype(np.float32)
    return np.concatenate([sel, np.zeros_like(sel)], 1)


def program(nc, x_t, pair_w, bc_w, bc_conv, dt_w, dt_bias, a_log, c_t, mod_w, gate_w, shared_w,
            shared_d, expert_w, const, out_t):
    ctx = ExitStack()
    with ctx:
        def sb(name, shape, dt=F32):
            return ctx.enter_context(nc.sbuf_tensor(name, shape, dt))

        def sem(name):
            return ctx.enter_context(nc.semaphore(name))

        START = {"gate": 2, "wo_done": 2, "y_done": 2, "out_mm": 2, "y_sq": 2, "weighted": 2, "expert_mm": 3,
                 "res_done": 1, "taps": 1, "silu_g": 1, "xt_done": 1, "y_skip": 1, "ssq_done": 1, "ssm": 1,
                 "result": 1, "ssq_mm": 1, "stored": 16}

        consts = sb("consts", [P, 3 * P + CHUNK + P])
        ident, later, same = (consts[:, i * P:(i + 1) * P] for i in range(3))
        upto = consts[:, 3 * P:3 * P + CHUNK]
        ones = consts[:, 3 * P + CHUNK:]
        x_all = sb("x_all", [P, KE, TOKENS])
        h2_all = sb("h2_all", [P, KE, TOKENS])
        comb_t = sb("comb_t", [P, TOKENS])
        cvec = sb("cvec", [P, KE, BATCH])
        cact = sb("cact", [P, KE, BATCH])
        mod = sb("mod", [P, 6 * KE, BATCH])
        gneg = sb("gneg", [P, 2, KE, BATCH])
        gsign = sb("gsign", [P, 2, KE, BATCH])
        gmag = sb("gmag", [P, 2, KE, BATCH])
        bcw = sb("bcw", [P, 2, KE, P])
        bcc = sb("bcc", [P, 2, TAPS + 1])
        dtw = sb("dtw", [P, KE, HEADS])
        dtb = sb("dtb", [P, HEADS])
        alog = sb("alog", [P, HEADS])
        aneg = sb("aneg", [P, HEADS])
        gatew = sb("gatew", [P, KE, EXPERTS])
        shw = sb("shw", [P, KE, 2 * SHARED_INNER])
        shd = sb("shd", [P, SH_CHUNKS, EMB])

        xc = sb("xc", [P, KE, SEQ])
        xsq = sb("xsq", [P, KE, SEQ])
        var = sb("var", [P, SEQ])
        std = sb("std", [P, SEQ])
        rstd = sb("rstd", [P, SEQ])
        h1 = sb("h1", [P, KE, SEQ])
        z = sb("z", [P, TILES, HEADS])
        zabs = sb("zabs", [P, TILES, HEADS])
        zexp = sb("zexp", [P, TILES, HEADS])
        zln = sb("zln", [P, TILES, HEADS])
        dt = sb("dt", [P, TILES, HEADS])
        at = sb("at", [P, TILES, HEADS])
        decay = sb("decay", [P, TILES, HEADS])
        bcacc = sb("bcacc", [P, 2, SEQ])
        bcf = sb("bcf", [P, 2, SEQ])
        gmask = sb("gmask", [P, TILES, 2, P])
        mov = sb("mov", [P, 2, SEG])
        e1 = sb("e1", [P, SEG])
        e2 = sb("e2", [P, SEG])
        el = sb("el", [P, PAIRS, TILES, 2, CHUNK])
        modw = el[:, 0:6 * EMB * KE // (TILES * 2 * CHUNK), :, :, :].rearrange("p j t h l -> p (j t h l)")\
            .rearrange("p (k n) -> p k n", k=KE)

        pw = sb("pw", [P, 2, PAIR_COLS])
        wo = sb("wo", [P, 2, EMB])
        acc = sb("acc", [P, 2, SEQ])
        xf = sb("xf", [P, 2, SEQ])
        gs = sb("gs", [P, 2, SEQ])
        xt = sb("xt", [P, TILES, 3 * HEAD_DIM])
        m = sb("m", [P, TILES, 2, P])
        yt = sb("yt", [P, SEQ])
        y = sb("y", [P, 2, SEQ])
        ysq = sb("ysq", [P, SEQ])
        ssq = sb("ssq", [P, SEQ])
        attn = e1[:, 0:KE * SEQ].rearrange("p (k n) -> p k n", k=KE)

        zero = sb("zero", [P, 1])
        start = sb("start", [P, len(START)])
        order = sb("order", [P, 2])
        lmax = sb("lmax", [P, TILES])
        lsub = sb("lsub", [P, TILES, EXPERTS])
        lexp = sb("lexp", [P, TILES, EXPERTS])
        lsum = sb("lsum", [P, TILES])
        lrec = sb("lrec", [P, TILES])
        prob = sb("prob", [P, TILES, EXPERTS])
        top8 = sb("top8", [P, TILES, 8])
        rest = sb("rest", [P, TILES, EXPERTS])
        kept = sb("kept", [P, TILES, EXPERTS])
        ksum = sb("ksum", [P, TILES])
        krec = sb("krec", [P, TILES])
        comb = sb("comb", [P, TILES, P])

        ew = sb("ew", [P, 2, ECOLS])
        hs = e2[:, 0:2 * SEQ].rearrange("p (q n) -> p q n", q=2)
        hw = e2[:, 2 * SEQ:4 * SEQ].rearrange("p (q n) -> p q n", q=2)
        res = e1[:, KE * SEQ:2 * KE * SEQ].rearrange("p (k n) -> p k n", k=KE)

        bank = [ctx.enter_context(nc.psum_tensor(f"bank{i}", [P, SEQ], F32)) for i in range(8)]
        p_hid, p_gate, p_turn, p_y = bank[0:4]
        p_out = bank[4:6]
        p_mean, p_var = bank[6:8]
        p_inner, p_comb, p_moe = bank[0:2], bank[2:4], bank[4:8]

        S = {}
        for name in """setup moved credits silu_c mod_mm mod_copied mods_done aneg_exp aneg_done
            mean centred squared variance var_eps std_done xhat normed
            dt_mm z_done dt_abs dt_exp dt_ln dt_done decay_mm decay_done
            bc_mm bc_tap0 bc_taps bc_silu g_mm g_done mov_done seg_mm seg_exp seg_scaled seg_done
            w0 w1 hid gate tap0 taps silu_x silu_g turned xt_done m_done ssm y_skip y_done y_sq
            out_mm wo_done ssq_done ssq_zero ssq_mm ssq_var ssq_std rms_done attn_done res_done
            logit lmax_done lsub_done lexp_done router_chain comb_done comb_turned comb_copied
            ew0 ew1 inner cmb_mm inner_silu weighted expert_mm result stored zero_set""".split():
            S[name] = sem(name)

        block = ctx.enter_context(nc.Block())

        def modcol(which, k, b):
            return mod[:, which * KE + k, bass.ds(b, 1)]

        @block.sync
        def _(sp):
            for dst, src in ((consts[:, :], const), (cvec[:, :, :], c_t), (modw[:, :, :], mod_w),
                             (bcw[:, :, :, :], bc_w), (bcc[:, :, :], bc_conv), (dtw[:, :, :], dt_w),
                             (gatew[:, :, :], gate_w), (shw[:, :, :], shared_w), (shd[:, :, :], shared_d)):
                sp.dma_start(dst, src).then_inc(S["setup"], 16)
            for b in range(BATCH - 1):
                sp.dma_start(x_all[:, :, b * SEQ:(b + 1) * SEQ], x_t[:, :, b * SEQ:(b + 1) * SEQ])\
                    .then_inc(S["setup"], 16)
            sp.dma_start(x_all[:, :, (BATCH - 1) * SEQ:], x_t[:, :, (BATCH - 1) * SEQ:]).then_inc(S["setup"], 16)
            sp.dma_start(dtb[:, :], dt_bias.partition_broadcast(P)).then_inc(S["moved"], 16)
            sp.dma_start(alog[:, :], a_log.partition_broadcast(P)).then_inc(S["moved"], 16)
            with sp.Fori(0, BATCH) as b:
                with sp.Fori(0, PAIRS // 2) as jj:
                    j0 = 2 * jj
                    for par in range(2):
                        g = b * PAIRS + j0 + par
                        sp.wait_ge(S["gate"], START["gate"] + g - 1)
                        sp.wait_ge(S["wo_done"], START["wo_done"] + g - 1)
                        sp.wait_ge(S["y_done"], START["y_done"] + g - 1)
                        sp.dma_start(pw[:, par, :], pair_w[bass.ds(j0 + par, 1), :, :].rearrange("a p n -> p (a n)"))\
                            .then_inc(S[f"w{par}"], 16)
            def load_piece(hf, c, par, units):
                sp.wait_ge(S["expert_mm"], START["expert_mm"] + hf * UNITS + units - BPH)
                sp.dma_start(ew[:, par, :], expert_w[bass.ds(c, 1), :, :].rearrange("a p n -> p (a n)"))\
                    .then_inc(S[f"ew{par}"], 16)

            with sp.Fori(0, HALVES) as hf:
                for par in range(2):
                    load_piece(hf, par, par, par * BPH)
                with sp.Fori(1, ECHUNKS // 2) as cc:
                    for par in range(2):
                        c = 2 * cc + par
                        load_piece(hf, c, par, (SH_CHUNKS + c) * BPH)
                for q in range(BPH):
                    b = hf * BPH + q
                    sp.wait_ge(S["result"], START["result"] + (b + 1) * KE)
                    sp.dma_start(out_t[:, :, bass.ds(b * SEQ, SEQ)], res[:, :, :]).then_inc(S["stored"], 16)
            sp.wait_ge(S["stored"], START["stored"] + 16 * BATCH)

        @block.tensor
        def _(pe):
            mm = nc.tensor.matmul

            def norm_sums(b, which):
                if which == 0:
                    pe.wait_ge(S["res_done"], START["res_done"] + b * KE)
                else:
                    pe.wait_ge(S["res_done"], START["res_done"] + b * KE + KE)
                for k in range(KE):
                    i = mm(p_mean[:, :], ones, x_all[:, k, bass.ds(b * SEQ, SEQ)], start=k == 0, stop=k == KE - 1)
                i.then_inc(S["mean"], 1)
                pe.wait_ge(S["squared"], 2 * b + which + 1)
                for k in range(KE):
                    i = mm(p_var[:, :], ones, xsq[:, k, :], start=k == 0, stop=k == KE - 1)
                i.then_inc(S["variance"], 1)

            def slot(b, j, do_in, do_mid, do_out, par):
                g = b * PAIRS + j
                if do_mid:
                    q = 1 - par
                    pe.wait_ge(S["silu_x"], g)
                    pe.wait_ge(S["xt_done"], START["xt_done"] + g - 1)
                    for t in range(TILES):
                        i = nc.tensor.transpose(p_turn[:, t * P:(t + 1) * P], xf[:, q, t * P:(t + 1) * P], ident)
                    i.then_inc(S["turned"], 1)
                if do_in:
                    pe.wait_ge(S[f"w{par}"], 8 * (g - par) + 16)
                    pe.wait_ge(S["taps"], START["taps"] + (TAPS - 1) * g)
                    for k in range(KE):
                        i = mm(p_hid[:, :], pw[:, par, (2 + k) * P:(3 + k) * P], h1[:, k, :], start=k == 0, stop=k == KE - 1)
                    i.then_inc(S["hid"], 1)
                    pe.wait_ge(S["silu_g"], START["silu_g"] + g)
                    for k in range(KE):
                        i = mm(p_gate[:, :], pw[:, par, k * P:(k + 1) * P], h1[:, k, :], start=k == 0, stop=k == KE - 1)
                    i.then_inc(S["gate"], 1)
                if do_mid:
                    pe.wait_ge(S["xt_done"], START["xt_done"] + g)
                    pe.wait_ge(S["m_done"], g)
                    pe.wait_ge(S["y_skip"], START["y_skip"] + g - 1)
                    for t in range(TILES):
                        for h in range(2):
                            i = mm(p_y[:, t * P:(t + 1) * P], xt[:, t, h * HEAD_DIM:h * HEAD_DIM + P], m[:, t, h, :],
                                   start=h == 0, stop=h == 1)
                    i.then_inc(S["ssm"], 1)
                if do_out:
                    pe.wait_ge(S["y_done"], START["y_done"] + g - 1)
                    pe.wait_ge(S["wo_done"], START["wo_done"] + g - 1)
                    for k in range(KE):
                        i = mm(p_out[k][:, :], wo[:, par, k * P:(k + 1) * P], y[:, par, :],
                               start=do_out == "first", stop=do_out == "last")
                    i.then_inc(S["out_mm"], 1)

            pe.wait_ge(S["setup"], 16 * 13)
            pe.wait_ge(S["silu_c"], 1)
            for n in range(6 * KE):
                for k in range(KE):
                    i = mm(p_hid[:, n * BATCH:(n + 1) * BATCH], modw[:, k, n * P:(n + 1) * P], cact[:, k, :],
                           start=k == 0, stop=k == KE - 1)
            i.then_inc(S["mod_mm"], 1)
            pe.wait_ge(S["mod_copied"], 1)

            with pe.Fori(0, BATCH) as b:
                norm_sums(b, 0)
                pe.wait_ge(S["normed"], 2 * KE * b + KE)
                for t in range(TILES):
                    for k in range(KE):
                        i = mm(p_turn[:, t * HEADS:(t + 1) * HEADS], h1[:, k, t * P:(t + 1) * P], dtw[:, k, :],
                               start=k == 0, stop=k == KE - 1)
                i.then_inc(S["dt_mm"], 1)
                for n, p in enumerate((p_hid, p_gate)):
                    for k in range(KE):
                        i = mm(p[:, :], bcw[:, n, k, :], h1[:, k, :], start=k == 0, stop=k == KE - 1)
                    i.then_inc(S["bc_mm"], 1)
                pe.wait_ge(S["dt_done"], b + 1)
                mm(p_mean[:, 0:TILES * HEADS], later, at[:, :, :], start=True, stop=True).then_inc(S["decay_mm"], 1)
                pe.wait_ge(S["bc_silu"], 2 * b + 2)
                for t in range(TILES):
                    i = mm(p_var[:, t * P:(t + 1) * P], bcf[:, 0, t * P:(t + 1) * P], bcf[:, 1, t * P:(t + 1) * P],
                           start=True, stop=True)
                i.then_inc(S["g_mm"], 1)
                for t in range(TILES):
                    pe.wait_ge(S["mov_done"], b * TILES + t + 1)
                    for n in range(SEG_MM):
                        if t or n >= 2:
                            pe.wait_ge(S["seg_exp"], 2 * ((b * TILES + t) * SEG_MM + n - 1))
                        src = mov[:, t % 2, n * SEQ:(n + 1) * SEQ]
                        mm(bank[n % 2][:, :], later, src, start=True, stop=True)
                        mm(bank[2 + n % 2][:, :], same, src, start=True, stop=True).then_inc(S["seg_mm"], 1)
                pe.wait_ge(S["seg_exp"], 2 * (b + 1) * TILES * SEG_MM)

                slot(b, 0, True, False, "", 0)
                slot(b, 1, True, True, "", 1)
                slot(b, 2, True, True, "first", 0)
                slot(b, 3, True, True, "mid", 1)
                with pe.Fori(2, PAIRS // 2) as jj:
                    j = 2 * jj
                    slot(b, j, True, True, "mid", 0)
                    slot(b, j + 1, True, True, "mid", 1)
                slot(b, PAIRS, False, True, "mid", 0)
                slot(b, PAIRS + 1, False, False, "last", 1)

                pe.wait_ge(S["ssq_done"], START["ssq_done"] + (b + 1) * PAIRS)
                mm(p_hid[:, :], ones, ssq[:, :], start=True, stop=True).then_inc(S["ssq_mm"], 1)

                norm_sums(b, 1)
                pe.wait_ge(S["normed"], 2 * KE * b + 2 * KE)
                for t in range(TILES):
                    for k in range(KE):
                        i = mm(p_turn[:, t * EXPERTS:(t + 1) * EXPERTS], h1[:, k, t * P:(t + 1) * P], gatew[:, k, :],
                               start=k == 0, stop=k == KE - 1)
                i.then_inc(S["logit"], 1)
                pe.wait_ge(S["comb_done"], b + 1)
                for t in range(TILES):
                    i = nc.tensor.transpose(p_y[:, t * P:(t + 1) * P], comb[:, t, :], ident)
                i.then_inc(S["comb_turned"], 1)

            pe.wait_ge(S["comb_copied"], BATCH)

            def inner_expert(u, hf, par, c, q):
                pe.wait_ge(S[f"ew{par}"], 8 * (hf * ECHUNKS + c - par) + 16)
                pe.wait_ge(S["weighted"], START["weighted"] + u - 1)
                x = bass.ds((hf * BPH + q) * SEQ, SEQ)
                for k in range(KE):
                    mm(p_inner[q][:, :], ew[:, par, k * P:(k + 1) * P], h2_all[:, k, x], start=k == 0, stop=k == KE - 1)
                mm(p_comb[q][:, :], ew[:, par, SEL_AT:], comb_t[:, x], start=True, stop=True)\
                    .then_inc(S["inner"], 1)

            def down(u, w, rows, q, start=False, stop=False):
                pe.wait_ge(S["weighted"], START["weighted"] + u + 1)
                for k in range(KE):
                    i = mm(p_moe[q * KE + k][:, :], w[0:rows, k * P:(k + 1) * P], hw[0:rows, q, :], start=start, stop=stop)
                i.then_inc(S["expert_mm"], 1)

            with pe.Fori(0, HALVES) as hf:
                base = hf * UNITS
                pe.wait_ge(S["result"], START["result"] + hf * BPH * KE)

                def sh_inner(u):
                    n, q = divmod(u, BPH)
                    rows = min(P, SHARED_INNER - n * P)
                    pe.wait_ge(S["weighted"], START["weighted"] + base + u - 1)
                    x = bass.ds((hf * BPH + q) * SEQ, SEQ)
                    for p, at_ in ((p_inner[q], 0), (p_comb[q], SHARED_INNER)):
                        for k in range(KE):
                            i = mm(p[0:rows, :], shw[:, k, at_ + n * P:at_ + n * P + rows], h2_all[:, k, x],
                                   start=k == 0, stop=k == KE - 1)
                    i.then_inc(S["inner"], 1)

                SU = SH_CHUNKS * BPH
                for u in range(SU):
                    sh_inner(u)
                    if u:
                        n, q = divmod(u - 1, BPH)
                        down(base + u - 1, shd[:, n, :], min(P, SHARED_INNER - n * P), q, start=n == 0)
                inner_expert(base + SU, hf, 0, 0, 0)
                n, q = divmod(SU - 1, BPH)
                down(base + SU - 1, shd[:, n, :], min(P, SHARED_INNER - n * P), q)

                def piece(c, par, last=False):
                    u = base + SU + c * BPH
                    w = ew[:, par, E2_AT:SEL_AT]
                    inner_expert(u + 1, hf, par, c, 1)
                    down(u, w, P, 0, stop=last)
                    if not last:
                        inner_expert(u + 2, hf, 1 - par, c + 1, 0)
                    down(u + 1, w, P, 1, stop=last)

                with pe.Fori(0, ECHUNKS // 2 - 1) as cc:
                    c = 2 * cc
                    piece(c, 0)
                    piece(c + 1, 1)
                piece(ECHUNKS - 2, 0)
                piece(ECHUNKS - 1, 1, True)

        @block.scalar
        def _(act):
            f = nc.scalar.activation
            act.wait_ge(S["setup"], 16 * 13)
            act.wait_ge(S["moved"], 32)
            f(cact[:, :, :], cvec[:, :, :], ACT.Silu).then_inc(S["silu_c"], 1)
            f(aneg[:, :], alog[:, :], ACT.Exp).then_inc(S["aneg_exp"], 1)

            def norm(b, which):
                act.wait_ge(S["centred"], (2 * b + which + 1) * KE)
                f(xsq[:, :, :], xc[:, :, :], ACT.Square).then_inc(S["squared"], 1)
                act.wait_ge(S["var_eps"], 2 * b + which + 1)
                f(std[:, :], var[:, :], ACT.Sqrt).then_inc(S["std_done"], 1)
                act.wait_ge(S["xhat"], 2 * b + which + 1)
                for k in range(KE):
                    f(h1[:, k, :], xc[:, k, :], ACT.Identity, bias=modcol(3 * which, k, b),
                      scale=modcol(3 * which + 1, k, b)).then_inc(S["normed"], 1)

            def slot(b, j, do_in, do_sq, par):
                g = b * PAIRS + j
                if do_sq:
                    act.wait_ge(S["y_done"], START["y_done"] + g - 1)
                    act.wait_ge(S["ssq_done"], START["ssq_done"] + g - 2)
                    f(ysq[:, :], y[:, par, :], ACT.Square).then_inc(S["y_sq"], 1)
                if do_in:
                    act.wait_ge(S["hid"], g + 1)
                    f(acc[:, par, :], p_hid[:, :], ACT.Identity, bias=pw[:, par, TAP_AT + TAPS:TAP_AT + TAPS + 1],
                      scale=pw[:, par, TAP_AT + TAPS - 1:TAP_AT + TAPS]).then_inc(S["tap0"], 1)
                    act.wait_ge(S["gate"], START["gate"] + g + 1)
                    f(gs[:, par, :], p_gate[:, :], ACT.Silu).then_inc(S["silu_g"], 1)
                    act.wait_ge(S["taps"], START["taps"] + (TAPS - 1) * (g + 1))
                    f(xf[:, par, :], acc[:, par, :], ACT.Silu).then_inc(S["silu_x"], 1)

            act.wait_ge(S["mods_done"], 1)
            with act.Fori(0, BATCH) as b:
                norm(b, 0)
                for n, p in enumerate((p_hid, p_gate)):
                    act.wait_ge(S["bc_mm"], 2 * b + n + 1)
                    f(bcacc[:, n, :], p[:, :], ACT.Identity, bias=bcc[:, n, TAPS:TAPS + 1],
                      scale=bcc[:, n, TAPS - 1:TAPS]).then_inc(S["bc_tap0"], 1)
                act.wait_ge(S["z_done"], b + 1)
                f(zabs[:, :, :], z[:, :, :], ACT.Abs).then_inc(S["dt_abs"], 1)
                act.wait_ge(S["dt_abs"], b + 1)
                f(zexp[:, :, :], zabs[:, :, :], ACT.Exp, scale=-1.0).then_inc(S["dt_exp"], 1)
                act.wait_ge(S["dt_exp"], b + 1)
                f(zln[:, :, :], zexp[:, :, :], ACT.Ln, bias=1.0).then_inc(S["dt_ln"], 1)
                act.wait_ge(S["decay_mm"], b + 1)
                f(decay[:, :, :], p_mean[:, 0:TILES * HEADS], ACT.Exp).then_inc(S["decay_done"], 1)
                act.wait_ge(S["bc_taps"], 2 * (TAPS - 1) * (b + 1))
                for n in range(2):
                    f(bcf[:, n, :], bcacc[:, n, :], ACT.Silu).then_inc(S["bc_silu"], 1)
                for t in range(TILES):
                    if t:
                        act.wait_ge(S["seg_done"], b * TILES + t)
                    for n in range(SEG_MM):
                        act.wait_ge(S["seg_mm"], (b * TILES + t) * SEG_MM + n + 1)
                        f(e1[:, n * SEQ:(n + 1) * SEQ], bank[n % 2][:, :], ACT.Exp).then_inc(S["seg_exp"], 1)
                        f(e2[:, n * SEQ:(n + 1) * SEQ], bank[2 + n % 2][:, :], ACT.Exp).then_inc(S["seg_exp"], 1)

                slot(b, 0, True, False, 0)
                slot(b, 1, True, False, 1)
                with act.Fori(1, PAIRS // 2) as jj:
                    j = 2 * jj
                    slot(b, j, True, True, 0)
                    slot(b, j + 1, True, True, 1)
                slot(b, PAIRS, False, True, 0)
                slot(b, PAIRS + 1, False, True, 1)

                act.wait_ge(S["ssq_var"], b + 1)
                f(std[:, :], var[:, :], ACT.Sqrt).then_inc(S["ssq_std"], 1)
                norm(b, 1)
                for k in range(KE):
                    act.wait_ge(S["normed"], 2 * KE * b + 2 * KE)
                    f(h2_all[:, k, bass.ds(b * SEQ, SEQ)], h1[:, k, :], ACT.Identity).then_inc(S["moved"], 1)
                act.wait_ge(S["lsub_done"], b + 1)
                f(lexp[:, :, :], lsub[:, :, :], ACT.Exp).then_inc(S["lexp_done"], 1)
                act.wait_ge(S["comb_turned"], b + 1)
                f(comb_t[:, bass.ds(b * SEQ, SEQ)], p_y[:, :], ACT.Identity).then_inc(S["comb_copied"], 1)

            def unit(u, q, rows=P):
                act.wait_ge(S["inner"], u + 1)
                act.wait_ge(S["weighted"], START["weighted"] + u - 1)
                f(hs[0:rows, q, :], p_inner[q][0:rows, :], ACT.Silu).then_inc(S["inner_silu"], 1)

            with act.Fori(0, HALVES) as hf:
                for n in range(SH_CHUNKS):
                    for q in range(BPH):
                        unit(hf * UNITS + n * BPH + q, q, min(P, SHARED_INNER - n * P))
                with act.Fori(0, ECHUNKS) as c:
                    u = BPH * c
                    for q in range(BPH):
                        unit(hf * UNITS + SH_CHUNKS * BPH + u + q, q)

        @block.vector
        def _(dve):
            v = nc.vector

            v.memset(xt[:, :, :], 0.0)
            v.memset(comb[:, :, :], 0.0)
            for n, (name, count) in enumerate(START.items()):
                v.memset(start[:, n:n + 1], 0.0).then_inc(S[name], count)

            dve.wait_ge(S["mod_mm"], 1)
            v.tensor_copy(mod[:, :, :], p_hid[:, 0:6 * KE * BATCH].rearrange("p (n b) -> p n b", b=BATCH))\
                .then_inc(S["mod_copied"], 1)
            dve.wait_ge(S["mod_copied"], 1)
            dve.wait_ge(S["aneg_exp"], 1)
            v.tensor_scalar(alog[:, :], aneg[:, :], -1.0, None, ALU.mult).then_inc(S["aneg_done"], 1)
            for n in (1, 4):
                c = mod[:, n * KE:(n + 1) * KE, :]
                v.tensor_scalar(c, c, 1.0, None, ALU.add)
            for n, w in enumerate((2, 5)):
                g = mod[:, w * KE:(w + 1) * KE, :]
                v.tensor_scalar(gneg[:, n], g, -1.0, None, ALU.mult)
                v.tensor_scalar(gsign[:, n], g, 0.0, 2.0, ALU.is_ge, ALU.mult).then_inc(S["credits"], 1)
            dve.wait_ge(S["credits"], 2)
            for n, w in enumerate((2, 5)):
                g = mod[:, w * KE:(w + 1) * KE, :]
                v.tensor_tensor(gmag[:, n], g, gneg[:, n], ALU.max).then_inc(S["credits"], 1)
            dve.wait_ge(S["credits"], 4)
            v.tensor_scalar(gmag[:, :], gmag[:, :], 0.25, None, ALU.max).then_inc(S["credits"], 1)
            v.tensor_scalar(gsign[:, :], gsign[:, :], -1.0, None, ALU.add).then_inc(S["credits"], 1)
            dve.wait_ge(S["credits"], 6)
            for n, w in enumerate((2, 5)):
                i = v.tensor_tensor(mod[:, w * KE:(w + 1) * KE, :], gmag[:, n], gsign[:, n], ALU.mult)
                i.then_inc(S["credits"], 1)
            dve.wait_ge(S["credits"], 8)
            v.memset(y[:, 0, 6:7], 0.0).then_inc(S["mods_done"], 1)

            def norm(b, which):
                r = 2 * b + which + 1
                x = bass.ds(b * SEQ, SEQ)
                dve.wait_ge(S["mean"], r)
                for k in range(KE):
                    v.scalar_tensor_tensor(xc[:, k, :], p_mean[:, :], -1.0 / EMB, x_all[:, k, x], ALU.mult, ALU.add)\
                        .then_inc(S["centred"], 1)
                dve.wait_ge(S["variance"], r)
                v.tensor_scalar(var[:, :], p_var[:, :], 1.0 / EMB, EPS, ALU.mult, ALU.add).then_inc(S["var_eps"], 1)
                dve.wait_ge(S["std_done"], r)
                v.reciprocal(rstd[:, :], std[:, :]).then_inc(S["rms_done"], 1)
                dve.wait_ge(S["rms_done"], 3 * b + 2 * which + 1)
                v.tensor_tensor(xc[:, :, :], xc[:, :, :], rstd[:, None, :].broadcast_to([P, KE, SEQ]), ALU.mult)\
                    .then_inc(S["xhat"], 1)

            def conv(dst, src, taps, done, base):
                for d in range(1, TAPS):
                    if d > 1:
                        dve.wait_ge(done, base + d - 1)
                    v.scalar_tensor_tensor(dst[:, d:], src[:, 0:SEQ - d], taps[:, TAPS - 1 - d:TAPS - d], dst[:, d:],
                                           ALU.mult, ALU.add).then_inc(done, 1)

            def moving(b, t):
                if t >= 2:
                    dve.wait_ge(S["seg_mm"], (b * TILES + t - 1) * SEG_MM)
                a = at[:, t, :, None].broadcast_to([P, HEADS, CHUNK])
                v.tensor_tensor(mov[:, t % 2, :].rearrange("p (h l) -> p h l", l=CHUNK), a,
                                upto[:, None, :].broadcast_to([P, HEADS, CHUNK]), ALU.mult).then_inc(S["mov_done"], 1)

            def segments(b, t):
                r = b * TILES + t
                dve.wait_ge(S["seg_exp"], 2 * (r + 1) * SEG_MM)
                e1v = e1[:, :].rearrange("p (h l) -> p h l", l=CHUNK)
                e2v = e2[:, :].rearrange("p (h l) -> p h l", l=CHUNK)
                v.tensor_tensor(e1v, e1v, upto[:, None, :].broadcast_to([P, HEADS, CHUNK]), ALU.mult)\
                    .then_inc(S["seg_scaled"], 1)
                v.tensor_tensor(e2v, e2v, decay[:, t, :, None].broadcast_to([P, HEADS, CHUNK]), ALU.mult)\
                    .then_inc(S["seg_scaled"], 1)
                dve.wait_ge(S["seg_scaled"], 2 * (r + 1))
                v.tensor_tensor(el[:, :, t, :, :].rearrange("p j h l -> p j (h l)"),
                                e1[:, :].rearrange("p (j n) -> p j n", j=PAIRS),
                                e2[:, :].rearrange("p (j n) -> p j n", j=PAIRS), ALU.add).then_inc(S["seg_done"], 1)

            def slot(b, j, do_in, do_mid, par):
                g = b * PAIRS + j
                q = 1 - par
                if do_mid:
                    dve.wait_ge(S["ssm"], START["ssm"] + g - 1)
                    e = el[:, bass.ds(j - 1, 1), :, :, :].rearrange("p a t h l -> p (a t h) l")
                    v.tensor_tensor(m[:, :, :, :].rearrange("p t h (r l) -> p (t h) r l", l=CHUNK),
                                    e[:, :, None, :].broadcast_to([P, TILES * 2, CPT, CHUNK]),
                                    gmask[:, :, :, :].rearrange("p t h (r l) -> p (t h) r l", l=CHUNK), ALU.mult)\
                        .then_inc(S["m_done"], 1)
                    dve.wait_ge(S["turned"], g)
                    d = dt[:, :, bass.ds(2 * (j - 1), 2)]
                    v.tensor_tensor(xt[:, :, :].rearrange("p t (a n) -> p t a n", a=3)[:, :, 0:3:2, :],
                                    p_turn[:, :].rearrange("p (t a n) -> p t a n", t=TILES, a=2),
                                    d[:, :, :, None].broadcast_to([P, TILES, 2, HEAD_DIM]), ALU.mult)\
                        .then_inc(S["xt_done"], 1)
                if do_in:
                    dve.wait_ge(S["tap0"], g + 1)
                    conv(acc[:, par, :], p_hid, pw[:, par, TAP_AT:TAP_AT + TAPS], S["taps"], START["taps"] + (TAPS - 1) * g)
                if do_mid:
                    dve.wait_ge(S["ssm"], START["ssm"] + g)
                    v.scalar_tensor_tensor(yt[:, :], xf[:, q, :], pw[:, q, D_AT:D_AT + 1], p_y[:, :], ALU.mult, ALU.add)\
                        .then_inc(S["y_skip"], 1)
                    dve.wait_ge(S["y_skip"], START["y_skip"] + g)
                    dve.wait_ge(S["out_mm"], START["out_mm"] + g - 2)
                    dve.wait_ge(S["y_sq"], START["y_sq"] + g - 2)
                    v.tensor_tensor(y[:, q, :], yt[:, :], gs[:, q, :], ALU.mult).then_inc(S["y_done"], 1)

            dve.wait_ge(S["aneg_done"], 1)
            with dve.Fori(0, BATCH) as b:
                norm(b, 0)
                dve.wait_ge(S["dt_mm"], b + 1)
                v.tensor_tensor(z[:, :, :], p_turn[:, 0:TILES * HEADS].rearrange("p (t h) -> p t h", t=TILES),
                                dtb[:, None, :].broadcast_to([P, TILES, HEADS]), ALU.add).then_inc(S["z_done"], 1)
                for n, p in enumerate((p_hid, p_gate)):
                    dve.wait_ge(S["bc_tap0"], 2 * b + n + 1)
                    conv(bcacc[:, n, :], p, bcc[:, n, :], S["bc_taps"], (TAPS - 1) * (2 * b + n))
                dve.wait_ge(S["dt_ln"], b + 1)
                v.scalar_tensor_tensor(dt[:, :, :], z[:, :, :], 0.0, zln[:, :, :], ALU.max, ALU.add)\
                    .then_inc(S["router_chain"], 1)
                dve.wait_ge(S["router_chain"], 10 * b + 1)
                v.tensor_tensor(at[:, :, :], dt[:, :, :], alog[:, None, :].broadcast_to([P, TILES, HEADS]), ALU.mult)\
                    .then_inc(S["dt_done"], 1)
                dve.wait_ge(S["dt_done"], b + 1)
                moving(b, 0)
                dve.wait_ge(S["g_mm"], b + 1)
                for h in range(2):
                    v.tensor_tensor(gmask[:, :, h, :], p_var[:, :].rearrange("p (t l) -> p t l", t=TILES),
                                    same[:, None, :].broadcast_to([P, TILES, P]), ALU.mult).then_inc(S["g_done"], 1)
                dve.wait_ge(S["decay_done"], b + 1)
                for t in range(TILES):
                    if t + 1 < TILES:
                        moving(b, t + 1)
                    segments(b, t)
                dve.wait_ge(S["seg_done"], (b + 1) * TILES)
                dve.wait_ge(S["g_done"], 2 * (b + 1))

                slot(b, 0, True, False, 0)
                slot(b, 1, True, True, 1)
                with dve.Fori(1, PAIRS // 2) as jj:
                    j = 2 * jj
                    slot(b, j, True, True, 0)
                    slot(b, j + 1, True, True, 1)
                slot(b, PAIRS, False, True, 0)

                dve.wait_ge(S["ssq_mm"], START["ssq_mm"] + b + 1)
                v.tensor_scalar(var[:, :], p_hid[:, :], 1.0 / INTER, EPS, ALU.mult, ALU.add).then_inc(S["ssq_var"], 1)
                dve.wait_ge(S["ssq_std"], b + 1)
                v.reciprocal(rstd[:, :], std[:, :]).then_inc(S["rms_done"], 1)
                dve.wait_ge(S["rms_done"], 3 * b + 2)
                dve.wait_ge(S["out_mm"], START["out_mm"] + (b + 1) * PAIRS)
                for k in range(KE):
                    v.tensor_tensor(attn[:, k, :], p_out[k][:, :], rstd[:, :], ALU.mult).then_inc(S["attn_done"], 1)
                dve.wait_ge(S["attn_done"], (b + 1) * KE)
                for k in range(KE):
                    xs = x_all[:, k, bass.ds(b * SEQ, SEQ)]
                    v.scalar_tensor_tensor(xs, attn[:, k, :], modcol(2, k, b), xs, ALU.mult, ALU.add)\
                        .then_inc(S["res_done"], 1)
                dve.wait_ge(S["res_done"], START["res_done"] + (b + 1) * KE)
                norm(b, 1)

                chain = [10 * b + 1]

                def step(i):
                    i.then_inc(S["router_chain"], 1)
                    chain[0] = chain[0] + 1
                    dve.wait_ge(S["router_chain"], chain[0])

                def wide(col):
                    return col[:, :, None].broadcast_to([P, TILES, EXPERTS])

                dve.wait_ge(S["logit"], b + 1)
                logits = p_turn[:, 0:TILES * EXPERTS].rearrange("p (t e) -> p t e", t=TILES)
                step(v.tensor_reduce(lmax[:, :], logits, AX_X, ALU.max))
                v.tensor_tensor(lsub[:, :, :], logits, wide(lmax), ALU.subtract).then_inc(S["lsub_done"], 1)
                dve.wait_ge(S["lexp_done"], b + 1)
                step(v.tensor_reduce(lsum[:, :], lexp[:, :, :], AX_X, ALU.add))
                step(v.reciprocal(lrec[:, :], lsum[:, :]))
                step(v.tensor_tensor(prob[:, :, :], lexp[:, :, :], wide(lrec), ALU.mult))
                v.tensor_copy(order[:, 0:1], lrec[:, 0:1])
                for t in range(TILES):
                    i = v.max(top8[:, t, :], prob[:, t, :])
                step(i)
                step(v.memset(top8[:, :, TOP_K:], TINY))
                v.tensor_copy(order[:, 1:2], lrec[:, 0:1])
                for t in range(TILES):
                    i = v.match_replace(rest[:, t, :], top8[:, t, :], prob[:, t, :], TINY)
                step(i)
                step(v.scalar_tensor_tensor(kept[:, :, :], rest[:, :, :], 0.0, prob[:, :, :], ALU.max, ALU.subtract))
                step(v.tensor_reduce(ksum[:, :], kept[:, :, :], AX_X, ALU.add))
                v.reciprocal(krec[:, :], ksum[:, :]).then_inc(S["lmax_done"], 1)
                dve.wait_ge(S["lmax_done"], b + 1)
                v.tensor_tensor(comb[:, :, 0:EXPERTS], kept[:, :, :], wide(krec), ALU.mult).then_inc(S["comb_done"], 1)

            def unit(u, q, rows=P):
                dve.wait_ge(S["inner_silu"], u + 1)
                dve.wait_ge(S["expert_mm"], START["expert_mm"] + u - 1)
                v.tensor_tensor(hw[0:rows, q, :], hs[0:rows, q, :], p_comb[q][0:rows, :], ALU.mult)\
                    .then_inc(S["weighted"], 1)

            with dve.Fori(0, HALVES) as hf:
                for n in range(SH_CHUNKS):
                    for q in range(BPH):
                        unit(hf * UNITS + n * BPH + q, q, min(P, SHARED_INNER - n * P))
                with dve.Fori(0, ECHUNKS) as c:
                    u = BPH * c
                    for q in range(BPH):
                        unit(hf * UNITS + SH_CHUNKS * BPH + u + q, q)
                dve.wait_ge(S["expert_mm"], START["expert_mm"] + (hf + 1) * UNITS)
                for q in range(BPH):
                    b = hf * BPH + q
                    dve.wait_ge(S["stored"], START["stored"] + 16 * b)
                    for k in range(KE):
                        v.scalar_tensor_tensor(res[:, k, :], p_moe[q * KE + k][:, :], modcol(5, k, b),
                                               x_all[:, k, bass.ds(b * SEQ, SEQ)], ALU.mult, ALU.add)\
                            .then_inc(S["result"], 1)

        @block.gpsimd
        def _(pool):
            g_ = nc.gpsimd

            def pair(b, j, par):
                g = b * PAIRS + j
                pool.wait_ge(S[f"w{par}"], 8 * (g - par) + 16)
                pool.wait_ge(S["out_mm"], START["out_mm"] + g - 1)
                g_.tensor_tensor(wo[:, par, :], pw[:, par, WO_AT:WO_AT + EMB],
                                 pw[:, par, NW_AT:NW_AT + 1].broadcast_to([P, EMB]), ALU.mult)\
                    .then_inc(S["wo_done"], 1)
                pool.wait_ge(S["y_sq"], START["y_sq"] + g + 1)
                pool.wait_ge(S["ssq_zero"], b + 1)
                pool.wait_ge(S["ssq_done"], START["ssq_done"] + g)
                g_.tensor_tensor(ssq[:, :], ssq[:, :], ysq[:, :], ALU.add).then_inc(S["ssq_done"], 1)

            g_.memset(zero[:, :], 0.0).then_inc(S["zero_set"], 1)
            pool.wait_ge(S["zero_set"], 1)
            with pool.Fori(0, BATCH) as b:
                pool.wait_ge(S["ssq_mm"], START["ssq_mm"] + b)
                zeros = zero[:, :].broadcast_to([P, SEQ])
                g_.tensor_tensor(ssq[:, :], zeros, zeros, ALU.add).then_inc(S["ssq_zero"], 1)
                with pool.Fori(0, PAIRS // 2) as jj:
                    j = 2 * jj
                    pair(b, j, 0)
                    pair(b, j + 1, 1)


def kernel(L0_attn_input_states, L0_attn_mask, L0_attn_W_in, L0_attn_conv_w, L0_attn_conv_b, L0_attn_dt_bias,
           L0_attn_A_log, L0_attn_D, L0_attn_norm_w, L0_attn_W_out, L0_ffn_gate_w, L0_ffn_experts_w1,
           L0_ffn_experts_w2, L0_ffn_shared_gate_up, L0_ffn_shared_down, L0_c, L0_wmod):
    import concourse.bacc as bacc
    from concourse.bass_utils import run_bass_kernel_spmd

    def rows(a):
        return a.reshape(-1, P, a.shape[1]).transpose(1, 0, 2)

    x, w_in = np.asarray(L0_attn_input_states), np.asarray(L0_attn_W_in)
    w_gate, w_hid = (w_in[n * INTER:(n + 1) * INTER].reshape(PAIRS, P, KE, P).transpose(0, 3, 2, 1)
                     .reshape(PAIRS, P, KE * P) for n in range(2))
    w_out = np.asarray(L0_attn_W_out).T.reshape(PAIRS, P, EMB)
    conv = np.concatenate([L0_attn_conv_w, np.asarray(L0_attn_conv_b)[:, None]], 1)
    pair_w = np.concatenate([w_gate, w_hid, w_out, np.asarray(L0_attn_norm_w).reshape(PAIRS, P, 1),
                             np.repeat(L0_attn_D, HEAD_DIM).reshape(PAIRS, P, 1),
                             conv[:INTER].reshape(PAIRS, P, TAPS + 1)], 2)
    bc = w_in[2 * INTER:2 * INTER + 2 * STATE].reshape(2, P, KE, P).transpose(3, 0, 2, 1)
    w1 = np.asarray(L0_ffn_experts_w1).reshape(ECHUNKS, P, KE, P).transpose(0, 3, 2, 1).reshape(ECHUNKS, P, KE * P)
    w2 = np.asarray(L0_ffn_experts_w2).transpose(0, 2, 1).reshape(ECHUNKS, P, EMB)
    down = np.zeros((SH_CHUNKS * P, EMB), np.float32)
    down[:SHARED_INNER] = np.asarray(L0_ffn_shared_down).T
    arrays = {
        "x_t": rows(x.reshape(TOKENS, EMB).T),
        "pair_w": pair_w,
        "bc_w": bc,
        "bc_conv": conv[INTER:].reshape(2, P, TAPS + 1).transpose(1, 0, 2),
        "dt_w": rows(w_in[2 * INTER + 2 * STATE:].T),
        "dt_bias": np.asarray(L0_attn_dt_bias),
        "a_log": np.asarray(L0_attn_A_log),
        "c_t": rows(np.asarray(L0_c).T),
        "mod_w": rows(np.asarray(L0_wmod)),
        "gate_w": rows(np.asarray(L0_ffn_gate_w).T),
        "shared_w": rows(np.asarray(L0_ffn_shared_gate_up).T),
        "shared_d": rows(down),
        "expert_w": np.concatenate([w1, w2, selectors()], 2),
        "const": constants(),
    }
    nc = bacc.Bacc("TRN2", target_bir_lowering=False, num_devices=1)
    arrays = {n: np.ascontiguousarray(a) for n, a in arrays.items()}
    args = [nc.dram_tensor(n, a.shape, F32, kind="ExternalInput").ap() for n, a in arrays.items()]
    out = nc.dram_tensor("out_t", (P, KE, TOKENS), F32, kind="ExternalOutput").ap()
    program(nc, *args, out)
    got = run_bass_kernel_spmd(nc, [arrays], core_ids=[0]).results[0]["out_t"]
    return got.transpose(2, 1, 0).reshape(BATCH, SEQ, EMB)
```

```python
from contextlib import ExitStack

import numpy as np

import concourse.bass as bass
from concourse import mybir

P = 128
F32 = mybir.dt.float32
F32R = mybir.dt.float32r
ALU = mybir.AluOpType
ACT = mybir.ActivationFunctionType
AX_X = mybir.AxisListType.X

BATCH, SEQ, EMB = 4, 512, 256
HEADS, HEAD_DIM, STATE, TAPS, CHUNK = 64, 64, 128, 4, 32
INTER = HEADS * HEAD_DIM
EXPERTS, EXP_INNER, TOP_K = 64, 176, 6
SHARED_INNER = 2 * EXP_INNER
EPS = 1e-5

TOKENS = BATCH * SEQ
KE = EMB // P
TILES = SEQ // P
PAIRS = INTER // P
CPT = P // CHUNK
SEG = HEADS * CHUNK
SEG_UNIT = 2 * SEQ
UNITS_PER_TILE = SEG // SEG_UNIT
HPU = SEG_UNIT // CHUNK
IN_COLS = 2 * KE * P
NW_AT, D_AT, TAP_AT = 0, 1, 2
SCALARS = TAP_AT + TAPS + 1
EXP_ROWS = EXPERTS * EXP_INNER
ECHUNKS = EXP_ROWS // P
E2_AT, SEL_AT = KE * P, KE * P + EMB
ECOLS = SEL_AT + P
HALVES = 2
BPH = BATCH // HALVES
SH_CHUNKS = -(-SHARED_INNER // P)
UNITS = (SH_CHUNKS + ECHUNKS) * BPH
TINY = -1.0


def constants():
    k = np.arange(P)
    same = (k[:, None] // CHUNK) == (k[None, :] // CHUNK)
    ident = np.eye(P)
    later = same & (k[:, None] > k[None, :])
    upto = (k[:, None] % CHUNK) <= np.arange(CHUNK)
    return np.concatenate([ident, later, same, upto, (upto - 1.0) * 1e30, np.ones((P, P))], 1).astype(np.float32)


def selectors():
    row = np.arange(EXP_ROWS).reshape(ECHUNKS, 1, P) // EXP_INNER
    sel = (row == np.arange(EXPERTS)[None, :, None]).astype(np.float32)
    return np.concatenate([sel, sel], 1)


def program(nc, x_t, in_w, out_w, scalars, bc_w, bc_conv, dt_w, dt_bias, a_log, c_t, mod_w, gate_w, shared_w,
            shared_d, expert_w, const, out_t):
    ctx = ExitStack()
    with ctx:
        def sem(name):
            return ctx.enter_context(nc.semaphore(name))

        START = {"wi_lo": 2, "wo_lo": 2, "gate": 2, "y_done": 2, "out_mm": 2, "y_sq": 2, "y_hi": 2, "attn_res": 1,
                 "taps": 1, "silu_g": 1, "xt_done": 1, "y_skip": 1, "ssq_done": 1, "ssm": 1,
                 "result": 1, "ssq_mm": 1, "stored": 16, "seg_mm": 6, "seg_exp": 8, "seg_done": 2,
                 "weighted": 2, "hw_hi": 2, "expert_mm": 4, "ew_lo": 3}

        def sb(name, shape, dt=F32, on=ctx):
            return on.enter_context(nc.sbuf_tensor(name, shape, dt))

        CONSTS = 4 * P + 2 * CHUNK
        consts = sb("consts", [P, CONSTS])
        ident, later, same = (consts[:, i * P:(i + 1) * P] for i in range(3))
        upto = consts[:, 3 * P:3 * P + CHUNK]
        ones = consts[:, 3 * P + 2 * CHUNK:]
        consts_r = sb("consts_r", [P, 3 * P + 2 * CHUNK], F32R)
        ident_r, later_r, same_r = (consts_r[:, i * P:(i + 1) * P] for i in range(3))
        mask_r = consts_r[:, 3 * P + CHUNK:3 * P + 2 * CHUNK]
        x_all = sb("x_all", [P, KE, TOKENS])
        h_hi = sb("h_hi", [P, KE, TOKENS], F32R)
        h_lo = sb("h_lo", [P, KE, TOKENS], F32R)
        comb_t = sb("comb_t", [P, TOKENS], F32R)
        mod = sb("mod", [P, 6 * KE, BATCH])
        gatew = sb("gatew", [P, KE, EXPERTS])
        gatew_hi = sb("gatew_hi", [P, KE, EXPERTS], F32R)
        gatew_lo = sb("gatew_lo", [P, KE, EXPERTS], F32R)
        shw = sb("shw", [P, KE, 2 * SHARED_INNER])
        shd = sb("shd", [P, SH_CHUNKS, EMB])
        start = sb("start", [P, len(START)])
        scal = sb("scal", [P, PAIRS, SCALARS])
        bcw = sb("bcw", [P, 2, KE, P])
        bcw_hi = sb("bcw_hi", [P, 2, KE, P], F32R)
        bcw_lo = sb("bcw_lo", [P, 2, KE, P], F32R)
        bcc = sb("bcc", [P, 2, TAPS + 1])
        dtw = sb("dtw", [P, KE, P])
        dtw_hi = sb("dtw_hi", [P, KE, P], F32R)
        dtw_lo = sb("dtw_lo", [P, KE, P], F32R)
        dtb = sb("dtb", [P, 1])
        alog = sb("alog", [P, HEADS])
        aexp = sb("aexp", [P, HEADS])
        aneg = sb("aneg", [P, HEADS])

        with ExitStack() as part:
            xc = sb("xc", [P, 2, KE, SEQ], on=part)
            xsq = sb("xsq", [P, 2, KE, SEQ], on=part)
            var = sb("var", [P, 2, SEQ], on=part)
            std = sb("std", [P, 2, SEQ], on=part)
            rstd = sb("rstd", [P, 2, SEQ], on=part)
            h = sb("h", [P, 2, KE, SEQ], on=part)
            cvec = sb("cvec", [P, KE, BATCH], on=part)
            cact = sb("cact", [P, KE, BATCH], on=part)
            gneg = sb("gneg", [P, 2, KE, BATCH], on=part)
            gsign = sb("gsign", [P, 2, KE, BATCH], on=part)
            gmag = sb("gmag", [P, 2, KE, BATCH], on=part)
            modw = sb("modw", [P, KE, 6 * EMB], on=part)
            lmax = sb("lmax", [P, TILES], on=part)
            lsub = sb("lsub", [P, TILES, EXPERTS], on=part)
            lexp = sb("lexp", [P, TILES, EXPERTS], on=part)
            lsum = sb("lsum", [P, TILES], on=part)
            lrec = sb("lrec", [P, TILES], on=part)
            prob = sb("prob", [P, TILES, EXPERTS], on=part)
            top8 = sb("top8", [P, TILES, 8], on=part)
            rest = sb("rest", [P, TILES, EXPERTS], on=part)
            kept = sb("kept", [P, TILES, EXPERTS], on=part)
            ksum = sb("ksum", [P, TILES], on=part)
            krec = sb("krec", [P, TILES], on=part)
            share = sb("share", [P, TILES, EXPERTS], on=part)
            share_hi = sb("share_hi", [P, TILES, EXPERTS], F32R, on=part)
            comb = sb("comb", [P, TILES, P], on=part)

        with ExitStack() as part:
            z = sb("z", [P, SEQ], on=part)
            zabs = sb("zabs", [P, SEQ], on=part)
            zexp = sb("zexp", [P, SEQ], on=part)
            zln = sb("zln", [P, SEQ], on=part)
            dt_head = sb("dt_head", [P, SEQ], on=part)
            dt = sb("dt", [P, TILES, HEADS], on=part)
            at = sb("at", [P, TILES, HEADS], on=part)
            at_hi = sb("at_hi", [P, TILES, HEADS], F32R, on=part)
            at_lo = sb("at_lo", [P, TILES, HEADS], F32R, on=part)
            bcacc = sb("bcacc", [P, 2, SEQ], on=part)
            bcf = sb("bcf", [P, 2, SEQ], on=part)
            gmask = sb("gmask", [P, TILES, 2, P], on=part)
            mov_hi = sb("mov_hi", [P, 2, SEG_UNIT], F32R, on=part)
            mov_lo = sb("mov_lo", [P, 2, SEG_UNIT], F32R, on=part)
            e1 = sb("e1", [P, 2, SEG_UNIT], on=part)
            e2 = sb("e2", [P, 2, SEG_UNIT], on=part)
            el = sb("el", [P, PAIRS, TILES, 2, CHUNK], on=part)
            wi = sb("wi", [P, 2, IN_COLS], on=part)
            wi_hi = sb("wi_hi", [P, 2, IN_COLS], F32R, on=part)
            wi_lo = sb("wi_lo", [P, 2, IN_COLS], F32R, on=part)
            wo = sb("wo", [P, 2, EMB], on=part)
            wo_hi = sb("wo_hi", [P, 2, EMB], F32R, on=part)
            wo_lo = sb("wo_lo", [P, 2, EMB], F32R, on=part)
            xt = sb("xt", [P, TILES, 3 * HEAD_DIM], on=part)
            m = sb("m", [P, TILES, 2, P], on=part)
            yt = sb("yt", [P, SEQ], on=part)
            ysq = sb("ysq", [P, SEQ], on=part)
            ssq = sb("ssq", [P, SEQ], on=part)
            acc, xf, gs, y, y_hi, y_lo = (a[:, n, :].rearrange("p (q n) -> p q n", q=2) for a, n in
                                          ((e1, 0), (e1, 1), (e2, 0), (e2, 1), (mov_hi, 0), (mov_lo, 0)))
            attn, ms, rms, rinv = bcacc, z[:, :], zabs[:, :], zexp[:, :]
            zero = sb("zero", [P, 1], on=part)

        with ExitStack() as part:
            shw_hi = sb("shw_hi", [P, KE, 2 * SHARED_INNER], F32R, on=part)
            shw_lo = sb("shw_lo", [P, KE, 2 * SHARED_INNER], F32R, on=part)
            shd_hi = sb("shd_hi", [P, SH_CHUNKS, EMB], F32R, on=part)
            shd_lo = sb("shd_lo", [P, SH_CHUNKS, EMB], F32R, on=part)
            ew = sb("ew", [P, 2, ECOLS], on=part)
            ew_hi = sb("ew_hi", [P, 2, ECOLS], F32R, on=part)
            ew_lo = sb("ew_lo", [P, 2, SEL_AT], F32R, on=part)
            hs = sb("hs", [P, 2, SEQ], on=part)
            hw = sb("hw", [P, 2, SEQ], on=part)
            hw_hi = sb("hw_hi", [P, 2, SEQ], F32R, on=part)
            hw_lo = sb("hw_lo", [P, 2, SEQ], F32R, on=part)
            res = sb("res", [P, KE, SEQ], on=part)

        bank = [ctx.enter_context(nc.psum_tensor(f"bank{i}", [P, SEQ], F32)) for i in range(8)]
        p_hid, p_gate, p_turn, p_y = bank[0:4]
        p_out = bank[4:6]
        p_mean, p_var = bank[0:2], bank[2:4]
        p_inner, p_comb, p_moe = bank[0:2], bank[2:4], bank[4:8]

        S = {}
        for name in """setup consts_cast setup_hi setup_lo setup_raw silu_c mod_mm mod_copied mod_chain aneg_exp aneg_done
            mean centred squared variance var_eps std_done rstd_done xhat normed normed_hi normed_lo
            dt_mm z_done dt_abs dt_exp dt_ln dt_plus dt_turned dt_done at_done at_split_hi at_split_lo
            bc_mm bc_tap0 bc_taps bc_silu g_mm g_done mov_hi mov_lo seg_mm seg_exp seg_done
            wi0 wi1 wo0 wo1 wi_hi wi_lo wo_hi wo_lo
            hid gate tap0 taps silu_x silu_g turned xt_done m_done ssm y_skip y_done y_sq y_hi y_lo
            out_mm ssq_done ssq_zero ssq_mm ssq_var ssq_std ssq_inv attn_scaled attn_res
            logit lsub_done lexp_done router_chain comb_split comb_done comb_turned comb_copied
            ew0 ew1 ew_hi ew_lo inner inner_silu prod weighted hw_hi hw_lo expert_mm result stored zero_set""".split():
            S[name] = sem(name)

        block = ctx.enter_context(nc.Block())

        def modcol(which, k, b):
            return mod[:, which * KE + k, bass.ds(b, 1)]

        SETUP = 16 * 16

        @block.sync
        def _(sp):
            for dst, src in ((consts[:, :], const), (cvec[:, :, :], c_t), (modw[:, :, :], mod_w),
                             (scal[:, :, :], scalars), (bcw[:, :, :, :], bc_w), (bcc[:, :, :], bc_conv),
                             (dtw[:, :, :], dt_w), (dtb[:, :], dt_bias),
                             (alog[:, :], a_log.partition_broadcast(P)), (gatew[:, :, :], gate_w),
                             (shw[:, :, :], shared_w), (shd[:, :, :], shared_d)):
                sp.dma_start(dst, src).then_inc(S["setup"], 16)
            for b in range(BATCH):
                x = slice(b * SEQ, (b + 1) * SEQ)
                sp.dma_start(x_all[:, :, x], x_t[:, :, x]).then_inc(S["setup"], 16)
            with sp.Fori(0, BATCH) as b:
                with sp.Fori(0, PAIRS // 2) as jj:
                    for par in range(2):
                        g = b * PAIRS + 2 * jj + par
                        sp.wait_ge(S["wi_lo"], START["wi_lo"] + g - 1)
                        sp.dma_start(wi[:, par, :], in_w[bass.ds(2 * jj + par, 1), :, :].rearrange("a p n -> p (a n)"))\
                            .then_inc(S[f"wi{par}"], 16)
                        sp.wait_ge(S["wo_lo"], START["wo_lo"] + g - 1)
                        sp.dma_start(wo[:, par, :], out_w[bass.ds(2 * jj + par, 1), :, :].rearrange("a p n -> p (a n)"))\
                            .then_inc(S[f"wo{par}"], 16)
            sp.wait_ge(S["comb_copied"], BATCH)

            def load_piece(hf, c, par):
                sp.wait_ge(S["ew_lo"], START["ew_lo"] + hf * ECHUNKS + c - 1)
                sp.dma_start(ew[:, par, :], expert_w[bass.ds(c, 1), :, :].rearrange("a p n -> p (a n)"))\
                    .then_inc(S[f"ew{par}"], 16)

            with sp.Fori(0, HALVES) as hf:
                with sp.Fori(0, ECHUNKS // 2) as cc:
                    for par in range(2):
                        load_piece(hf, 2 * cc + par, par)
                for q in range(BPH):
                    b = hf * BPH + q
                    sp.wait_ge(S["result"], START["result"] + (b + 1) * KE)
                    sp.dma_start(out_t[:, :, bass.ds(b * SEQ, SEQ)], res[:, :, :]).then_inc(S["stored"], 16)
            sp.wait_ge(S["stored"], START["stored"] + 16 * BATCH)

        @block.tensor
        def _(pe):
            mm = nc.tensor.matmul

            def split_mm(out, w_hi, w_lo, x_hi, x_lo, first, last):
                mm(out, w_hi, x_hi, start=first, stop=False)
                mm(out, w_hi, x_lo, start=False, stop=False)
                return mm(out, w_lo, x_hi, start=False, stop=last)

            def norm(phase):
                def mean(b):
                    r = phase * BATCH + b
                    if r >= 2:
                        pe.wait_ge(S["centred"], (r - 1) * KE)
                    for k in range(KE):
                        i = mm(p_mean[r % 2][:, :], ones, x_all[:, k, b * SEQ:(b + 1) * SEQ], start=k == 0, stop=k == KE - 1)
                    i.then_inc(S["mean"], 1)

                mean(0)
                for b in range(BATCH):
                    r = phase * BATCH + b
                    if b + 1 < BATCH:
                        mean(b + 1)
                    pe.wait_ge(S["squared"], r + 1)
                    if r >= 2:
                        pe.wait_ge(S["var_eps"], r - 1)
                    for k in range(KE):
                        i = mm(p_var[r % 2][:, :], ones, xsq[:, r % 2, k, :], start=k == 0, stop=k == KE - 1)
                    i.then_inc(S["variance"], 1)

            def slot(b, j, par, do_in=True, do_mid=True, do_out="mid"):
                g = b * PAIRS + j
                x = bass.ds(b * SEQ, SEQ)
                if do_mid:
                    q = 1 - par
                    pe.wait_ge(S["silu_x"], g)
                    pe.wait_ge(S["xt_done"], START["xt_done"] + g - 1)
                    for t in range(TILES):
                        i = nc.tensor.transpose(p_turn[:, t * P:(t + 1) * P], xf[:, q, t * P:(t + 1) * P], ident)
                    i.then_inc(S["turned"], 1)
                if do_in:
                    pe.wait_ge(S["wi_lo"], START["wi_lo"] + g + 1)
                    pe.wait_ge(S["taps"], START["taps"] + (TAPS - 1) * g)
                    for k in range(KE):
                        w = slice((KE + k) * P, (KE + k + 1) * P)
                        i = split_mm(p_hid[:, :], wi_hi[:, par, w], wi_lo[:, par, w], h_hi[:, k, x], h_lo[:, k, x],
                                     k == 0, k == KE - 1)
                    i.then_inc(S["hid"], 1)
                    pe.wait_ge(S["silu_g"], START["silu_g"] + g)
                    for k in range(KE):
                        w = slice(k * P, (k + 1) * P)
                        i = split_mm(p_gate[:, :], wi_hi[:, par, w], wi_lo[:, par, w], h_hi[:, k, x], h_lo[:, k, x],
                                     k == 0, k == KE - 1)
                    i.then_inc(S["gate"], 1)
                if do_mid:
                    pe.wait_ge(S["xt_done"], START["xt_done"] + g)
                    pe.wait_ge(S["m_done"], g)
                    pe.wait_ge(S["y_skip"], START["y_skip"] + g - 1)
                    for t in range(TILES):
                        for hd in range(2):
                            i = mm(p_y[:, t * P:(t + 1) * P], xt[:, t, hd * HEAD_DIM:hd * HEAD_DIM + P], m[:, t, hd, :],
                                   start=hd == 0, stop=hd == 1)
                    i.then_inc(S["ssm"], 1)
                if do_out:
                    pe.wait_ge(S["y_lo"], g - 1)
                    pe.wait_ge(S["wo_lo"], START["wo_lo"] + g - 1)
                    for k in range(KE):
                        w = slice(k * P, (k + 1) * P)
                        i = split_mm(p_out[k][:, :], wo_hi[:, par, w], wo_lo[:, par, w], y_hi[:, par, :], y_lo[:, par, :],
                                     do_out == "first", do_out == "last")
                    i.then_inc(S["out_mm"], 1)

            pe.wait_ge(S["setup"], SETUP)
            pe.wait_ge(S["silu_c"], 1)
            for n in range(6 * KE):
                for k in range(KE):
                    i = mm(p_out[0][:, n * BATCH:(n + 1) * BATCH], modw[:, k, n * P:(n + 1) * P], cact[:, k, :],
                           start=k == 0, stop=k == KE - 1)
            i.then_inc(S["mod_mm"], 1)
            norm(0)

            pe.wait_ge(S["setup_lo"], 3)
            pe.wait_ge(S["normed_lo"], BATCH * KE)
            with pe.Fori(0, BATCH) as b:
                x0 = b * SEQ
                pe.wait_ge(S["attn_res"], START["attn_res"] + b * KE)
                x = bass.ds(b * SEQ, SEQ)
                for p, hi, lo, done in ((p_turn, dtw_hi, dtw_lo, "dt_mm"), (p_hid, bcw_hi[:, 0], bcw_lo[:, 0], "bc_mm"),
                                        (p_gate, bcw_hi[:, 1], bcw_lo[:, 1], "bc_mm")):
                    for k in range(KE):
                        i = split_mm(p[:, :], hi[:, k, :], lo[:, k, :], h_hi[:, k, x], h_lo[:, k, x],
                                     k == 0, k == KE - 1)
                    i.then_inc(S[done], 1)
                pe.wait_ge(S["dt_plus"], b + 1)
                for t in range(TILES):
                    i = nc.tensor.transpose(p_y[:, t * P:(t + 1) * P], dt_head[:, t * P:(t + 1) * P], ident)
                i.then_inc(S["dt_turned"], 1)
                pe.wait_ge(S["bc_silu"], 2 * b + 2)
                for t in range(TILES):
                    i = mm(p_out[0][:, t * P:(t + 1) * P], bcf[:, 0, t * P:(t + 1) * P], bcf[:, 1, t * P:(t + 1) * P],
                           start=True, stop=True)
                i.then_inc(S["g_mm"], 1)
                with pe.Fori(0, TILES) as t:
                    for n in range(UNITS_PER_TILE):
                        r = (b * TILES + t) * UNITS_PER_TILE + n
                        pe.wait_ge(S["mov_lo"], r + 1)
                        for c in range(2):
                            pe.wait_ge(S["seg_exp"], START["seg_exp"] + 4 * r + 2 * c - 2)
                            col = slice(c * SEQ, (c + 1) * SEQ)
                            hi, lo = mov_hi[:, n, col], mov_lo[:, n, col]
                            heads = bass.ds(t * HEADS + n * HPU + c * (HPU // 2), HPU // 2)
                            mm(bank[c][:, :], later_r, hi, start=True, stop=False)
                            mm(bank[c][:, :], later_r, lo, start=False, stop=False)
                            mm(bank[c][:, :], ident_r, mask_r[:, None, :].broadcast_to([P, HPU // 2, CHUNK]),
                               start=False, stop=True).then_inc(S["seg_mm"], 1)
                            mm(bank[2 + c][:, :], same_r, hi, start=True, stop=False)
                            mm(bank[2 + c][:, :], same_r, lo, start=False, stop=False)
                            for part_ in (at_hi, at_lo):
                                a = part_[:, :, :].rearrange("p t h -> p (t h)")[:, heads]
                                i = mm(bank[2 + c][:, :], later_r, a[:, :, None].broadcast_to([P, HPU // 2, CHUNK]),
                                       start=False, stop=part_ is at_lo)
                            i.then_inc(S["seg_mm"], 1)
                pe.wait_ge(S["seg_exp"], START["seg_exp"] + 4 * (b + 1) * TILES * UNITS_PER_TILE)
                pe.wait_ge(S["g_done"], 2 * (b + 1))

                slot(b, 0, 0, do_mid=False, do_out="")
                slot(b, 1, 1, do_out="")
                slot(b, 2, 0, do_out="first")
                slot(b, 3, 1)
                with pe.Fori(2, PAIRS // 2) as jj:
                    slot(b, 2 * jj, 0)
                    slot(b, 2 * jj + 1, 1)
                slot(b, PAIRS, 0, do_in=False)
                slot(b, PAIRS + 1, 1, do_in=False, do_mid=False, do_out="last")

                pe.wait_ge(S["ssq_done"], START["ssq_done"] + (b + 1) * PAIRS)
                mm(p_hid[:, :], ones, ssq[:, :], start=True, stop=True).then_inc(S["ssq_mm"], 1)

            pe.wait_ge(S["attn_res"], START["attn_res"] + BATCH * KE)
            norm(1)
            for b in range(BATCH):
                pe.wait_ge(S["normed_lo"], (BATCH + b + 1) * KE)
                if b >= 1:
                    pe.wait_ge(S["lsub_done"], b)
                for t in range(TILES):
                    x = slice(b * SEQ + t * P, b * SEQ + (t + 1) * P)
                    for k in range(KE):
                        i = split_mm(bank[4][:, t * EXPERTS:(t + 1) * EXPERTS], h_hi[:, k, x], h_lo[:, k, x],
                                     gatew_hi[:, k, :], gatew_lo[:, k, :], k == 0, k == KE - 1)
                i.then_inc(S["logit"], 1)
                pe.wait_ge(S["comb_done"], 2 * (b + 1))
                if b >= 1:
                    pe.wait_ge(S["comb_copied"], b)
                for t in range(TILES):
                    i = nc.tensor.transpose(bank[5][:, t * P:(t + 1) * P], comb[:, t, :], ident)
                i.then_inc(S["comb_turned"], 1)

            pe.wait_ge(S["comb_copied"], BATCH)
            pe.wait_ge(S["setup_lo"], 5)

            def inner_expert(u, hf, c, par, q):
                pe.wait_ge(S["ew_lo"], START["ew_lo"] + hf * ECHUNKS + c + 1)
                pe.wait_ge(S["weighted"], START["weighted"] + u - 1)
                x = bass.ds((hf * BPH + q) * SEQ, SEQ)
                for k in range(KE):
                    w = slice(k * P, (k + 1) * P)
                    split_mm(p_inner[q][:, :], ew_hi[:, par, w], ew_lo[:, par, w], h_hi[:, k, x], h_lo[:, k, x],
                             k == 0, k == KE - 1)
                mm(p_comb[q][:, :], ew_hi[:, par, SEL_AT:], comb_t[:, x], start=True, stop=True)\
                    .then_inc(S["inner"], 1)

            def down(u, w_hi, w_lo, rows, q, first=False, last=False):
                hi, lo = hw_hi[0:rows, q, :], hw_lo[0:rows, q, :]
                pe.wait_ge(S["hw_hi"], START["hw_hi"] + u + 1)
                for k in range(KE):
                    w = slice(k * P, (k + 1) * P)
                    mm(p_moe[q * KE + k][:, :], w_hi[0:rows, w], hi, start=first, stop=False)
                    mm(p_moe[q * KE + k][:, :], w_lo[0:rows, w], hi, start=False, stop=False)
                pe.wait_ge(S["weighted"], START["weighted"] + u + 1)
                for k in range(KE):
                    i = mm(p_moe[q * KE + k][:, :], w_hi[0:rows, k * P:(k + 1) * P], lo, start=False, stop=last)
                i.then_inc(S["expert_mm"], 1)

            with pe.Fori(0, HALVES) as hf:
                base = hf * UNITS
                pe.wait_ge(S["result"], START["result"] + hf * BPH * KE)

                def shared_rows(n):
                    return min(P, SHARED_INNER - n * P)

                def inner_shared(u):
                    n, q = divmod(u, BPH)
                    rows = shared_rows(n)
                    pe.wait_ge(S["weighted"], START["weighted"] + base + u - 1)
                    x = bass.ds((hf * BPH + q) * SEQ, SEQ)
                    for p, at_ in ((p_inner[q], 0), (p_comb[q], SHARED_INNER)):
                        for k in range(KE):
                            w = slice(at_ + n * P, at_ + n * P + rows)
                            i = split_mm(p[0:rows, :], shw_hi[:, k, w], shw_lo[:, k, w], h_hi[:, k, x], h_lo[:, k, x],
                                         k == 0, k == KE - 1)
                    i.then_inc(S["inner"], 1)

                def down_shared(u):
                    n, q = divmod(u, BPH)
                    down(base + u, shd_hi[:, n, :], shd_lo[:, n, :], shared_rows(n), q, first=n == 0)

                SU = SH_CHUNKS * BPH
                for u in range(SU):
                    inner_shared(u)
                    if u:
                        down_shared(u - 1)
                inner_expert(base + SU, hf, 0, 0, 0)
                down_shared(SU - 1)

                def piece(c, par, last=False):
                    u = base + SU + c * BPH
                    w_hi, w_lo = ew_hi[:, par, E2_AT:SEL_AT], ew_lo[:, par, E2_AT:SEL_AT]
                    inner_expert(u + 1, hf, c, par, 1)
                    down(u, w_hi, w_lo, P, 0, last=last)
                    if not last:
                        inner_expert(u + 2, hf, c + 1, 1 - par, 0)
                    down(u + 1, w_hi, w_lo, P, 1, last=last)

                with pe.Fori(0, ECHUNKS // 2 - 1) as cc:
                    piece(2 * cc, 0)
                    piece(2 * cc + 1, 1)
                piece(ECHUNKS - 2, 0)
                piece(ECHUNKS - 1, 1, True)

        @block.scalar
        def _(act):
            f = nc.scalar.activation

            def high(dst, src):
                return f(dst, src, ACT.Identity)

            act.wait_ge(S["setup"], SETUP)
            f(cact[:, :, :], cvec[:, :, :], ACT.Silu).then_inc(S["silu_c"], 1)
            f(consts_r[:, :], consts[:, 0:3 * P + 2 * CHUNK], ACT.Identity).then_inc(S["consts_cast"], 1)
            for dst, src in ((dtw_hi, dtw), (bcw_hi, bcw), (gatew_hi, gatew)):
                high(dst[:], src[:]).then_inc(S["setup_hi"], 1)
            f(aexp[:, :], alog[:, :], ACT.Exp).then_inc(S["aneg_exp"], 1)

            def norm(phase):
                def square(b):
                    r = phase * BATCH + b
                    act.wait_ge(S["centred"], (r + 1) * KE)
                    if r >= 2:
                        act.wait_ge(S["variance"], r - 1)
                    f(xsq[:, r % 2], xc[:, r % 2], ACT.Square).then_inc(S["squared"], 1)

                square(0)
                for b in range(BATCH):
                    r = phase * BATCH + b
                    if b + 1 < BATCH:
                        square(b + 1)
                    act.wait_ge(S["var_eps"], r + 1)
                    if r >= 2:
                        act.wait_ge(S["rstd_done"], r - 1)
                    f(std[:, r % 2, :], var[:, r % 2, :], ACT.Sqrt).then_inc(S["std_done"], 1)
                    act.wait_ge(S["xhat"], r + 1)
                    if r >= 2:
                        act.wait_ge(S["normed_lo"], (r - 1) * KE)
                    for k in range(KE):
                        f(h[:, r % 2, k, :], xc[:, r % 2, k, :], ACT.Identity, bias=mod[:, 3 * phase * KE + k, b:b + 1],
                          scale=mod[:, (3 * phase + 1) * KE + k, b:b + 1]).then_inc(S["normed"], 1)
                        act.wait_ge(S["normed"], r * KE + k + 1)
                        high(h_hi[:, k, b * SEQ:(b + 1) * SEQ], h[:, r % 2, k, :]).then_inc(S["normed_hi"], 1)

            def take_in(b, j, par):
                g = b * PAIRS + j
                act.wait_ge(S[f"wi{par}"], 8 * (g - par) + 16)
                act.wait_ge(S["gate"], START["gate"] + g - 1)
                high(wi_hi[:, par, :], wi[:, par, :]).then_inc(S["wi_hi"], 1)

            def slot(b, j, par, do_in=True, next_in=True, take_out=True, finish=True):
                g = b * PAIRS + j
                if finish:
                    act.wait_ge(S["y_done"], START["y_done"] + g - 1)
                    act.wait_ge(S["out_mm"], START["out_mm"] + g - 3)
                    f(y_hi[:, par, :], y[:, par, :], ACT.Identity, scale=scal[:, bass.ds(j - 2, 1), NW_AT:NW_AT + 1]
                      .rearrange("p a n -> p (a n)")).then_inc(S["y_hi"], 1)
                    act.wait_ge(S["ssq_done"], START["ssq_done"] + g - 2)
                    f(ysq[:, :], y[:, par, :], ACT.Square).then_inc(S["y_sq"], 1)
                if do_in:
                    def col(at_):
                        return scal[:, bass.ds(j, 1), at_:at_ + 1].rearrange("p a n -> p (a n)")

                    act.wait_ge(S["hid"], g + 1)
                    f(acc[:, par, :], p_hid[:, :], ACT.Identity, bias=col(TAP_AT + TAPS),
                      scale=col(TAP_AT + TAPS - 1)).then_inc(S["tap0"], 1)
                if next_in:
                    take_in(b, j + 1, 1 - par)
                if do_in:
                    act.wait_ge(S["gate"], START["gate"] + g + 1)
                    f(gs[:, par, :], p_gate[:, :], ACT.Silu).then_inc(S["silu_g"], 1)
                    act.wait_ge(S["taps"], START["taps"] + (TAPS - 1) * (g + 1))
                    f(xf[:, par, :], acc[:, par, :], ACT.Silu).then_inc(S["silu_x"], 1)
                if take_out:
                    q = 1 - par
                    act.wait_ge(S[f"wo{q}"], 8 * (g - 1 - q) + 16)
                    act.wait_ge(S["out_mm"], START["out_mm"] + g - 2)
                    high(wo_hi[:, q, :], wo[:, q, :]).then_inc(S["wo_hi"], 1)

            act.wait_ge(S["mod_chain"], 10)
            norm(0)
            with act.Fori(0, BATCH) as b:
                act.wait_ge(S["z_done"], 2 * b + 2)
                f(zexp[:, :], zabs[:, :], ACT.Exp, scale=-1.0).then_inc(S["dt_exp"], 1)
                act.wait_ge(S["dt_exp"], b + 1)
                f(zln[:, :], zexp[:, :], ACT.Ln, bias=1.0).then_inc(S["dt_ln"], 1)
                for n, p in enumerate((p_hid, p_gate)):
                    act.wait_ge(S["bc_mm"], 2 * b + n + 1)
                    f(bcacc[:, n, :], p[:, :], ACT.Identity, bias=bcc[:, n, TAPS:TAPS + 1],
                      scale=bcc[:, n, TAPS - 1:TAPS]).then_inc(S["bc_tap0"], 1)
                act.wait_ge(S["at_done"], b + 1)
                high(at_hi[:, :, :], at[:, :, :]).then_inc(S["at_split_hi"], 1)
                act.wait_ge(S["bc_taps"], 2 * (TAPS - 1) * (b + 1))
                for n in range(2):
                    f(bcf[:, n, :], bcacc[:, n, :], ACT.Silu).then_inc(S["bc_silu"], 1)
                with act.Fori(0, TILES) as t:
                    for n in range(UNITS_PER_TILE):
                        r = (b * TILES + t) * UNITS_PER_TILE + n
                        act.wait_ge(S["seg_done"], START["seg_done"] + r - 1)
                        for c in range(2):
                            act.wait_ge(S["seg_mm"], START["seg_mm"] + 4 * r + 2 * c + 2)
                            f(e1[:, n, c * SEQ:(c + 1) * SEQ], bank[c][:, :], ACT.Exp).then_inc(S["seg_exp"], 1)
                            f(e2[:, n, c * SEQ:(c + 1) * SEQ], bank[2 + c][:, :], ACT.Exp).then_inc(S["seg_exp"], 1)

                take_in(b, 0, 0)
                act.wait_ge(S["seg_done"], START["seg_done"] + (b + 1) * TILES * UNITS_PER_TILE)
                slot(b, 0, 0, take_out=False, finish=False)
                slot(b, 1, 1, finish=False)
                with act.Fori(1, PAIRS // 2 - 1) as jj:
                    slot(b, 2 * jj, 0)
                    slot(b, 2 * jj + 1, 1)
                slot(b, PAIRS - 2, 0)
                slot(b, PAIRS - 1, 1, next_in=False)
                slot(b, PAIRS, 0, do_in=False, next_in=False)
                slot(b, PAIRS + 1, 1, do_in=False, next_in=False, take_out=False)

                act.wait_ge(S["ssq_var"], b + 1)
                f(rms, ms, ACT.Sqrt).then_inc(S["ssq_std"], 1)

            act.wait_ge(S["attn_res"], START["attn_res"] + BATCH * KE)
            norm(1)
            act.wait_ge(S["setup_raw"], 3)
            for dst, src in ((shw_hi, shw), (shd_hi, shd)):
                high(dst[:], src[:]).then_inc(S["setup_hi"], 1)
            for b in range(BATCH):
                act.wait_ge(S["lsub_done"], b + 1)
                f(lexp[:, :, :], lsub[:, :, :], ACT.Exp).then_inc(S["lexp_done"], 1)
                act.wait_ge(S["comb_turned"], b + 1)
                f(comb_t[:, b * SEQ:(b + 1) * SEQ], bank[5][:, :], ACT.Identity).then_inc(S["comb_copied"], 1)

            def take_piece(hf, c, par, free):
                act.wait_ge(S[f"ew{par}"], 8 * (hf * ECHUNKS + c - par) + 16)
                act.wait_ge(S["expert_mm"], START["expert_mm"] + free)
                high(ew_hi[:, par, :], ew[:, par, :]).then_inc(S["ew_hi"], 1)

            def unit(u, q, rows=P):
                act.wait_ge(S["inner"], u + 1)
                act.wait_ge(S["weighted"], START["weighted"] + u - 1)
                f(hs[0:rows, q, :], p_inner[q][0:rows, :], ACT.Silu).then_inc(S["inner_silu"], 1)
                act.wait_ge(S["prod"], u + 1)
                act.wait_ge(S["expert_mm"], START["expert_mm"] + u - 1)
                high(hw_hi[0:rows, q, :], hw[0:rows, q, :]).then_inc(S["hw_hi"], 1)

            SU = SH_CHUNKS * BPH
            with act.Fori(0, HALVES) as hf:
                take_piece(hf, 0, 0, hf * UNITS)
                for u in range(SU):
                    unit(hf * UNITS + u, u % BPH, min(P, SHARED_INNER - u // BPH * P))
                take_piece(hf, 1, 1, hf * UNITS)

                def piece(c, par, more=True):
                    u = hf * UNITS + SU + BPH * c
                    unit(u, 0)
                    if more:
                        take_piece(hf, c + 1, 1 - par, u)
                    unit(u + 1, 1)

                piece(0, 0, more=False)
                piece(1, 1)
                with act.Fori(1, ECHUNKS // 2 - 1) as cc:
                    piece(2 * cc, 0)
                    piece(2 * cc + 1, 1)
                piece(ECHUNKS - 2, 0)
                piece(ECHUNKS - 1, 1, more=False)

        @block.vector
        def _(dve):
            v = nc.vector

            def low(dst, src, hi):
                return v.tensor_tensor(dst, src, hi.bitcast(F32), ALU.subtract)

            for n, (name, count) in enumerate(START.items()):
                v.memset(start[:, n:n + 1], 0.0).then_inc(S[name], count)

            dve.wait_ge(S["setup"], SETUP)
            dve.wait_ge(S["setup_hi"], 3)
            for dst, src, hi in ((dtw_lo, dtw, dtw_hi), (bcw_lo, bcw, bcw_hi), (gatew_lo, gatew, gatew_hi)):
                low(dst[:], src[:], hi[:]).then_inc(S["setup_lo"], 1)

            dve.wait_ge(S["mod_mm"], 1)
            v.tensor_copy(mod[:, :, :], p_out[0][:, 0:6 * KE * BATCH].rearrange("p (n b) -> p n b", b=BATCH))\
                .then_inc(S["mod_chain"], 1)
            dve.wait_ge(S["mod_chain"], 1)
            dve.wait_ge(S["aneg_exp"], 1)
            v.tensor_scalar(aneg[:, :], aexp[:, :], -1.0, None, ALU.mult).then_inc(S["aneg_done"], 1)
            for n in (1, 4):
                c = mod[:, n * KE:(n + 1) * KE, :]
                v.tensor_scalar(c, c, 1.0, None, ALU.add)
            for n, w in enumerate((2, 5)):
                g = mod[:, w * KE:(w + 1) * KE, :]
                v.tensor_scalar(gneg[:, n], g, -1.0, None, ALU.mult)
                v.tensor_scalar(gsign[:, n], g, 0.0, 2.0, ALU.is_ge, ALU.mult).then_inc(S["mod_chain"], 1)
            dve.wait_ge(S["mod_chain"], 3)
            for n, w in enumerate((2, 5)):
                g = mod[:, w * KE:(w + 1) * KE, :]
                v.tensor_tensor(gmag[:, n], g, gneg[:, n], ALU.max).then_inc(S["mod_chain"], 1)
            dve.wait_ge(S["mod_chain"], 5)
            v.tensor_scalar(gmag[:, :], gmag[:, :], 0.25, None, ALU.max).then_inc(S["mod_chain"], 1)
            v.tensor_scalar(gsign[:, :], gsign[:, :], -1.0, None, ALU.add).then_inc(S["mod_chain"], 1)
            dve.wait_ge(S["mod_chain"], 7)
            for n, w in enumerate((2, 5)):
                v.tensor_tensor(mod[:, w * KE:(w + 1) * KE, :], gmag[:, n], gsign[:, n], ALU.mult)\
                    .then_inc(S["mod_chain"], 1)
            dve.wait_ge(S["mod_chain"], 9)
            v.memset(start[:, 0:1], 0.0).then_inc(S["mod_chain"], 1)

            def norm(phase):
                def centre(b):
                    r = phase * BATCH + b
                    dve.wait_ge(S["mean"], r + 1)
                    if r >= 2:
                        dve.wait_ge(S["normed"], (r - 1) * KE)
                        dve.wait_ge(S["squared"], r - 1)
                    for k in range(KE):
                        v.scalar_tensor_tensor(xc[:, r % 2, k, :], p_mean[r % 2][:, :], -1.0 / EMB,
                                               x_all[:, k, b * SEQ:(b + 1) * SEQ], ALU.mult, ALU.add)\
                            .then_inc(S["centred"], 1)

                centre(0)
                for b in range(BATCH):
                    r = phase * BATCH + b
                    if b + 1 < BATCH:
                        if b + 1 >= 2:
                            split(b - 1, phase)
                        centre(b + 1)
                    dve.wait_ge(S["variance"], r + 1)
                    if r >= 2:
                        dve.wait_ge(S["std_done"], r - 1)
                    v.tensor_scalar(var[:, r % 2, :], p_var[r % 2][:, :], 1.0 / EMB, EPS, ALU.mult, ALU.add)\
                        .then_inc(S["var_eps"], 1)
                    dve.wait_ge(S["std_done"], r + 1)
                    v.reciprocal(rstd[:, r % 2, :], std[:, r % 2, :]).then_inc(S["rstd_done"], 1)
                    dve.wait_ge(S["rstd_done"], r + 1)
                    dve.wait_ge(S["squared"], r + 1)
                    v.tensor_tensor(xc[:, r % 2], xc[:, r % 2], rstd[:, r % 2, None, :].broadcast_to([P, KE, SEQ]),
                                    ALU.mult).then_inc(S["xhat"], 1)
                for b in (BATCH - 2, BATCH - 1):
                    split(b, phase)

            def split(b, phase):
                r = phase * BATCH + b
                dve.wait_ge(S["normed_hi"], (r + 1) * KE)
                for k in range(KE):
                    x = slice(b * SEQ, (b + 1) * SEQ)
                    low(h_lo[:, k, x], h[:, r % 2, k, :], h_hi[:, k, x]).then_inc(S["normed_lo"], 1)

            def conv(dst, src, taps, done, base):
                for d in range(1, TAPS):
                    if d > 1:
                        dve.wait_ge(S[done], START.get(done, 0) + base + d - 1)
                    v.scalar_tensor_tensor(dst[:, d:], src[:, 0:SEQ - d], taps(TAPS - 1 - d), dst[:, d:],
                                           ALU.mult, ALU.add).then_inc(S[done], 1)

            def moving(b, t, n):
                r = (b * TILES + t) * UNITS_PER_TILE + n
                dve.wait_ge(S["seg_mm"], START["seg_mm"] + 4 * (r - 1))
                a = at[:, :, :].rearrange("p t h -> p (t h)")[:, bass.ds(t * HEADS + n * HPU, HPU)]
                v.tensor_tensor(mov_hi[:, n, :].rearrange("p (h l) -> p h l", l=CHUNK),
                                a[:, :, None].broadcast_to([P, HPU, CHUNK]),
                                upto[:, None, :].broadcast_to([P, HPU, CHUNK]), ALU.mult).then_inc(S["mov_hi"], 1)

            def segments(b, t, n):
                r = (b * TILES + t) * UNITS_PER_TILE + n
                dve.wait_ge(S["seg_exp"], START["seg_exp"] + 4 * (r + 1))
                J = PAIRS // UNITS_PER_TILE
                out = el[:, n * J:(n + 1) * J, bass.ds(t, 1), :, :].rearrange("p j a h l -> p j (a h l)")
                v.tensor_tensor(out, e1[:, n, :].rearrange("p (j n) -> p j n", j=J),
                                e2[:, n, :].rearrange("p (j n) -> p j n", j=J), ALU.add).then_inc(S["seg_done"], 1)

            def slot(b, j, par, do_in=True, do_mid=True, finish=True):
                g = b * PAIRS + j
                q = 1 - par

                def col(pair, at_):
                    return scal[:, bass.ds(pair, 1), at_:at_ + 1].rearrange("p a n -> p (a n)")

                if do_mid:
                    dve.wait_ge(S["ssm"], START["ssm"] + g - 1)
                    e = el[:, bass.ds(j - 1, 1), :, :, :].rearrange("p a t h l -> p (a t h) l")
                    v.tensor_tensor(m[:, :, :, :].rearrange("p t h (r l) -> p (t h) r l", l=CHUNK),
                                    e[:, :, None, :].broadcast_to([P, TILES * 2, CPT, CHUNK]),
                                    gmask[:, :, :, :].rearrange("p t h (r l) -> p (t h) r l", l=CHUNK), ALU.mult)\
                        .then_inc(S["m_done"], 1)
                    dve.wait_ge(S["turned"], g)
                    d = dt[:, :, bass.ds(2 * (j - 1), 2)]
                    v.tensor_tensor(xt[:, :, :].rearrange("p t (a n) -> p t a n", a=3)[:, :, 0:3:2, :],
                                    p_turn[:, :].rearrange("p (t a n) -> p t a n", t=TILES, a=2),
                                    d[:, :, :, None].broadcast_to([P, TILES, 2, HEAD_DIM]), ALU.mult)\
                        .then_inc(S["xt_done"], 1)
                if finish:
                    dve.wait_ge(S["y_hi"], START["y_hi"] + g - 1)
                    dve.wait_ge(S["out_mm"], START["out_mm"] + g - 3)
                    v.scalar_tensor_tensor(y_lo[:, par, :], y[:, par, :], col(j - 2, NW_AT), y_hi[:, par, :].bitcast(F32),
                                           ALU.mult, ALU.subtract).then_inc(S["y_lo"], 1)
                if do_in:
                    dve.wait_ge(S["tap0"], g + 1)
                    conv(acc[:, par, :], p_hid, lambda n: col(j, TAP_AT + n), "taps", (TAPS - 1) * g)
                if do_mid:
                    dve.wait_ge(S["ssm"], START["ssm"] + g)
                    v.scalar_tensor_tensor(yt[:, :], xf[:, q, :], col(j - 1, D_AT), p_y[:, :], ALU.mult, ALU.add)\
                        .then_inc(S["y_skip"], 1)
                    dve.wait_ge(S["y_skip"], START["y_skip"] + g)
                    dve.wait_ge(S["y_sq"], START["y_sq"] + g - 2)
                    v.tensor_tensor(y[:, q, :], yt[:, :], gs[:, q, :], ALU.mult).then_inc(S["y_done"], 1)

            norm(0)
            v.memset(xt[:, :, :], 0.0).then_inc(S["aneg_done"], 1)
            with dve.Fori(0, BATCH) as b:
                dve.wait_ge(S["dt_mm"], b + 1)
                v.tensor_scalar(z[:, :], p_turn[:, :], dtb[:, 0:1], None, ALU.add).then_inc(S["z_done"], 1)
                dve.wait_ge(S["z_done"], 2 * b + 1)
                v.scalar_tensor_tensor(zabs[:, :], z[:, :], -1.0, z[:, :], ALU.mult, ALU.max).then_inc(S["z_done"], 1)
                dve.wait_ge(S["dt_ln"], b + 1)
                v.scalar_tensor_tensor(dt_head[:, :], z[:, :], 0.0, zln[:, :], ALU.max, ALU.add)\
                    .then_inc(S["dt_plus"], 1)
                for n, p in enumerate((p_hid, p_gate)):
                    dve.wait_ge(S["bc_tap0"], 2 * b + n + 1)
                    conv(bcacc[:, n, :], p, lambda i, n=n: bcc[:, n, i:i + 1], "bc_taps", (TAPS - 1) * (2 * b + n))
                dve.wait_ge(S["dt_turned"], b + 1)
                v.tensor_copy(dt[:, :, :], p_y[:, :].rearrange("p (t h) -> p t h", t=TILES)[:, :, 0:HEADS])\
                    .then_inc(S["dt_done"], 1)
                dve.wait_ge(S["dt_done"], b + 1)
                v.tensor_tensor(at[:, :, :], dt[:, :, :], aneg[:, None, :].broadcast_to([P, TILES, HEADS]), ALU.mult)\
                    .then_inc(S["at_done"], 1)
                dve.wait_ge(S["at_split_hi"], b + 1)
                low(at_lo[:, :, :], at[:, :, :], at_hi[:, :, :]).then_inc(S["at_split_lo"], 1)
                dve.wait_ge(S["g_mm"], b + 1)
                for hd in range(2):
                    v.tensor_tensor(gmask[:, :, hd, :], p_out[0][:, :].rearrange("p (t l) -> p t l", t=TILES),
                                    same[:, None, :].broadcast_to([P, TILES, P]), ALU.mult).then_inc(S["g_done"], 1)
                moving(b, 0, 0)
                with dve.Fori(0, TILES - 1) as t:
                    moving(b, t, 1)
                    segments(b, t, 0)
                    moving(b, t + 1, 0)
                    segments(b, t, 1)
                moving(b, TILES - 1, 1)
                segments(b, TILES - 1, 0)
                segments(b, TILES - 1, 1)
                dve.wait_ge(S["seg_done"], START["seg_done"] + (b + 1) * TILES * UNITS_PER_TILE)

                slot(b, 0, 0, do_mid=False, finish=False)
                slot(b, 1, 1, finish=False)
                with dve.Fori(1, PAIRS // 2) as jj:
                    slot(b, 2 * jj, 0)
                    slot(b, 2 * jj + 1, 1)
                slot(b, PAIRS, 0, do_in=False)
                slot(b, PAIRS + 1, 1, do_in=False, do_mid=False)

                dve.wait_ge(S["ssq_mm"], START["ssq_mm"] + b + 1)
                v.tensor_scalar(ms, p_hid[:, :], 1.0 / INTER, EPS, ALU.mult, ALU.add).then_inc(S["ssq_var"], 1)
                dve.wait_ge(S["ssq_std"], b + 1)
                v.reciprocal(rinv, rms).then_inc(S["ssq_inv"], 1)
                dve.wait_ge(S["ssq_inv"], b + 1)
                dve.wait_ge(S["out_mm"], START["out_mm"] + (b + 1) * PAIRS)
                for k in range(KE):
                    v.tensor_tensor(attn[:, k, :], p_out[k][:, :], rinv, ALU.mult)\
                        .then_inc(S["attn_scaled"], 1)
                dve.wait_ge(S["attn_scaled"], (b + 1) * KE)
                for k in range(KE):
                    xs = x_all[:, k, bass.ds(b * SEQ, SEQ)]
                    v.scalar_tensor_tensor(xs, attn[:, k, :], modcol(2, k, b), xs, ALU.mult, ALU.add)\
                        .then_inc(S["attn_res"], 1)
            dve.wait_ge(S["attn_res"], START["attn_res"] + BATCH * KE)
            norm(1)
            v.memset(comb[:, :, :], 0.0).then_inc(S["setup_raw"], 3)
            dve.wait_ge(S["setup_hi"], 5)
            for dst, src, hi in ((shw_lo, shw, shw_hi), (shd_lo, shd, shd_hi)):
                low(dst[:], src[:], hi[:]).then_inc(S["setup_lo"], 1)

            chain = [0]

            def step(i):
                i.then_inc(S["router_chain"], 1)
                chain[0] = chain[0] + 1
                dve.wait_ge(S["router_chain"], chain[0])

            def wide(a):
                return a[:, :, None].broadcast_to([P, TILES, EXPERTS])

            for b in range(BATCH):
                dve.wait_ge(S["logit"], b + 1)
                logits = bank[4][:, 0:TILES * EXPERTS].rearrange("p (t e) -> p t e", t=TILES)
                step(v.tensor_reduce(lmax[:, :], logits, AX_X, ALU.max))
                v.tensor_tensor(lsub[:, :, :], logits, wide(lmax), ALU.subtract).then_inc(S["lsub_done"], 1)
                dve.wait_ge(S["lexp_done"], b + 1)
                step(v.tensor_reduce(lsum[:, :], lexp[:, :, :], AX_X, ALU.add))
                step(v.reciprocal(lrec[:, :], lsum[:, :]))
                step(v.tensor_tensor(prob[:, :, :], lexp[:, :, :], wide(lrec), ALU.mult))
                for t in range(TILES):
                    i = v.max(top8[:, t, :], prob[:, t, :])
                step(i)
                step(v.memset(top8[:, :, TOP_K:], TINY))
                for t in range(TILES):
                    i = v.match_replace(rest[:, t, :], top8[:, t, :], prob[:, t, :], TINY)
                step(i)
                step(v.scalar_tensor_tensor(kept[:, :, :], rest[:, :, :], 0.0, prob[:, :, :], ALU.max, ALU.subtract))
                step(v.tensor_reduce(ksum[:, :], kept[:, :, :], AX_X, ALU.add))
                step(v.reciprocal(krec[:, :], ksum[:, :]))
                step(v.tensor_tensor(share[:, :, :], kept[:, :, :], wide(krec), ALU.mult))
                if b:
                    dve.wait_ge(S["comb_turned"], b)
                v.tensor_copy(share_hi[:, :, :], share[:, :, :]).then_inc(S["comb_split"], 1)
                dve.wait_ge(S["comb_split"], b + 1)
                v.tensor_copy(comb[:, :, 0:EXPERTS], share_hi[:, :, :].bitcast(F32)).then_inc(S["comb_done"], 1)
                low(comb[:, :, EXPERTS:], share[:, :, :], share_hi[:, :, :]).then_inc(S["comb_done"], 1)

            def unit(u, q, rows=P):
                dve.wait_ge(S["inner_silu"], u + 1)
                dve.wait_ge(S["hw_hi"], START["hw_hi"] + u - 1)
                v.tensor_tensor(hw[0:rows, q, :], hs[0:rows, q, :], p_comb[q][0:rows, :], ALU.mult)\
                    .then_inc(S["prod"], 1)
                dve.wait_ge(S["hw_hi"], START["hw_hi"] + u + 1)
                dve.wait_ge(S["expert_mm"], START["expert_mm"] + u - 1)
                low(hw_lo[0:rows, q, :], hw[0:rows, q, :], hw_hi[0:rows, q, :]).then_inc(S["weighted"], 1)

            with dve.Fori(0, HALVES) as hf:
                for u in range(SH_CHUNKS * BPH):
                    unit(hf * UNITS + u, u % BPH, min(P, SHARED_INNER - u // BPH * P))
                with dve.Fori(0, ECHUNKS) as c:
                    for q in range(BPH):
                        unit(hf * UNITS + (SH_CHUNKS + c) * BPH + q, q)
                dve.wait_ge(S["expert_mm"], START["expert_mm"] + (hf + 1) * UNITS)
                for q in range(BPH):
                    b = hf * BPH + q
                    dve.wait_ge(S["stored"], START["stored"] + 16 * b)
                    for k in range(KE):
                        v.scalar_tensor_tensor(res[:, k, :], p_moe[q * KE + k][:, :], modcol(5, k, b),
                                               x_all[:, k, bass.ds(b * SEQ, SEQ)], ALU.mult, ALU.add)\
                            .then_inc(S["result"], 1)

        @block.gpsimd
        def _(pool):
            g_ = nc.gpsimd

            def low(dst, src, hi):
                return g_.tensor_tensor(dst, src, hi.bitcast(F32), ALU.subtract)

            def take_in(b, j, par):
                g = b * PAIRS + j
                pool.wait_ge(S["wi_hi"], g + 1)
                low(wi_lo[:, par, :], wi[:, par, :], wi_hi[:, par, :]).then_inc(S["wi_lo"], 1)

            def slot(b, j, par, next_in=True, take_out=True, finish=True):
                g = b * PAIRS + j
                if finish:
                    pool.wait_ge(S["y_sq"], START["y_sq"] + g - 1)
                    pool.wait_ge(S["ssq_done"], START["ssq_done"] + g - 2)
                    pool.wait_ge(S["ssq_zero"], b + 1)
                    g_.tensor_tensor(ssq[:, :], ssq[:, :], ysq[:, :], ALU.add).then_inc(S["ssq_done"], 1)
                if next_in:
                    take_in(b, j + 1, 1 - par)
                if take_out:
                    pool.wait_ge(S["wo_hi"], g)
                    low(wo_lo[:, 1 - par, :], wo[:, 1 - par, :], wo_hi[:, 1 - par, :]).then_inc(S["wo_lo"], 1)

            pool.wait_ge(S["normed_lo"], BATCH * KE)
            g_.memset(zero[:, :], 0.0).then_inc(S["zero_set"], 1)
            pool.wait_ge(S["zero_set"], 1)
            g_.memset(ssq[:, :], 0.0).then_inc(S["zero_set"], 1)
            pool.wait_ge(S["zero_set"], 2)
            with pool.Fori(0, BATCH) as b:
                pool.wait_ge(S["ssq_mm"], START["ssq_mm"] + b)
                zeros = zero[:, :].broadcast_to([P, SEQ])
                g_.tensor_tensor(ssq[:, :], zeros, zeros, ALU.add).then_inc(S["ssq_zero"], 1)
                with pool.Fori(0, TILES) as t:
                    for n in range(UNITS_PER_TILE):
                        r = (b * TILES + t) * UNITS_PER_TILE + n
                        pool.wait_ge(S["at_split_lo"], b + 1)
                        pool.wait_ge(S["mov_hi"], r + 1)
                        a = at_lo[:, :, :].bitcast(F32).rearrange("p t h -> p (t h)")[:, bass.ds(t * HEADS + n * HPU, HPU)]
                        g_.tensor_tensor(mov_lo[:, n, :].rearrange("p (h l) -> p h l", l=CHUNK),
                                         a[:, :, None].broadcast_to([P, HPU, CHUNK]),
                                         upto[:, None, :].broadcast_to([P, HPU, CHUNK]), ALU.mult)\
                            .then_inc(S["mov_lo"], 1)

                take_in(b, 0, 0)
                slot(b, 0, 0, take_out=False, finish=False)
                slot(b, 1, 1, finish=False)
                with pool.Fori(1, PAIRS // 2 - 1) as jj:
                    slot(b, 2 * jj, 0)
                    slot(b, 2 * jj + 1, 1)
                slot(b, PAIRS - 2, 0)
                slot(b, PAIRS - 1, 1, next_in=False)
                slot(b, PAIRS, 0, next_in=False)
                slot(b, PAIRS + 1, 1, next_in=False, take_out=False)

            def take_piece(hf, c, par):
                pool.wait_ge(S["ew_hi"], hf * ECHUNKS + c + 1)
                low(ew_lo[:, par, :], ew[:, par, 0:SEL_AT], ew_hi[:, par, 0:SEL_AT]).then_inc(S["ew_lo"], 1)

            with pool.Fori(0, HALVES) as hf:
                with pool.Fori(0, ECHUNKS // 2) as cc:
                    take_piece(hf, 2 * cc, 0)
                    take_piece(hf, 2 * cc + 1, 1)


def kernel(L0_attn_input_states, L0_attn_mask, L0_attn_W_in, L0_attn_conv_w, L0_attn_conv_b, L0_attn_dt_bias,
           L0_attn_A_log, L0_attn_D, L0_attn_norm_w, L0_attn_W_out, L0_ffn_gate_w, L0_ffn_experts_w1,
           L0_ffn_experts_w2, L0_ffn_shared_gate_up, L0_ffn_shared_down, L0_c, L0_wmod):
    import concourse.bacc as bacc
    from concourse.bass_utils import run_bass_kernel_spmd

    def rows(a):
        return a.reshape(-1, P, a.shape[1]).transpose(1, 0, 2)

    x, w_in = np.asarray(L0_attn_input_states), np.asarray(L0_attn_W_in)
    w_gate, w_hid = (w_in[n * INTER:(n + 1) * INTER].reshape(PAIRS, P, KE, P).transpose(0, 3, 2, 1)
                     .reshape(PAIRS, P, KE * P) for n in range(2))
    w_out = np.asarray(L0_attn_W_out).T.reshape(PAIRS, P, EMB)
    conv = np.concatenate([L0_attn_conv_w, np.asarray(L0_attn_conv_b)[:, None]], 1)
    scalars = np.concatenate([np.asarray(L0_attn_norm_w).reshape(PAIRS, P, 1),
                              np.repeat(L0_attn_D, HEAD_DIM).reshape(PAIRS, P, 1),
                              conv[:INTER].reshape(PAIRS, P, TAPS + 1)], 2)
    bc = w_in[2 * INTER:2 * INTER + 2 * STATE].reshape(2, P, KE, P).transpose(3, 0, 2, 1)
    w1 = np.asarray(L0_ffn_experts_w1).reshape(ECHUNKS, P, KE, P).transpose(0, 3, 2, 1).reshape(ECHUNKS, P, KE * P)
    w2 = np.asarray(L0_ffn_experts_w2).transpose(0, 2, 1).reshape(ECHUNKS, P, EMB)
    down = np.zeros((SH_CHUNKS * P, EMB), np.float32)
    down[:SHARED_INNER] = np.asarray(L0_ffn_shared_down).T
    arrays = {
        "x_t": rows(x.reshape(TOKENS, EMB).T),
        "in_w": np.concatenate([w_gate, w_hid], 2),
        "out_w": w_out,
        "scalars": scalars.transpose(1, 0, 2),
        "bc_w": bc,
        "bc_conv": conv[INTER:].reshape(2, P, TAPS + 1).transpose(1, 0, 2),
        "dt_w": rows(np.pad(w_in[2 * INTER + 2 * STATE:].T, ((0, 0), (0, P - HEADS)))),
        "dt_bias": np.pad(np.asarray(L0_attn_dt_bias), (0, P - HEADS))[:, None],
        "a_log": np.asarray(L0_attn_A_log),
        "c_t": rows(np.asarray(L0_c).T),
        "mod_w": rows(np.asarray(L0_wmod)),
        "gate_w": rows(np.asarray(L0_ffn_gate_w).T),
        "shared_w": rows(np.asarray(L0_ffn_shared_gate_up).T),
        "shared_d": rows(down),
        "expert_w": np.concatenate([w1, w2, selectors()], 2),
        "const": constants(),
    }
    nc = bacc.Bacc("TRN2", target_bir_lowering=False, num_devices=1)
    arrays = {n: np.ascontiguousarray(a) for n, a in arrays.items()}
    args = [nc.dram_tensor(n, a.shape, F32, kind="ExternalInput").ap() for n, a in arrays.items()]
    out = nc.dram_tensor("out_t", (P, KE, TOKENS), F32, kind="ExternalOutput").ap()
    program(nc, *args, out)
    got = run_bass_kernel_spmd(nc, [arrays], core_ids=[0]).results[0]["out_t"]
    return got.transpose(2, 1, 0).reshape(BATCH, SEQ, EMB)
```

```python
from contextlib import ExitStack

import numpy as np

import concourse.bass as bass
from concourse import mybir

P = 128
F32 = mybir.dt.float32
F32R = mybir.dt.float32r
U32 = mybir.dt.uint32
ALU = mybir.AluOpType
ACT = mybir.ActivationFunctionType
AX_X = mybir.AxisListType.X

BATCH, SEQ, EMB = 4, 512, 256
HEADS, HEAD_DIM, STATE, TAPS, CHUNK = 64, 64, 128, 4, 32
INTER = HEADS * HEAD_DIM
EXPERTS, EXP_INNER, TOP_K = 64, 176, 6
SHARED_INNER = 2 * EXP_INNER
EPS = 1e-5

TOKENS = BATCH * SEQ
KE = EMB // P
TILES = SEQ // P
PAIRS = INTER // P
CPT = P // CHUNK
SEG = HEADS * CHUNK
SEG_UNIT = 2 * SEQ
UNITS_PER_TILE = SEG // SEG_UNIT
HPU = SEG_UNIT // CHUNK
IN_COLS = 2 * KE * P
NW_AT, D_AT, TAP_AT = 0, 1, 2
SCALARS = TAP_AT + TAPS + 1
W1_COLS = KE * EXP_INNER
IHALF = EXP_INNER // 2
ECOLS = W1_COLS + 2 * EMB
HALVES = 2
BPH = BATCH // HALVES
SH_CHUNKS = -(-SHARED_INNER // P)
UNITS = SH_CHUNKS * BPH
GTILES = TOKENS // P
ETILES = (TOKENS * TOP_K) // P + EXPERTS
EROWS = ETILES * P
DEEP = 4
ZERO_COLS = EROWS * EMB // (BATCH * PAIRS // 2 * P)
TINY = -1.0
WARM_UP = 24


def constants():
    k = np.arange(P)
    same = (k[:, None] // CHUNK) == (k[None, :] // CHUNK)
    ident = np.eye(P)
    later = same & (k[:, None] > k[None, :])
    upto = (k[:, None] % CHUNK) <= np.arange(CHUNK)
    return np.concatenate([ident, later, same, upto, (upto - 1.0) * 1e30, np.ones((P, P))], 1).astype(np.float32)


def routing_constants():
    k = np.arange(P)
    return np.concatenate([k[:, None] < k[None, :], (k[:, None] <= k[None, :])[:, :EXPERTS],
                           np.tile(np.arange(ETILES), (P, 1)), np.tile(np.arange(GTILES) * P, (P, 1))], 1).astype(np.float32)


def program(nc, x_t, in_w, out_w, scalars, bc_w, bc_conv, dt_w, dt_bias, a_log, c_t, mod_w, gate_w, shared_w,
            shared_d, expert_w, const, route_const, grouped, outputs, out_t):
    ctx = ExitStack()
    with ctx:
        def sem(name):
            return ctx.enter_context(nc.semaphore(name))

        START = {"wi_lo": 2, "wo_lo": 2, "gate": 2, "y_done": 2, "out_mm": 2, "y_sq": 2, "y_hi": 2, "attn_res": 1,
                 "taps": 1, "silu_g": 1, "xt_done": 1, "y_skip": 1, "ssq_done": 1, "ssm": 1,
                 "result": 1, "ssq_mm": 1, "seg_mm": 6, "seg_exp": 8, "seg_done": 2,
                 "weighted": 2, "hw_hi": 2, "expert_mm": 4,
                 "x_turned": 4, "x_lo": 2, "first_mm": 4, "second_mm": 4, "w_lo": 4, "hid_silu": 2, "hid_lo": 2,
                 "row_done": 2, "row_out0": 16, "row_out1": 16, "w2_lo": 4, "acc_chain": 7, "acc_turned": 2, "final": 3}

        def sb(name, shape, dt=F32, on=ctx):
            return on.enter_context(nc.sbuf_tensor(name, shape, dt))

        CONSTS = 4 * P + 2 * CHUNK
        consts = sb("consts", [P, CONSTS])
        ident, later, same = (consts[:, i * P:(i + 1) * P] for i in range(3))
        upto = consts[:, 3 * P:3 * P + CHUNK]
        ones = consts[:, 3 * P + 2 * CHUNK:]
        consts_r = sb("consts_r", [P, 3 * P + 2 * CHUNK], F32R)
        ident_r, later_r, same_r = (consts_r[:, i * P:(i + 1) * P] for i in range(3))
        mask_r = consts_r[:, 3 * P + CHUNK:3 * P + 2 * CHUNK]
        x_all = sb("x_all", [P, KE, TOKENS])
        h_hi = sb("h_hi", [P, KE, TOKENS], F32R)
        h_lo = sb("h_lo", [P, KE, TOKENS], F32R)
        mod = sb("mod", [P, 6 * KE, BATCH])
        gatew = sb("gatew", [P, KE, EXPERTS])
        gatew_hi = sb("gatew_hi", [P, KE, EXPERTS], F32R)
        gatew_lo = sb("gatew_lo", [P, KE, EXPERTS], F32R)
        shw = sb("shw", [P, KE, 2 * SHARED_INNER])
        shd = sb("shd", [P, SH_CHUNKS, EMB])
        start = sb("start", [P, len(START)])
        scal = sb("scal", [P, PAIRS, SCALARS])
        bcw = sb("bcw", [P, 2, KE, P])
        bcw_hi = sb("bcw_hi", [P, 2, KE, P], F32R)
        bcw_lo = sb("bcw_lo", [P, 2, KE, P], F32R)
        bcc = sb("bcc", [P, 2, TAPS + 1])
        dtw = sb("dtw", [P, KE, P])
        dtw_hi = sb("dtw_hi", [P, KE, P], F32R)
        dtw_lo = sb("dtw_lo", [P, KE, P], F32R)
        dtb = sb("dtb", [P, 1])
        alog = sb("alog", [P, HEADS])
        aexp = sb("aexp", [P, HEADS])
        aneg = sb("aneg", [P, HEADS])
        RC = P + EXPERTS + ETILES + GTILES
        rconst = sb("rconst", [P, RC])
        before, upto_e = rconst[:, 0:P], rconst[:, P:P + EXPERTS]
        tile_no = rconst[:, P + EXPERTS:P + EXPERTS + ETILES]
        steps_of_p = rconst[:, P + EXPERTS + ETILES:RC]
        zeros_out = sb("zeros_out", [P, ZERO_COLS])

        with ExitStack() as part:
            xc = sb("xc", [P, 2, KE, SEQ], on=part)
            xsq = sb("xsq", [P, 2, KE, SEQ], on=part)
            var = sb("var", [P, 2, TILES], on=part)
            std = sb("std", [P, 2, TILES], on=part)
            rstd = sb("rstd", [P, 2, TILES], on=part)
            rdiag = sb("rdiag", [P, 2, TILES, P], on=part)
            h = sb("h", [P, 2, KE, SEQ], on=part)
            cvec = sb("cvec", [P, KE, BATCH], on=part)
            cact = sb("cact", [P, KE, BATCH], on=part)
            gneg = sb("gneg", [P, 2, KE, BATCH], on=part)
            gsign = sb("gsign", [P, 2, KE, BATCH], on=part)
            gmag = sb("gmag", [P, 2, KE, BATCH], on=part)
            modw = sb("modw", [P, KE, 6 * EMB], on=part)
            lmax = sb("lmax", [P, GTILES], on=part)
            lsub = sb("lsub", [P, GTILES, EXPERTS], on=part)
            lexp = sb("lexp", [P, GTILES, EXPERTS], on=part)
            lsum = sb("lsum", [P, GTILES], on=part)
            lrec = sb("lrec", [P, GTILES], on=part)
            prob = sb("prob", [P, GTILES, EXPERTS], on=part)
            top8 = sb("top8", [P, GTILES, 8], on=part)
            rest = sb("rest", [P, GTILES, EXPERTS], on=part)
            kept = sb("kept", [P, GTILES, EXPERTS], on=part)
            ksum = sb("ksum", [P, GTILES], on=part)
            krec = sb("krec", [P, GTILES], on=part)

        with ExitStack() as part:
            hs = sb("hs", [P, 2, SEQ], on=part)
            hw = sb("hw", [P, 2, SEQ], on=part)
            hw_hi = sb("hw_hi", [P, 2, SEQ], F32R, on=part)
            hw_lo = sb("hw_lo", [P, 2, SEQ], F32R, on=part)
            x_rows = sb("x_rows", [P, DEEP, EMB], on=part)
            ew = sb("ew", [P, DEEP, ECOLS], on=part)
            ew_hi = sb("ew_hi", [P, DEEP, ECOLS], F32R, on=part)
            ew_lo = sb("ew_lo", [P, DEEP, ECOLS], F32R, on=part)
            xe_hi, xe_lo = (a[:, :, :].rearrange("p q (t n) -> p (q t) n", n=EMB) for a in (hw_hi, hw_lo))
            hid = sb("hid_rows", [P, 2, 2 * P], on=part)
            hid_hi = sb("hid_hi_rows", [P, 2, 2 * P], F32R, on=part)
            hid_lo = sb("hid_lo_rows", [P, 2, 2 * P], F32R, on=part)
            y_rows = sb("y_rows", [P, DEEP, EMB], on=part)
            shw_hi = sb("shw_hi", [P, KE, 2 * SHARED_INNER], F32R, on=part)
            shw_lo = sb("shw_lo", [P, KE, 2 * SHARED_INNER], F32R, on=part)
            shd_hi = sb("shd_hi", [P, SH_CHUNKS, EMB], F32R, on=part)
            shd_lo = sb("shd_lo", [P, SH_CHUNKS, EMB], F32R, on=part)
            before_r = sb("before_r", [P, P], F32R, on=part)
            taken_r = sb("taken_r", [P, GTILES, EXPERTS], F32R, on=part)
            shares = sb("shares", [P, GTILES, EXPERTS], on=part)
            ht = sb("ht", [P, GTILES, EMB], on=part)
            count = sb("count", [P, 1], on=part)
            over = sb("over", [P, GTILES], on=part)
            tiles_of = sb("tiles_of", [P, 1], on=part)
            tiles_row = sb("tiles_row", [P, P], on=part)
            offset = sb("offset", [P, EXPERTS], on=part)
            last_of = sb("last_of", [P, 1], on=part)
            passed = sb("passed", [P, ETILES], on=part)
            owner_no = sb("owner_no", [P, ETILES], U32, on=part)
            pos = sb("pos", [P, GTILES, EXPERTS], on=part)
            key = sb("key", [P, GTILES, EXPERTS], on=part)
            sum2, sum4, sum8, earlier = pos, key, pos, key
            key8 = sb("key8", [P, GTILES, 8], on=part)
            same_key = pos
            rows6 = sb("rows6", [P, GTILES, TOP_K], U32, on=part)
            share6 = sb("share6", [P, GTILES, TOP_K], on=part)
            no = sb("no", [P, 8], U32, on=part)
            row_at = sb("row_at", [P, 2, TOP_K], U32, on=part)
            passing = sb("passing", [P, 1], U32, on=part)

        with ExitStack() as part:
            z = sb("z", [P, SEQ], on=part)
            zabs = sb("zabs", [P, SEQ], on=part)
            zexp = sb("zexp", [P, SEQ], on=part)
            zln = sb("zln", [P, SEQ], on=part)
            dt_head = sb("dt_head", [P, SEQ], on=part)
            dt = sb("dt", [P, TILES, HEADS], on=part)
            at = sb("at", [P, TILES, HEADS], on=part)
            at_hi = sb("at_hi", [P, TILES, HEADS], F32R, on=part)
            at_lo = sb("at_lo", [P, TILES, HEADS], F32R, on=part)
            bcacc = sb("bcacc", [P, 2, SEQ], on=part)
            bcf = sb("bcf", [P, 2, SEQ], on=part)
            gmask = sb("gmask", [P, TILES, 2, P], on=part)
            mov_hi = sb("mov_hi", [P, 2, SEG_UNIT], F32R, on=part)
            mov_lo = sb("mov_lo", [P, 2, SEG_UNIT], F32R, on=part)
            e1 = sb("e1", [P, 2, SEG_UNIT], on=part)
            e2 = sb("e2", [P, 2, SEG_UNIT], on=part)
            el = sb("el", [P, PAIRS, TILES, 2, CHUNK], on=part)
            wi = sb("wi", [P, 2, IN_COLS], on=part)
            wi_hi = sb("wi_hi", [P, 2, IN_COLS], F32R, on=part)
            wi_lo = sb("wi_lo", [P, 2, IN_COLS], F32R, on=part)
            wo = sb("wo", [P, 2, EMB], on=part)
            wo_hi = sb("wo_hi", [P, 2, EMB], F32R, on=part)
            wo_lo = sb("wo_lo", [P, 2, EMB], F32R, on=part)
            xt = sb("xt", [P, TILES, 3 * HEAD_DIM], on=part)
            m = sb("m", [P, TILES, 2, P], on=part)
            yt = sb("yt", [P, SEQ], on=part)
            ysq = sb("ysq", [P, SEQ], on=part)
            ssq = sb("ssq", [P, SEQ], on=part)
            acc, xf, gs, y, y_hi, y_lo = (a[:, n, :].rearrange("p (q n) -> p q n", q=2) for a, n in
                                          ((e1, 0), (e1, 1), (e2, 0), (e2, 1), (mov_hi, 0), (mov_lo, 0)))
            attn, ms, rms, rinv, rinv_diag = bcacc, z[:, 0:TILES], zabs[:, 0:TILES], zln[:, 0:TILES], zexp[:, :]
            zero = sb("zero", [P, 1], on=part)

        got = ht[:, 0:2 * TOP_K, :].rearrange("p (r k) n -> p r k n", r=2)

        h_send = x_rows[:, 0:2, :]
        acc_rows = ht[:, 2 * TOP_K:2 * TOP_K + 2, :]

        bank = [ctx.enter_context(nc.psum_tensor(f"bank{i}", [P, SEQ], F32)) for i in range(8)]
        p_hid, p_gate, p_turn, p_y = bank[0:4]
        p_out = bank[4:6]
        p_mean, p_var, p_rstd = bank[0:2], bank[2:4], bank[6:8]
        p_inner, p_up, p_moe = bank[0:2], bank[2:4], bank[4:8]
        p_logit, p_turned = bank[4:6], bank[6:8]
        p_rank, p_count, p_offset, p_owner = bank[0:2], bank[2], bank[3], bank[4]
        p_x, p_first, p_row = bank[0:2], bank[2:4], bank[4:6]

        S = {}
        for name in """mod_in setup x_in ffn_in consts_cast setup_hi setup_lo setup_raw silu_c mod_mm mod_chain aneg_exp aneg_done
            mean centred squared variance var_eps std_done rstd_done rstd_wide rstd_mm xhat normed normed_hi normed_lo
            dt_mm z_done dt_exp dt_ln dt_plus dt_turned dt_done at_done at_split_hi at_split_lo
            bc_mm bc_tap0 bc_taps bc_silu g_mm g_done mov_hi mov_lo seg_mm seg_exp seg_done
            wi0 wi1 wo0 wo1 wi_hi wi_lo wo_hi wo_lo
            hid gate tap0 taps silu_x silu_g turned xt_done m_done ssm y_skip y_done y_sq y_hi y_lo
            out_mm ssq_done ssq_zero ssq_mm ssq_var ssq_std ssq_inv ssq_wide rinv_mm attn_scaled attn_res
            logit lsub_done lexp_done router_chain h_turned h_copied taken route_chain rank_mm count_mm tiles_done
            offset_mm passed owner_mm owners rows_done xs_zero zeros_set row_at sent0 sent1
            inner inner_silu prod weighted hw_hi hw_lo expert_mm result stored zero_set
            x_in0 x_in1 w2_lo x_turned x_hi x_lo w_in0 w_in1 w_in2 w_in3 w_hi w_lo
            first_mm hid_silu hid_hi hid_lo second_mm row_done row_out0 row_out1
            got0 got1 share_chain shares sum8 earlier acc_chain acc_turned final""".split():
            S[name] = sem(name)

        block = ctx.enter_context(nc.Block())

        def tile_pair(a, n, h):
            return a[bass.ds((DEEP * n + 2 * h) * P, 2 * P), :].rearrange("(t p) n -> p t n", p=P)

        def by_token(p):
            return p[:, 0:8 * TILES].rearrange("p (t n) -> p t n", n=8)[:, :, 0]

        def modcol(which, k, b):
            return mod[:, which * KE + k, bass.ds(b, 1)]

        grouped_rows = grouped.rearrange("(r n) -> r n", n=EMB)
        SETUP = 7 * 16

        @block.sync
        def _(sp):
            for dst, src in ((consts[:, :], const), (cvec[:, :, :], c_t), (modw[:, :, :], mod_w)):
                sp.dma_start(dst, src).then_inc(S["mod_in"], 16)
            for dst, src in ((dtw[:, :, :], dt_w), (bcw[:, :, :, :], bc_w), (gatew[:, :, :], gate_w),
                             (alog[:, :], a_log.partition_broadcast(P)), (scal[:, :, :], scalars), (bcc[:, :, :], bc_conv),
                             (dtb[:, :], dt_bias)):
                sp.dma_start(dst, src).then_inc(S["setup"], 16)
            for b in range(BATCH):
                x = slice(b * SEQ, (b + 1) * SEQ)
                sp.dma_start(x_all[:, :, x], x_t[:, :, x]).then_inc(S["x_in"], 16)
            for dst, src in ((rconst[:, :], route_const), (shw[:, :, :], shared_w), (shd[:, :, :], shared_d)):
                sp.dma_start(dst, src).then_inc(S["ffn_in"], 16)
            sp.wait_ge(S["zeros_set"], 1)
            def load_in(b, j, par):
                sp.wait_ge(S["wi_lo"], START["wi_lo"] + b * PAIRS + j - 1)
                sp.dma_start(wi[:, par, :], in_w[bass.ds(j, 1), :, :].rearrange("a p n -> p (a n)"))\
                    .then_inc(S[f"wi{par}"], 16)

            def load_out(b, j, par):
                sp.wait_ge(S["wo_lo"], START["wo_lo"] + b * PAIRS + j - 1)
                sp.dma_start(wo[:, par, :], out_w[bass.ds(j, 1), :, :].rearrange("a p n -> p (a n)"))\
                    .then_inc(S[f"wo{par}"], 16)

            def fill_zeros(b, jj):
                sp.dma_start(grouped.rearrange("(c p n) -> c p n", p=P, n=ZERO_COLS)
                             [bass.ds(b * (PAIRS // 2) + jj, 1), :, :].rearrange("a p n -> p (a n)"), zeros_out[:, :])\
                    .then_inc(S["xs_zero"], 16)

            with sp.Fori(0, BATCH) as b:
                for par in range(2):
                    load_in(b, par, par)
                with sp.Fori(0, PAIRS // 2 - 1) as jj:
                    for par in range(2):
                        load_in(b, 2 * jj + 2 + par, par)
                        load_out(b, 2 * jj + par, par)
                    fill_zeros(b, jj)
                for par in range(2):
                    load_out(b, PAIRS - 2 + par, par)
                fill_zeros(b, PAIRS // 2 - 1)
            def load(n, h):
                i_ = DEEP * n + 2 * h
                owners = [sp.value_load(owner_no[0:1, bass.ds(i_ + c, 1)], min_val=0, max_val=EXPERTS - 1) for c in range(2)]
                for c, e in enumerate(owners):
                    sp.wait_ge(S["w_lo"], START["w_lo"] + i_ + c - 3)
                    sp.wait_ge(S["w2_lo"], START["w2_lo"] + i_ + c - 3)
                    sp.dma_start(ew[:, 2 * h + c, :], expert_w[bass.ds(e, 1), :, :].rearrange("a p n -> p (a n)"))\
                        .then_inc(S[f"w_in{2 * h + c}"], 16)

            def store(n, h):
                sp.wait_ge(S["row_done"], START["row_done"] + DEEP * n + 2 * h + 2)
                sp.dma_start(tile_pair(outputs, n, h), y_rows[:, 2 * h:2 * h + 2, :]).then_inc(S[f"row_out{h}"], 16)

            sp.wait_ge(S["owners"], 1)
            for n in range(2):
                for h in range(2):
                    load(n, h)
            with sp.Fori(1, ETILES // DEEP - 1) as n:
                for h in range(2):
                    store(n - 1, h)
                    load(n + 1, h)
            for n in (ETILES // DEEP - 2, ETILES // DEEP - 1):
                for h in range(2):
                    store(n, h)
            for b in range(BATCH):
                sp.wait_ge(S["final"], START["final"] + (b + 1) * TILES * KE)
                sp.dma_start(out_t[:, :, b * SEQ:(b + 1) * SEQ], x_all[:, :, b * SEQ:(b + 1) * SEQ]).then_inc(S["stored"], 16)
            sp.wait_ge(S["stored"], 16 * BATCH)

        @block.tensor
        def _(pe):
            mm = nc.tensor.matmul

            def split_mm(out, w_hi, w_lo, x_hi, x_lo, first, last):
                mm(out, w_hi, x_hi, start=first, stop=False)
                mm(out, w_hi, x_lo, start=False, stop=False)
                return mm(out, w_lo, x_hi, start=False, stop=last)

            def norm(phase):
                def mean(b):
                    r = phase * BATCH + b
                    if r >= 2:
                        pe.wait_ge(S["centred"], (r - 1) * KE)
                    for k in range(KE):
                        i = mm(p_mean[r % 2][:, :], ones, x_all[:, k, b * SEQ:(b + 1) * SEQ], start=k == 0, stop=k == KE - 1)
                    i.then_inc(S["mean"], 1)

                mean(0)
                mean(1)
                for b in range(BATCH):
                    r = phase * BATCH + b
                    pe.wait_ge(S["squared"], r + 1)
                    if r >= 2:
                        pe.wait_ge(S["var_eps"], r - 1)
                    for t in range(TILES):
                        for k in range(KE):
                            i = mm(p_var[r % 2][:, 8 * t:8 * t + 8], xsq[:, r % 2, k, t * P:(t + 1) * P], ones[:, 0:8],
                                   start=k == 0, stop=k == KE - 1)
                    i.then_inc(S["variance"], 1)
                    if b + 2 < BATCH:
                        mean(b + 2)
                    pe.wait_ge(S["rstd_wide"], r + 1)
                    if r >= 2:
                        pe.wait_ge(S["xhat"], r - 1)
                    for t in range(TILES):
                        i = mm(p_rstd[r % 2][:, t * P:(t + 1) * P], ones, rdiag[:, r % 2, t, :], start=True, stop=True)
                    i.then_inc(S["rstd_mm"], 1)

            def slot(b, j, par, do_in=True, do_mid=True, do_out="mid"):
                g = b * PAIRS + j
                x = bass.ds(b * SEQ, SEQ)
                if do_in:
                    pe.wait_ge(S["wi_lo"], START["wi_lo"] + g + 1)
                    pe.wait_ge(S["taps"], START["taps"] + (TAPS - 1) * g)
                    for k in range(KE):
                        w = slice((KE + k) * P, (KE + k + 1) * P)
                        i = split_mm(p_hid[:, :], wi_hi[:, par, w], wi_lo[:, par, w], h_hi[:, k, x], h_lo[:, k, x],
                                     k == 0, k == KE - 1)
                    i.then_inc(S["hid"], 1)
                if do_mid:
                    q = 1 - par
                    pe.wait_ge(S["silu_x"], g)
                    pe.wait_ge(S["xt_done"], START["xt_done"] + g - 1)
                    for t in range(TILES):
                        i = nc.tensor.transpose(p_turn[:, t * P:(t + 1) * P], xf[:, q, t * P:(t + 1) * P], ident)
                    i.then_inc(S["turned"], 1)
                if do_in:
                    pe.wait_ge(S["silu_g"], START["silu_g"] + g)
                    for k in range(KE):
                        w = slice(k * P, (k + 1) * P)
                        i = split_mm(p_gate[:, :], wi_hi[:, par, w], wi_lo[:, par, w], h_hi[:, k, x], h_lo[:, k, x],
                                     k == 0, k == KE - 1)
                    i.then_inc(S["gate"], 1)
                if do_mid:
                    pe.wait_ge(S["xt_done"], START["xt_done"] + g)
                    pe.wait_ge(S["m_done"], g)
                    pe.wait_ge(S["y_skip"], START["y_skip"] + g - 1)
                    for t in range(TILES):
                        for hd in range(2):
                            i = mm(p_y[:, t * P:(t + 1) * P], xt[:, t, hd * HEAD_DIM:hd * HEAD_DIM + P], m[:, t, hd, :],
                                   start=hd == 0, stop=hd == 1)
                    i.then_inc(S["ssm"], 1)
                if do_out:
                    pe.wait_ge(S["y_lo"], g - 1)
                    pe.wait_ge(S["wo_lo"], START["wo_lo"] + g - 1)
                    for k in range(KE):
                        w = slice(k * P, (k + 1) * P)
                        i = split_mm(p_out[k][:, :], wo_hi[:, par, w], wo_lo[:, par, w], y_hi[:, par, :], y_lo[:, par, :],
                                     do_out == "first", do_out == "last")
                    i.then_inc(S["out_mm"], 1)

            pe.wait_ge(S["mod_in"], 3 * 16)
            pe.wait_ge(S["silu_c"], 1)
            for n in range(6 * KE):
                for k in range(KE):
                    i = mm(p_out[0][:, n * BATCH:(n + 1) * BATCH], modw[:, k, n * P:(n + 1) * P], cact[:, k, :],
                           start=k == 0, stop=k == KE - 1)
            i.then_inc(S["mod_mm"], 1)
            pe.wait_ge(S["x_in"], 16 * BATCH)
            norm(0)

            pe.wait_ge(S["setup_lo"], 3)
            pe.wait_ge(S["normed_lo"], BATCH * KE)
            with pe.Fori(0, BATCH) as b:
                x0 = b * SEQ
                pe.wait_ge(S["attn_res"], START["attn_res"] + b * KE)
                x = bass.ds(b * SEQ, SEQ)
                for p, hi, lo, done in ((p_turn, dtw_hi, dtw_lo, "dt_mm"), (p_hid, bcw_hi[:, 0], bcw_lo[:, 0], "bc_mm"),
                                        (p_gate, bcw_hi[:, 1], bcw_lo[:, 1], "bc_mm")):
                    for k in range(KE):
                        i = split_mm(p[:, :], hi[:, k, :], lo[:, k, :], h_hi[:, k, x], h_lo[:, k, x],
                                     k == 0, k == KE - 1)
                    i.then_inc(S[done], 1)
                pe.wait_ge(S["dt_plus"], b + 1)
                for t in range(TILES):
                    i = nc.tensor.transpose(p_y[:, t * P:(t + 1) * P], dt_head[:, t * P:(t + 1) * P], ident)
                i.then_inc(S["dt_turned"], 1)
                with pe.Fori(0, TILES) as t:
                    for n in range(UNITS_PER_TILE):
                        r = (b * TILES + t) * UNITS_PER_TILE + n
                        if n == 1:
                            pe.wait_ge(S["bc_taps"], 2 * (TAPS - 1) * (b + 1))
                        pe.wait_ge(S["mov_lo"], r + 1)
                        for c in range(2):
                            pe.wait_ge(S["seg_exp"], START["seg_exp"] + 4 * r + 2 * c - 6)
                            col = slice(c * SEQ, (c + 1) * SEQ)
                            hi, lo = mov_hi[:, n, col], mov_lo[:, n, col]
                            heads = bass.ds(t * HEADS + n * HPU + c * (HPU // 2), HPU // 2)
                            mm(bank[4 * (1 - n) + c][:, :], later_r, hi, start=True, stop=False)
                            mm(bank[4 * (1 - n) + c][:, :], later_r, lo, start=False, stop=False)
                            mm(bank[4 * (1 - n) + c][:, :], ident_r, mask_r[:, None, :].broadcast_to([P, HPU // 2, CHUNK]),
                               start=False, stop=True).then_inc(S["seg_mm"], 1)
                            mm(bank[4 * (1 - n) + 2 + c][:, :], same_r, hi, start=True, stop=False)
                            mm(bank[4 * (1 - n) + 2 + c][:, :], same_r, lo, start=False, stop=False)
                            for part_ in (at_hi, at_lo):
                                a = part_[:, :, :].rearrange("p t h -> p (t h)")[:, heads]
                                i = mm(bank[4 * (1 - n) + 2 + c][:, :], later_r, a[:, :, None].broadcast_to([P, HPU // 2, CHUNK]),
                                       start=False, stop=part_ is at_lo)
                            i.then_inc(S["seg_mm"], 1)
                pe.wait_ge(S["seg_exp"], START["seg_exp"] + 4 * (b + 1) * TILES * UNITS_PER_TILE)
                slot(b, 0, 0, do_mid=False, do_out="")
                pe.wait_ge(S["bc_silu"], 2 * b + 2)
                for t in range(TILES):
                    i = mm(p_out[0][:, t * P:(t + 1) * P], bcf[:, 0, t * P:(t + 1) * P], bcf[:, 1, t * P:(t + 1) * P],
                           start=True, stop=True)
                i.then_inc(S["g_mm"], 1)
                slot(b, 1, 1, do_out="")
                pe.wait_ge(S["g_done"], 2 * (b + 1))
                slot(b, 2, 0, do_out="first")
                slot(b, 3, 1)
                with pe.Fori(2, PAIRS // 2) as jj:
                    slot(b, 2 * jj, 0)
                    slot(b, 2 * jj + 1, 1)
                slot(b, PAIRS, 0, do_in=False)
                slot(b, PAIRS + 1, 1, do_in=False, do_mid=False, do_out="last")

                pe.wait_ge(S["ssq_done"], START["ssq_done"] + (b + 1) * PAIRS)
                for t in range(TILES):
                    i = mm(p_hid[:, 8 * t:8 * t + 8], ssq[:, t * P:(t + 1) * P], ones[:, 0:8], start=True, stop=True)
                i.then_inc(S["ssq_mm"], 1)
                pe.wait_ge(S["ssq_wide"], b + 1)
                for t in range(TILES):
                    i = mm(p_gate[:, t * P:(t + 1) * P], ones, rinv_diag[:, t * P:(t + 1) * P], start=True, stop=True)
                i.then_inc(S["rinv_mm"], 1)

            pe.wait_ge(S["attn_res"], START["attn_res"] + BATCH * KE)
            norm(1)
            for b in range(BATCH):
                pe.wait_ge(S["normed_lo"], (BATCH + b + 1) * KE)
                for t in range(TILES):
                    g = b * TILES + t
                    x = slice(g * P, (g + 1) * P)
                    for k in range(KE):
                        i = split_mm(p_logit[g // 8][:, (g % 8) * EXPERTS:(g % 8 + 1) * EXPERTS], h_hi[:, k, x], h_lo[:, k, x],
                                     gatew_hi[:, k, :], gatew_lo[:, k, :], k == 0, k == KE - 1)
            i.then_inc(S["logit"], 1)
            for b in range(BATCH):
                if b >= 1:
                    pe.wait_ge(S["h_copied"], b)
                for t in range(TILES):
                    x = slice(b * SEQ + t * P, b * SEQ + (t + 1) * P)
                    for k in range(KE):
                        o = p_turned[t // 2][:, (t % 2) * EMB + k * P:(t % 2) * EMB + (k + 1) * P]
                        mm(o, h_hi[:, k, x], ident_r, start=True, stop=False)
                        i = mm(o, h_lo[:, k, x], ident_r, start=False, stop=True)
                i.then_inc(S["h_turned"], 1)

            pe.wait_ge(S["taken"], 1)
            pe.wait_ge(S["sum8"], 2)
            for g in (7, 15):
                i = mm(p_count[0:EXPERTS, 0:8], sum8[:, g, :], ones[:, 0:8], start=g == 7, stop=g == 15)
            i.then_inc(S["count_mm"], 1)
            pe.wait_ge(S["earlier"], 3)
            for n in range(2):
                o = p_rank[n][:, :].rearrange("p (t e) -> p t e", t=8)
                mm(o, before_r[:, :], taken_r[:, 8 * n:8 * n + 8, :], start=True, stop=False)
                i = mm(o, ones[:, :], earlier[:, 8 * n:8 * n + 8, :], start=False, stop=True)
            i.then_inc(S["rank_mm"], 1)
            pe.wait_ge(S["tiles_done"], 1)
            mm(p_offset[:, 0:EXPERTS], tiles_row[0:EXPERTS, :], before[0:EXPERTS, 0:EXPERTS], start=True, stop=True)
            mm(p_offset[0:EXPERTS, EXPERTS:EXPERTS + 8], upto_e[0:EXPERTS, :], tiles_row[0:EXPERTS, 0:8],
               start=True, stop=True).then_inc(S["offset_mm"], 1)
            pe.wait_ge(S["passed"], 1)
            mm(p_owner[:, 0:ETILES], ones[0:EXPERTS, :], passed[0:EXPERTS, :], start=True, stop=True)\
                .then_inc(S["owner_mm"], 1)

            pe.wait_ge(S["setup_lo"], 5)
            pe.wait_ge(S["h_copied"], BATCH)
            pe.wait_ge(S["owners"], 1)

            def down(u, w_hi, w_lo, rows, q, first=False, last=False):
                hi, lo = hw_hi[0:rows, q, :], hw_lo[0:rows, q, :]
                pe.wait_ge(S["hw_hi"], START["hw_hi"] + u + 1)
                for k in range(KE):
                    w = slice(k * P, (k + 1) * P)
                    mm(p_moe[q * KE + k][:, :], w_hi[0:rows, w], hi, start=first, stop=False)
                    mm(p_moe[q * KE + k][:, :], w_lo[0:rows, w], hi, start=False, stop=False)
                pe.wait_ge(S["weighted"], START["weighted"] + u + 1)
                for k in range(KE):
                    i = mm(p_moe[q * KE + k][:, :], w_hi[0:rows, k * P:(k + 1) * P], lo, start=False, stop=last)
                i.then_inc(S["expert_mm"], 1)

            with pe.Fori(0, HALVES) as hf:
                base = hf * UNITS
                pe.wait_ge(S["result"], START["result"] + hf * BPH * KE)

                def shared_rows(n):
                    return min(P, SHARED_INNER - n * P)

                def inner_shared(u):
                    n, q = divmod(u, BPH)
                    rows = shared_rows(n)
                    pe.wait_ge(S["weighted"], START["weighted"] + base + u - 1)
                    x = bass.ds((hf * BPH + q) * SEQ, SEQ)
                    for p, at_ in ((p_inner[q], 0), (p_up[q], SHARED_INNER)):
                        for k in range(KE):
                            w = slice(at_ + n * P, at_ + n * P + rows)
                            i = split_mm(p[0:rows, :], shw_hi[:, k, w], shw_lo[:, k, w], h_hi[:, k, x], h_lo[:, k, x],
                                         k == 0, k == KE - 1)
                    i.then_inc(S["inner"], 1)

                def down_shared(u):
                    n, q = divmod(u, BPH)
                    down(base + u, shd_hi[:, n, :], shd_lo[:, n, :], shared_rows(n), q, first=n == 0, last=n == SH_CHUNKS - 1)

                SU = SH_CHUNKS * BPH
                for u in range(SU):
                    inner_shared(u)
                    if u:
                        down_shared(u - 1)
                down_shared(SU - 1)

            def turn(n, r):
                i_ = DEEP * n + r
                pe.wait_ge(S[f"x_in{r // 2}"], 16 * n + 16)
                pe.wait_ge(S["x_lo"], START["x_lo"] + i_ - 1)
                for k in range(KE):
                    i = nc.tensor.transpose(p_x[r % 2][:, k * P:(k + 1) * P], x_rows[:, r, k * P:(k + 1) * P], ident)
                i.then_inc(S["x_turned"], 1)

            def first(n, r):
                i_ = DEEP * n + r
                pe.wait_ge(S["w_lo"], START["w_lo"] + i_ + 1)
                pe.wait_ge(S["hid_silu"], START["hid_silu"] + i_ - 1)
                pe.wait_ge(S["x_lo"], START["x_lo"] + i_ + 1)
                for a in range(2):
                    for k in range(KE):
                        w = slice(k * EXP_INNER + a * IHALF, k * EXP_INNER + (a + 1) * IHALF)
                        x = slice(k * P, (k + 1) * P)
                        i = split_mm(p_first[r % 2][0:IHALF, a * P:(a + 1) * P], ew_hi[:, r, w], ew_lo[:, r, w],
                                     xe_hi[:, r, x], xe_lo[:, r, x], k == 0, k == KE - 1)
                i.then_inc(S["first_mm"], 1)

            def second(n, r):
                i_ = DEEP * n + r
                pe.wait_ge(S["row_done"], START["row_done"] + i_ - 1)
                pe.wait_ge(S["w2_lo"], START["w2_lo"] + i_ + 1)
                pe.wait_ge(S["hid_lo"], START["hid_lo"] + i_ + 1)
                for a in range(2):
                    w = slice(W1_COLS + a * EMB, W1_COLS + (a + 1) * EMB)
                    x = slice(a * P, (a + 1) * P)
                    i = split_mm(p_row[r % 2][:, 0:EMB], hid_hi[0:IHALF, r % 2, x], hid_lo[0:IHALF, r % 2, x],
                                 ew_hi[0:IHALF, r, w], ew_lo[0:IHALF, r, w], a == 0, a == 1)
                i.then_inc(S["second_mm"], 1)

            def step(n, r, before_it=True, ahead=True):
                if ahead:
                    turn(n + (r + 2) // DEEP, (r + 2) % DEEP)
                first(n, r)
                if before_it:
                    second(n - 1 if r == 0 else n, (r - 1) % DEEP)

            pe.wait_ge(S["result"], START["result"] + BATCH * KE)
            pe.wait_ge(S["weighted"], START["weighted"] + HALVES * UNITS)
            pe.wait_ge(S["x_in0"], 16)
            for _ in range(WARM_UP):
                mm(bank[6][:, :], ident_r, h_hi[:, 0, 0:SEQ], start=True, stop=True)
            turn(0, 0)
            turn(0, 1)
            for r in range(DEEP):
                step(0, r, before_it=r > 0)
            with pe.Fori(1, ETILES // DEEP - 1) as n:
                for r in range(DEEP):
                    step(n, r)
            for r in range(DEEP):
                step(ETILES // DEEP - 1, r, ahead=r < DEEP - 2)
            second(ETILES // DEEP - 1, DEEP - 1)

            with pe.Fori(0, BATCH) as b:
                for t in range(TILES):
                    g = b * TILES + t
                    pe.wait_ge(S["final"], START["final"] + KE * (g - 1))
                    pe.wait_ge(S["acc_chain"], START["acc_chain"] + TOP_K * (g + 1))
                    for k in range(KE):
                        i = nc.tensor.transpose(p_x[t % 2][:, k * P:(k + 1) * P], acc_rows[:, t % 2, k * P:(k + 1) * P], ident)
                    i.then_inc(S["acc_turned"], 1)

        @block.scalar
        def _(act):
            f = nc.scalar.activation

            def high(dst, src):
                return f(dst, src, ACT.Identity)

            act.wait_ge(S["mod_in"], 3 * 16)
            f(cact[:, :, :], cvec[:, :, :], ACT.Silu).then_inc(S["silu_c"], 1)
            f(consts_r[:, :], consts[:, 0:3 * P + 2 * CHUNK], ACT.Identity).then_inc(S["consts_cast"], 1)
            act.wait_ge(S["setup"], SETUP)
            for dst, src in ((dtw_hi, dtw), (bcw_hi, bcw), (gatew_hi, gatew)):
                high(dst[:], src[:]).then_inc(S["setup_hi"], 1)
            f(aexp[:, :], alog[:, :], ACT.Exp).then_inc(S["aneg_exp"], 1)

            def norm(phase):
                def square(b):
                    r = phase * BATCH + b
                    act.wait_ge(S["centred"], (r + 1) * KE)
                    if r >= 2:
                        act.wait_ge(S["variance"], r - 1)
                    f(xsq[:, r % 2], xc[:, r % 2], ACT.Square).then_inc(S["squared"], 1)

                square(0)
                for b in range(BATCH):
                    r = phase * BATCH + b
                    act.wait_ge(S["var_eps"], r + 1)
                    if r >= 2:
                        act.wait_ge(S["rstd_done"], r - 1)
                    f(std[:, r % 2, :], var[:, r % 2, :], ACT.Sqrt).then_inc(S["std_done"], 1)
                    if b + 1 < BATCH:
                        square(b + 1)
                    act.wait_ge(S["xhat"], r + 1)
                    if r >= 2:
                        act.wait_ge(S["normed_lo"], (r - 1) * KE)
                    for k in range(KE):
                        f(h[:, r % 2, k, :], xc[:, r % 2, k, :], ACT.Identity, bias=mod[:, 3 * phase * KE + k, b:b + 1],
                          scale=mod[:, (3 * phase + 1) * KE + k, b:b + 1]).then_inc(S["normed"], 1)
                        act.wait_ge(S["normed"], r * KE + k + 1)
                        high(h_hi[:, k, b * SEQ:(b + 1) * SEQ], h[:, r % 2, k, :]).then_inc(S["normed_hi"], 1)

            def take_in(b, j, par):
                g = b * PAIRS + j
                act.wait_ge(S[f"wi{par}"], 8 * (g - par) + 16)
                act.wait_ge(S["gate"], START["gate"] + g - 1)
                high(wi_hi[:, par, :], wi[:, par, :]).then_inc(S["wi_hi"], 1)

            def slot(b, j, par, do_in=True, next_in=True, take_out=True, finish=True):
                g = b * PAIRS + j
                if finish:
                    act.wait_ge(S["y_done"], START["y_done"] + g - 1)
                    act.wait_ge(S["out_mm"], START["out_mm"] + g - 3)
                    f(y_hi[:, par, :], y[:, par, :], ACT.Identity, scale=scal[:, bass.ds(j - 2, 1), NW_AT:NW_AT + 1]
                      .rearrange("p a n -> p (a n)")).then_inc(S["y_hi"], 1)
                if do_in:
                    def col(at_):
                        return scal[:, bass.ds(j, 1), at_:at_ + 1].rearrange("p a n -> p (a n)")

                    act.wait_ge(S["hid"], g + 1)
                    f(acc[:, par, :], p_hid[:, :], ACT.Identity, bias=col(TAP_AT + TAPS),
                      scale=col(TAP_AT + TAPS - 1)).then_inc(S["tap0"], 1)
                if finish:
                    act.wait_ge(S["ssq_done"], START["ssq_done"] + g - 2)
                    f(ysq[:, :], y[:, par, :], ACT.Square).then_inc(S["y_sq"], 1)
                if next_in:
                    take_in(b, j + 1, 1 - par)
                if do_in:
                    act.wait_ge(S["gate"], START["gate"] + g + 1)
                    f(gs[:, par, :], p_gate[:, :], ACT.Silu).then_inc(S["silu_g"], 1)
                    act.wait_ge(S["taps"], START["taps"] + (TAPS - 1) * (g + 1))
                    f(xf[:, par, :], acc[:, par, :], ACT.Silu).then_inc(S["silu_x"], 1)
                if take_out:
                    q = 1 - par
                    act.wait_ge(S[f"wo{q}"], 8 * (g - 1 - q) + 16)
                    act.wait_ge(S["out_mm"], START["out_mm"] + g - 2)
                    high(wo_hi[:, q, :], wo[:, q, :]).then_inc(S["wo_hi"], 1)

            act.wait_ge(S["mod_chain"], 10)
            norm(0)
            with act.Fori(0, BATCH) as b:
                act.wait_ge(S["z_done"], 2 * b + 2)
                f(zexp[:, :], zabs[:, :], ACT.Exp, scale=-1.0).then_inc(S["dt_exp"], 1)
                act.wait_ge(S["dt_exp"], b + 1)
                f(zln[:, :], zexp[:, :], ACT.Ln, bias=1.0).then_inc(S["dt_ln"], 1)
                for n, p in enumerate((p_hid, p_gate)):
                    act.wait_ge(S["bc_mm"], 2 * b + n + 1)
                    f(bcacc[:, n, :], p[:, :], ACT.Identity, bias=bcc[:, n, TAPS:TAPS + 1],
                      scale=bcc[:, n, TAPS - 1:TAPS]).then_inc(S["bc_tap0"], 1)
                act.wait_ge(S["at_done"], b + 1)
                high(at_hi[:, :, :], at[:, :, :]).then_inc(S["at_split_hi"], 1)
                with act.Fori(0, TILES) as t:
                    for n in range(UNITS_PER_TILE):
                        r = (b * TILES + t) * UNITS_PER_TILE + n
                        act.wait_ge(S["seg_done"], START["seg_done"] + r - 1)
                        for c in range(2):
                            act.wait_ge(S["seg_mm"], START["seg_mm"] + 4 * r + 2 * c + 2)
                            f(e1[:, n, c * SEQ:(c + 1) * SEQ], bank[4 * (1 - n) + c][:, :], ACT.Exp).then_inc(S["seg_exp"], 1)
                            f(e2[:, n, c * SEQ:(c + 1) * SEQ], bank[4 * (1 - n) + 2 + c][:, :], ACT.Exp).then_inc(S["seg_exp"], 1)

                take_in(b, 0, 0)
                act.wait_ge(S["bc_taps"], 2 * (TAPS - 1) * (b + 1))
                for n in range(2):
                    f(bcf[:, n, :], bcacc[:, n, :], ACT.Silu).then_inc(S["bc_silu"], 1)
                act.wait_ge(S["seg_done"], START["seg_done"] + (b + 1) * TILES * UNITS_PER_TILE)
                slot(b, 0, 0, take_out=False, finish=False)
                slot(b, 1, 1, finish=False)
                with act.Fori(1, PAIRS // 2 - 1) as jj:
                    slot(b, 2 * jj, 0)
                    slot(b, 2 * jj + 1, 1)
                slot(b, PAIRS - 2, 0)
                slot(b, PAIRS - 1, 1, next_in=False)
                slot(b, PAIRS, 0, do_in=False, next_in=False)
                slot(b, PAIRS + 1, 1, do_in=False, next_in=False, take_out=False)

                act.wait_ge(S["ssq_var"], b + 1)
                f(rms, ms, ACT.Sqrt).then_inc(S["ssq_std"], 1)

            act.wait_ge(S["attn_res"], START["attn_res"] + BATCH * KE)
            norm(1)
            act.wait_ge(S["ffn_in"], 3 * 16)
            act.wait_ge(S["setup_raw"], 3)
            f(before_r[:, :], before, ACT.Identity).then_inc(S["setup_hi"], 1)
            for dst, src in ((shw_hi, shw), (shd_hi, shd)):
                high(dst[:], src[:]).then_inc(S["setup_hi"], 1)
            act.wait_ge(S["lsub_done"], 2)
            f(lexp[:, :, :], lsub[:, :, :], ACT.Exp).then_inc(S["lexp_done"], 1)
            for b in range(BATCH):
                act.wait_ge(S["h_turned"], b + 1)
                for n in range(2):
                    i = f(ht[:, b * TILES + 2 * n:b * TILES + 2 * n + 2, :], p_turned[n][:, :].rearrange("p (t n) -> p t n", t=2),
                          ACT.Identity)
                i.then_inc(S["h_copied"], 1)

            def unit(u, q, rows=P):
                act.wait_ge(S["inner"], u + 1)
                act.wait_ge(S["weighted"], START["weighted"] + u - 1)
                f(hs[0:rows, q, :], p_inner[q][0:rows, :], ACT.Silu).then_inc(S["inner_silu"], 1)
                act.wait_ge(S["prod"], u + 1)
                act.wait_ge(S["expert_mm"], START["expert_mm"] + u - 1)
                high(hw_hi[0:rows, q, :], hw[0:rows, q, :]).then_inc(S["hw_hi"], 1)

            with act.Fori(0, HALVES) as hf:
                for u in range(UNITS):
                    unit(hf * UNITS + u, u % BPH, min(P, SHARED_INNER - u // BPH * P))

            def weights(n, r):
                i_ = DEEP * n + r
                act.wait_ge(S[f"w_in{r}"], 16 * n + 16)
                act.wait_ge(S["second_mm"], START["second_mm"] + i_ - 3)
                high(ew_hi[:, r, :], ew[:, r, :]).then_inc(S["w_hi"], 1)

            def rows_in(n, r):
                i_ = DEEP * n + r
                act.wait_ge(S["x_turned"], START["x_turned"] + i_ + 1)
                act.wait_ge(S["first_mm"], START["first_mm"] + i_ - 3)
                high(xe_hi[:, r, :], p_x[r % 2][:, 0:EMB]).then_inc(S["x_hi"], 1)

            def step(n, r, ahead1=True, ahead=True):
                i_ = DEEP * n + r
                if ahead1:
                    weights(n + (r + 1) // DEEP, (r + 1) % DEEP)
                if ahead:
                    rows_in(n + (r + 2) // DEEP, (r + 2) % DEEP)
                act.wait_ge(S["hid_lo"], START["hid_lo"] + i_ - 1)
                act.wait_ge(S["first_mm"], START["first_mm"] + i_ + 1)
                f(hid[0:IHALF, r % 2, :], p_first[r % 2][0:IHALF, 0:2 * P], ACT.Silu).then_inc(S["hid_silu"], 1)
                act.wait_ge(S["second_mm"], START["second_mm"] + i_ - 1)
                act.wait_ge(S["hid_silu"], START["hid_silu"] + i_ + 1)
                high(hid_hi[0:IHALF, r % 2, :], hid[0:IHALF, r % 2, :]).then_inc(S["hid_hi"], 1)

            weights(0, 0)
            rows_in(0, 0)
            rows_in(0, 1)
            with act.Fori(0, ETILES // DEEP - 1) as n:
                for r in range(DEEP):
                    step(n, r)
            for r in range(DEEP):
                step(ETILES // DEEP - 1, r, ahead1=r < DEEP - 1, ahead=r < DEEP - 2)

        @block.vector
        def _(dve):
            v = nc.vector

            def low(dst, src, hi):
                return v.tensor_tensor(dst, src, hi.bitcast(F32), ALU.subtract)

            for n, (name, credit) in enumerate(START.items()):
                v.memset(start[:, n:n + 1], 0.0).then_inc(S[name], credit)
            v.memset(zeros_out[:, :], 0.0).then_inc(S["zeros_set"], 1)

            dve.wait_ge(S["setup"], SETUP)
            dve.wait_ge(S["setup_hi"], 3)
            for dst, src, hi in ((dtw_lo, dtw, dtw_hi), (bcw_lo, bcw, bcw_hi), (gatew_lo, gatew, gatew_hi)):
                low(dst[:], src[:], hi[:]).then_inc(S["setup_lo"], 1)

            dve.wait_ge(S["mod_mm"], 1)
            v.tensor_copy(mod[:, :, :], p_out[0][:, 0:6 * KE * BATCH].rearrange("p (n b) -> p n b", b=BATCH))\
                .then_inc(S["mod_chain"], 1)
            dve.wait_ge(S["mod_chain"], 1)
            dve.wait_ge(S["aneg_exp"], 1)
            v.tensor_scalar(aneg[:, :], aexp[:, :], -1.0, None, ALU.mult).then_inc(S["aneg_done"], 1)
            for n in (1, 4):
                c = mod[:, n * KE:(n + 1) * KE, :]
                v.tensor_scalar(c, c, 1.0, None, ALU.add)
            for n, w in enumerate((2, 5)):
                g = mod[:, w * KE:(w + 1) * KE, :]
                v.tensor_scalar(gneg[:, n], g, -1.0, None, ALU.mult)
                v.tensor_scalar(gsign[:, n], g, 0.0, 2.0, ALU.is_ge, ALU.mult).then_inc(S["mod_chain"], 1)
            dve.wait_ge(S["mod_chain"], 3)
            for n, w in enumerate((2, 5)):
                g = mod[:, w * KE:(w + 1) * KE, :]
                v.tensor_tensor(gmag[:, n], g, gneg[:, n], ALU.max).then_inc(S["mod_chain"], 1)
            dve.wait_ge(S["mod_chain"], 5)
            v.tensor_scalar(gmag[:, :], gmag[:, :], 0.25, None, ALU.max).then_inc(S["mod_chain"], 1)
            v.tensor_scalar(gsign[:, :], gsign[:, :], -1.0, None, ALU.add).then_inc(S["mod_chain"], 1)
            dve.wait_ge(S["mod_chain"], 7)
            for n, w in enumerate((2, 5)):
                v.tensor_tensor(mod[:, w * KE:(w + 1) * KE, :], gmag[:, n], gsign[:, n], ALU.mult)\
                    .then_inc(S["mod_chain"], 1)
            dve.wait_ge(S["mod_chain"], 9)
            v.memset(start[:, 0:1], 0.0).then_inc(S["mod_chain"], 1)

            def norm(phase):
                def centre(b):
                    r = phase * BATCH + b
                    dve.wait_ge(S["mean"], r + 1)
                    if r >= 2:
                        dve.wait_ge(S["normed"], (r - 1) * KE)
                        dve.wait_ge(S["squared"], r - 1)
                    for k in range(KE):
                        v.scalar_tensor_tensor(xc[:, r % 2, k, :], p_mean[r % 2][:, :], -1.0 / EMB,
                                               x_all[:, k, b * SEQ:(b + 1) * SEQ], ALU.mult, ALU.add)\
                            .then_inc(S["centred"], 1)

                centre(0)
                for b in range(BATCH):
                    r = phase * BATCH + b
                    dve.wait_ge(S["variance"], r + 1)
                    if r >= 2:
                        dve.wait_ge(S["std_done"], r - 1)
                    v.tensor_scalar(var[:, r % 2, :], by_token(p_var[r % 2]), 1.0 / EMB, EPS, ALU.mult, ALU.add)\
                        .then_inc(S["var_eps"], 1)
                    if b >= 1:
                        split(b - 1, phase)
                    dve.wait_ge(S["std_done"], r + 1)
                    v.reciprocal(rstd[:, r % 2, :], std[:, r % 2, :]).then_inc(S["rstd_done"], 1)
                    dve.wait_ge(S["rstd_done"], r + 1)
                    if r >= 2:
                        dve.wait_ge(S["rstd_mm"], r - 1)
                    v.tensor_tensor(rdiag[:, r % 2], ident[:, None, :].broadcast_to([P, TILES, P]),
                                    rstd[:, r % 2, :, None].broadcast_to([P, TILES, P]), ALU.mult).then_inc(S["rstd_wide"], 1)
                    if b + 1 < BATCH:
                        centre(b + 1)
                    dve.wait_ge(S["rstd_mm"], r + 1)
                    dve.wait_ge(S["squared"], r + 1)
                    v.tensor_tensor(xc[:, r % 2], xc[:, r % 2], p_rstd[r % 2][:, None, :].broadcast_to([P, KE, SEQ]),
                                    ALU.mult).then_inc(S["xhat"], 1)
                split(BATCH - 1, phase)

            def split(b, phase):
                r = phase * BATCH + b
                dve.wait_ge(S["normed_hi"], (r + 1) * KE)
                for k in range(KE):
                    x = slice(b * SEQ, (b + 1) * SEQ)
                    low(h_lo[:, k, x], h[:, r % 2, k, :], h_hi[:, k, x]).then_inc(S["normed_lo"], 1)

            def tap(d, dst, src, taps, done, base):
                if d > 1:
                    dve.wait_ge(S[done], START.get(done, 0) + base + d - 1)
                v.scalar_tensor_tensor(dst[:, d:], src[:, 0:SEQ - d], taps(TAPS - 1 - d), dst[:, d:],
                                       ALU.mult, ALU.add).then_inc(S[done], 1)

            def conv(dst, src, taps, done, base):
                for d in range(1, TAPS):
                    tap(d, dst, src, taps, done, base)

            def moving(b, t, n):
                r = (b * TILES + t) * UNITS_PER_TILE + n
                dve.wait_ge(S["seg_mm"], START["seg_mm"] + 4 * (r - 1))
                a = at[:, :, :].rearrange("p t h -> p (t h)")[:, bass.ds(t * HEADS + n * HPU, HPU)]
                v.tensor_tensor(mov_hi[:, n, :].rearrange("p (h l) -> p h l", l=CHUNK),
                                a[:, :, None].broadcast_to([P, HPU, CHUNK]),
                                upto[:, None, :].broadcast_to([P, HPU, CHUNK]), ALU.mult).then_inc(S["mov_hi"], 1)

            def segments(b, t, n):
                r = (b * TILES + t) * UNITS_PER_TILE + n
                dve.wait_ge(S["seg_exp"], START["seg_exp"] + 4 * (r + 1))
                J = PAIRS // UNITS_PER_TILE
                out = el[:, n * J:(n + 1) * J, bass.ds(t, 1), :, :].rearrange("p j a h l -> p j (a h l)")
                v.tensor_tensor(out, e1[:, n, :].rearrange("p (j n) -> p j n", j=J),
                                e2[:, n, :].rearrange("p (j n) -> p j n", j=J), ALU.add).then_inc(S["seg_done"], 1)

            def slot(b, j, par, do_in=True, do_mid=True, finish=True):
                g = b * PAIRS + j
                q = 1 - par

                def col(pair, at_):
                    return scal[:, bass.ds(pair, 1), at_:at_ + 1].rearrange("p a n -> p (a n)")

                if do_mid:
                    dve.wait_ge(S["ssm"], START["ssm"] + g - 1)
                    e = el[:, bass.ds(j - 1, 1), :, :, :].rearrange("p a t h l -> p (a t h) l")
                    v.tensor_tensor(m[:, :, :, :].rearrange("p t h (r l) -> p (t h) r l", l=CHUNK),
                                    e[:, :, None, :].broadcast_to([P, TILES * 2, CPT, CHUNK]),
                                    gmask[:, :, :, :].rearrange("p t h (r l) -> p (t h) r l", l=CHUNK), ALU.mult)\
                        .then_inc(S["m_done"], 1)
                    dve.wait_ge(S["turned"], g)
                    d = dt[:, :, bass.ds(2 * (j - 1), 2)]
                    v.tensor_tensor(xt[:, :, :].rearrange("p t (a n) -> p t a n", a=3)[:, :, 0:3:2, :],
                                    p_turn[:, :].rearrange("p (t a n) -> p t a n", t=TILES, a=2),
                                    d[:, :, :, None].broadcast_to([P, TILES, 2, HEAD_DIM]), ALU.mult)\
                        .then_inc(S["xt_done"], 1)
                if do_in:
                    dve.wait_ge(S["tap0"], g + 1)
                    tap(1, acc[:, par, :], p_hid, lambda n: col(j, TAP_AT + n), "taps", (TAPS - 1) * g)
                if finish:
                    dve.wait_ge(S["y_hi"], START["y_hi"] + g - 1)
                    dve.wait_ge(S["out_mm"], START["out_mm"] + g - 3)
                    v.scalar_tensor_tensor(y_lo[:, par, :], y[:, par, :], col(j - 2, NW_AT), y_hi[:, par, :].bitcast(F32),
                                           ALU.mult, ALU.subtract).then_inc(S["y_lo"], 1)
                if do_in:
                    for d in range(2, TAPS):
                        tap(d, acc[:, par, :], p_hid, lambda n: col(j, TAP_AT + n), "taps", (TAPS - 1) * g)
                if do_mid:
                    dve.wait_ge(S["ssm"], START["ssm"] + g)
                    v.scalar_tensor_tensor(yt[:, :], xf[:, q, :], col(j - 1, D_AT), p_y[:, :], ALU.mult, ALU.add)\
                        .then_inc(S["y_skip"], 1)
                    dve.wait_ge(S["y_skip"], START["y_skip"] + g)
                    dve.wait_ge(S["y_sq"], START["y_sq"] + g - 2)
                    v.tensor_tensor(y[:, q, :], yt[:, :], gs[:, q, :], ALU.mult).then_inc(S["y_done"], 1)

            norm(0)
            v.memset(xt[:, :, :], 0.0).then_inc(S["aneg_done"], 1)
            with dve.Fori(0, BATCH) as b:
                dve.wait_ge(S["dt_mm"], b + 1)
                v.tensor_scalar(z[:, :], p_turn[:, :], dtb[:, 0:1], None, ALU.add).then_inc(S["z_done"], 1)
                dve.wait_ge(S["z_done"], 2 * b + 1)
                v.scalar_tensor_tensor(zabs[:, :], z[:, :], -1.0, z[:, :], ALU.mult, ALU.max).then_inc(S["z_done"], 1)
                dve.wait_ge(S["dt_ln"], b + 1)
                v.scalar_tensor_tensor(dt_head[:, :], z[:, :], 0.0, zln[:, :], ALU.max, ALU.add)\
                    .then_inc(S["dt_plus"], 1)
                dve.wait_ge(S["dt_turned"], b + 1)
                v.tensor_copy(dt[:, :, :], p_y[:, :].rearrange("p (t h) -> p t h", t=TILES)[:, :, 0:HEADS])\
                    .then_inc(S["dt_done"], 1)
                dve.wait_ge(S["dt_done"], b + 1)
                v.tensor_tensor(at[:, :, :], dt[:, :, :], aneg[:, None, :].broadcast_to([P, TILES, HEADS]), ALU.mult)\
                    .then_inc(S["at_done"], 1)
                dve.wait_ge(S["at_split_hi"], b + 1)
                low(at_lo[:, :, :], at[:, :, :], at_hi[:, :, :]).then_inc(S["at_split_lo"], 1)
                moving(b, 0, 0)
                moving(b, 0, 1)
                for n, p in enumerate((p_hid, p_gate)):
                    dve.wait_ge(S["bc_tap0"], 2 * b + n + 1)
                    conv(bcacc[:, n, :], p, lambda i, n=n: bcc[:, n, i:i + 1], "bc_taps", (TAPS - 1) * (2 * b + n))
                with dve.Fori(0, TILES - 1) as t:
                    for n in range(UNITS_PER_TILE):
                        moving(b, t + 1, n)
                        segments(b, t, n)
                segments(b, TILES - 1, 0)
                segments(b, TILES - 1, 1)
                dve.wait_ge(S["seg_done"], START["seg_done"] + (b + 1) * TILES * UNITS_PER_TILE)

                slot(b, 0, 0, do_mid=False, finish=False)
                dve.wait_ge(S["g_mm"], b + 1)
                for hd in range(2):
                    v.tensor_tensor(gmask[:, :, hd, :], p_out[0][:, :].rearrange("p (t l) -> p t l", t=TILES),
                                    same[:, None, :].broadcast_to([P, TILES, P]), ALU.mult).then_inc(S["g_done"], 1)
                dve.wait_ge(S["g_done"], 2 * (b + 1))
                slot(b, 1, 1, finish=False)
                with dve.Fori(1, PAIRS // 2) as jj:
                    slot(b, 2 * jj, 0)
                    slot(b, 2 * jj + 1, 1)
                slot(b, PAIRS, 0, do_in=False)
                slot(b, PAIRS + 1, 1, do_in=False, do_mid=False)

                dve.wait_ge(S["ssq_mm"], START["ssq_mm"] + b + 1)
                v.tensor_scalar(ms, by_token(p_hid), 1.0 / INTER, EPS, ALU.mult, ALU.add).then_inc(S["ssq_var"], 1)
                dve.wait_ge(S["ssq_std"], b + 1)
                v.reciprocal(rinv, rms).then_inc(S["ssq_inv"], 1)
                dve.wait_ge(S["ssq_inv"], b + 1)
                v.tensor_tensor(rinv_diag.rearrange("p (t n) -> p t n", t=TILES), ident[:, None, :].broadcast_to([P, TILES, P]),
                                rinv[:, :, None].broadcast_to([P, TILES, P]), ALU.mult).then_inc(S["ssq_wide"], 1)
                dve.wait_ge(S["out_mm"], START["out_mm"] + (b + 1) * PAIRS)
                for k in range(KE):
                    v.tensor_scalar(attn[:, k, :], p_out[k][:, :], modcol(2, k, b), None, ALU.mult)\
                        .then_inc(S["attn_scaled"], 1)
                dve.wait_ge(S["rinv_mm"], b + 1)
                dve.wait_ge(S["attn_scaled"], (2 * b + 1) * KE)
                for k in range(KE):
                    v.tensor_tensor(attn[:, k, :], attn[:, k, :], p_gate[:, :], ALU.mult).then_inc(S["attn_scaled"], 1)
                dve.wait_ge(S["attn_scaled"], (2 * b + 2) * KE)
                for k in range(KE):
                    xs = x_all[:, k, bass.ds(b * SEQ, SEQ)]
                    v.tensor_tensor(xs, attn[:, k, :], xs, ALU.add)\
                        .then_inc(S["attn_res"], 1)
            dve.wait_ge(S["attn_res"], START["attn_res"] + BATCH * KE)
            norm(1)
            v.memset(no[:, :], 0).then_inc(S["setup_raw"], 3)
            dve.wait_ge(S["setup_hi"], 6)
            for dst, src, hi in ((shw_lo, shw, shw_hi), (shd_lo, shd, shd_hi)):
                low(dst[:], src[:], hi[:]).then_inc(S["setup_lo"], 1)

            chain = [0]

            def step(i):
                i.then_inc(S["router_chain"], 1)
                chain[0] = chain[0] + 1
                dve.wait_ge(S["router_chain"], chain[0])

            def wide(a):
                return a[:, :, None].broadcast_to([P, GTILES, EXPERTS])

            dve.wait_ge(S["logit"], 1)
            logits = [p[:, :].rearrange("p (t e) -> p t e", t=8) for p in p_logit]
            for n in range(2):
                i = v.tensor_reduce(lmax[:, 8 * n:8 * n + 8], logits[n], AX_X, ALU.max)
            step(i)
            for n in range(2):
                v.tensor_tensor(lsub[:, 8 * n:8 * n + 8, :], logits[n],
                                lmax[:, 8 * n:8 * n + 8, None].broadcast_to([P, 8, EXPERTS]), ALU.subtract)\
                    .then_inc(S["lsub_done"], 1)
            dve.wait_ge(S["lexp_done"], 1)
            step(v.tensor_reduce(lsum[:, :], lexp[:, :, :], AX_X, ALU.add))
            step(v.reciprocal(lrec[:, :], lsum[:, :]))
            step(v.tensor_tensor(prob[:, :, :], lexp[:, :, :], wide(lrec), ALU.mult))
            for t in range(GTILES):
                i = v.max(top8[:, t, :], prob[:, t, :])
            step(i)
            step(v.memset(top8[:, :, TOP_K:], TINY))
            for t in range(GTILES):
                i = v.match_replace(rest[:, t, :], top8[:, t, :], prob[:, t, :], TINY)
            step(i)
            v.tensor_scalar(taken_r[:, :, :], rest[:, :, :], 0.0, None, ALU.is_lt).then_inc(S["taken"], 1)

            route = [0]

            def link(i):
                i.then_inc(S["route_chain"], 1)
                route[0] = route[0] + 1
                dve.wait_ge(S["route_chain"], route[0])

            taken = taken_r[:, :, :].bitcast(F32)
            dve.wait_ge(S["taken"], 1)
            v.tensor_copy(sum2[:, 0:1, :], taken[:, 0:1, :])
            link(v.tensor_tensor(sum2[:, 1:, :], taken[:, 1:, :], taken[:, 0:GTILES - 1, :], ALU.add))
            v.tensor_copy(sum4[:, 0:2, :], sum2[:, 0:2, :])
            link(v.tensor_tensor(sum4[:, 2:, :], sum2[:, 2:, :], sum2[:, 0:GTILES - 2, :], ALU.add))
            v.tensor_copy(sum8[:, 0:4, :], sum4[:, 0:4, :]).then_inc(S["sum8"], 1)
            v.tensor_tensor(sum8[:, 4:, :], sum4[:, 4:, :], sum4[:, 0:GTILES - 4, :], ALU.add).then_inc(S["sum8"], 1)
            dve.wait_ge(S["sum8"], 2)
            v.memset(earlier[:, 0:1, :], 0.0).then_inc(S["earlier"], 1)
            v.tensor_copy(earlier[:, 1:9, :], sum8[:, 0:8, :]).then_inc(S["earlier"], 1)
            v.tensor_tensor(earlier[:, 9:, :], sum8[:, 8:GTILES - 1, :], sum8[:, 0:7, :], ALU.add)\
                .then_inc(S["earlier"], 1)
            dve.wait_ge(S["count_mm"], 1)
            link(v.tensor_copy(count[0:EXPERTS, :], p_count[0:EXPERTS, 0:1]))
            link(v.tensor_scalar(over[0:EXPERTS, :], steps_of_p[0:EXPERTS, :], count[0:EXPERTS, 0:1], None, ALU.is_lt))
            link(v.tensor_reduce(tiles_of[0:EXPERTS, :], over[0:EXPERTS, :], AX_X, ALU.add))
            v.tensor_scalar(tiles_row[0:EXPERTS, :], ones[0:EXPERTS, :], tiles_of[0:EXPERTS, 0:1], None, ALU.mult)\
                .then_inc(S["tiles_done"], 1)
            dve.wait_ge(S["offset_mm"], 1)
            v.tensor_copy(offset[:, :], p_offset[:, 0:EXPERTS])
            link(v.tensor_copy(last_of[0:EXPERTS, :], p_offset[0:EXPERTS, EXPERTS:EXPERTS + 1]))
            v.tensor_scalar(passed[0:EXPERTS, :], tile_no[0:EXPERTS, :], last_of[0:EXPERTS, 0:1], None, ALU.is_ge)\
                .then_inc(S["passed"], 1)
            dve.wait_ge(S["rank_mm"], 1)
            for n in range(2):
                i = v.scalar_tensor_tensor(pos[:, 8 * n:8 * n + 8, :], offset[:, None, :].broadcast_to([P, 8, EXPERTS]),
                                           float(P), p_rank[n][:, :].rearrange("p (t e) -> p t e", t=8), ALU.mult, ALU.add)
            link(i)
            link(v.scalar_tensor_tensor(key[:, :, :], pos[:, :, :], 1.0, taken_r[:, :, :].bitcast(F32), ALU.add, ALU.mult))
            for g in range(GTILES):
                i = v.max(key8[:, g, :], key[:, g, :])
            link(i)
            v.tensor_scalar(rows6[:, :, :], key8[:, :, 0:TOP_K], -1.0, None, ALU.add).then_inc(S["rows_done"], 1)
            dve.wait_ge(S["owner_mm"], 1)
            v.tensor_scalar(owner_no[:, :], p_owner[:, 0:ETILES], float(EXPERTS - 1), None, ALU.min).then_inc(S["owners"], 1)

            step(v.scalar_tensor_tensor(kept[:, :, :], rest[:, :, :], 0.0, prob[:, :, :], ALU.max, ALU.subtract))
            step(v.tensor_reduce(ksum[:, :], kept[:, :, :], AX_X, ALU.add))
            step(v.reciprocal(krec[:, :], ksum[:, :]))
            v.tensor_tensor(shares[:, :, :], kept[:, :, :], wide(krec), ALU.mult)\
                .then_inc(S["shares"], 1)

            def unit(u, q, rows=P):
                dve.wait_ge(S["inner_silu"], u + 1)
                dve.wait_ge(S["hw_hi"], START["hw_hi"] + u - 1)
                v.tensor_tensor(hw[0:rows, q, :], hs[0:rows, q, :], p_up[q][0:rows, :], ALU.mult)\
                    .then_inc(S["prod"], 1)
                dve.wait_ge(S["hw_hi"], START["hw_hi"] + u + 1)
                dve.wait_ge(S["expert_mm"], START["expert_mm"] + u - 1)
                low(hw_lo[0:rows, q, :], hw[0:rows, q, :], hw_hi[0:rows, q, :]).then_inc(S["weighted"], 1)

            with dve.Fori(0, HALVES) as hf:
                for u in range(UNITS):
                    unit(hf * UNITS + u, u % BPH, min(P, SHARED_INNER - u // BPH * P))
                dve.wait_ge(S["expert_mm"], START["expert_mm"] + (hf + 1) * UNITS)
                for q in range(BPH):
                    b = hf * BPH + q
                    for k in range(KE):
                        xs = x_all[:, k, bass.ds(b * SEQ, SEQ)]
                        v.scalar_tensor_tensor(xs, p_moe[q * KE + k][:, :], modcol(5, k, b), xs, ALU.mult, ALU.add)\
                            .then_inc(S["result"], 1)

            dve.wait_ge(S["shares"], 1)
            for k in range(TOP_K):
                if k:
                    dve.wait_ge(S["share_chain"], 3 * k)
                v.tensor_tensor(same_key[:, :, :], key[:, :, :], key8[:, :, k:k + 1].broadcast_to([P, GTILES, EXPERTS]),
                                ALU.is_equal).then_inc(S["share_chain"], 1)
                dve.wait_ge(S["share_chain"], 3 * k + 1)
                v.tensor_tensor(same_key[:, :, :], same_key[:, :, :], shares[:, :, :], ALU.mult).then_inc(S["share_chain"], 1)
                dve.wait_ge(S["share_chain"], 3 * k + 2)
                v.tensor_reduce(share6[:, :, k], same_key[:, :, :], AX_X, ALU.add).then_inc(S["share_chain"], 1)

            def rows_in(n, r):
                dve.wait_ge(S["x_hi"], DEEP * n + r + 1)
                low(xe_lo[:, r, :], p_x[r % 2][:, 0:EMB], xe_hi[:, r, :]).then_inc(S["x_lo"], 1)

            def second_weights(n, r):
                dve.wait_ge(S["w_hi"], DEEP * n + r + 1)
                w = slice(W1_COLS, ECOLS)
                low(ew_lo[:, r, w], ew[:, r, w], ew_hi[:, r, w]).then_inc(S["w2_lo"], 1)

            def row_out(n, r):
                i_ = DEEP * n + r
                dve.wait_ge(S["second_mm"], START["second_mm"] + i_ + 1)
                dve.wait_ge(S[f"row_out{r // 2}"], START["row_out0"] + 16 * n)
                v.tensor_copy(y_rows[:, r, :], p_row[r % 2][:, 0:EMB]).then_inc(S["row_done"], 1)

            def step(n, r, before_it=True, ahead=True, ahead2=True):
                if ahead2:
                    rows_in(n + (r + 2) // DEEP, (r + 2) % DEEP)
                dve.wait_ge(S["hid_hi"], DEEP * n + r + 1)
                low(hid_lo[0:IHALF, r % 2, :], hid[0:IHALF, r % 2, :], hid_hi[0:IHALF, r % 2, :]).then_inc(S["hid_lo"], 1)
                if ahead:
                    second_weights(n + (r + 1) // DEEP, (r + 1) % DEEP)
                if before_it:
                    row_out(n - 1 if r == 0 else n, (r - 1) % DEEP)

            rows_in(0, 0)
            rows_in(0, 1)
            second_weights(0, 0)
            for r in range(DEEP):
                step(0, r, before_it=r > 0)
            with dve.Fori(1, ETILES // DEEP - 1) as n:
                for r in range(DEEP):
                    step(n, r)
            for r in range(DEEP):
                step(ETILES // DEEP - 1, r, ahead=r < DEEP - 1, ahead2=r < DEEP - 2)
            row_out(ETILES // DEEP - 1, DEEP - 1)

            dve.wait_ge(S["share_chain"], 3 * TOP_K)
            with dve.Fori(0, BATCH) as b:
                for t in range(TILES):
                    g = b * TILES + t
                    done = START["acc_chain"] + TOP_K * g
                    a = acc_rows[:, t % 2, :]
                    share_of = share6[:, :, :].rearrange("p t k -> p (t k)")
                    dve.wait_ge(S[f"got{t % 2}"], 16 * TOP_K * (2 * b + t // 2 + 1))
                    dve.wait_ge(S["acc_turned"], START["acc_turned"] + g - 1)
                    v.tensor_scalar(a, got[:, t % 2, 0, :], share_of[:, bass.ds(g * TOP_K, 1)], None, ALU.mult)\
                        .then_inc(S["acc_chain"], 1)
                    for k in range(1, TOP_K):
                        dve.wait_ge(S["acc_chain"], done + k)
                        v.scalar_tensor_tensor(a, got[:, t % 2, k, :], share_of[:, bass.ds(g * TOP_K + k, 1)], a,
                                               ALU.mult, ALU.add).then_inc(S["acc_chain"], 1)
                    dve.wait_ge(S["acc_turned"], START["acc_turned"] + g + 1)
                    for k in range(KE):
                        xs = x_all[:, k, bass.ds(g * P, P)]
                        v.scalar_tensor_tensor(xs, p_x[t % 2][:, k * P:(k + 1) * P], modcol(5, k, b), xs, ALU.mult, ALU.add)\
                            .then_inc(S["final"], 1)

        @block.gpsimd
        def _(pool):
            g_ = nc.gpsimd

            def low(dst, src, hi):
                return g_.tensor_tensor(dst, src, hi.bitcast(F32), ALU.subtract)

            def take_in(b, j, par):
                g = b * PAIRS + j
                pool.wait_ge(S["wi_hi"], g + 1)
                low(wi_lo[:, par, :], wi[:, par, :], wi_hi[:, par, :]).then_inc(S["wi_lo"], 1)

            def slot(b, j, par, next_in=True, take_out=True, finish=True):
                g = b * PAIRS + j
                if finish:
                    pool.wait_ge(S["y_sq"], START["y_sq"] + g - 1)
                    pool.wait_ge(S["ssq_done"], START["ssq_done"] + g - 2)
                    pool.wait_ge(S["ssq_zero"], b + 1)
                    g_.tensor_tensor(ssq[:, :], ssq[:, :], ysq[:, :], ALU.add).then_inc(S["ssq_done"], 1)
                if next_in:
                    take_in(b, j + 1, 1 - par)
                if take_out:
                    pool.wait_ge(S["wo_hi"], g)
                    low(wo_lo[:, 1 - par, :], wo[:, 1 - par, :], wo_hi[:, 1 - par, :]).then_inc(S["wo_lo"], 1)

            pool.wait_ge(S["normed_lo"], BATCH * KE)
            g_.memset(zero[:, :], 0.0).then_inc(S["zero_set"], 1)
            pool.wait_ge(S["zero_set"], 1)
            g_.memset(ssq[:, :], 0.0).then_inc(S["zero_set"], 1)
            pool.wait_ge(S["zero_set"], 2)
            with pool.Fori(0, BATCH) as b:
                pool.wait_ge(S["ssq_mm"], START["ssq_mm"] + b)
                zeros = zero[:, :].broadcast_to([P, SEQ])
                g_.tensor_tensor(ssq[:, :], zeros, zeros, ALU.add).then_inc(S["ssq_zero"], 1)
                with pool.Fori(0, TILES) as t:
                    for n in range(UNITS_PER_TILE):
                        r = (b * TILES + t) * UNITS_PER_TILE + n
                        pool.wait_ge(S["at_split_lo"], b + 1)
                        pool.wait_ge(S["mov_hi"], r + 1)
                        a = at_lo[:, :, :].bitcast(F32).rearrange("p t h -> p (t h)")[:, bass.ds(t * HEADS + n * HPU, HPU)]
                        g_.tensor_tensor(mov_lo[:, n, :].rearrange("p (h l) -> p h l", l=CHUNK),
                                         a[:, :, None].broadcast_to([P, HPU, CHUNK]),
                                         upto[:, None, :].broadcast_to([P, HPU, CHUNK]), ALU.mult)\
                            .then_inc(S["mov_lo"], 1)

                take_in(b, 0, 0)
                slot(b, 0, 0, take_out=False, finish=False)
                slot(b, 1, 1, finish=False)
                with pool.Fori(1, PAIRS // 2 - 1) as jj:
                    slot(b, 2 * jj, 0)
                    slot(b, 2 * jj + 1, 1)
                slot(b, PAIRS - 2, 0)
                slot(b, PAIRS - 1, 1, next_in=False)
                slot(b, PAIRS, 0, next_in=False)
                slot(b, PAIRS + 1, 1, next_in=False, take_out=False)

            def pass_by():
                return g_.tensor_tensor(passing[:, :], no[:, 0:1], no[:, 0:1], ALU.add)

            def row_numbers(g, par):
                g_.tensor_tensor(row_at[:, par, :], rows6[:, :, :].rearrange("p t k -> p (t k)")[:, bass.ds(g * TOP_K, TOP_K)],
                                 no[:, 0:TOP_K], ALU.add).then_inc(S["row_at"], 1)

            pool.wait_ge(S["h_copied"], BATCH)
            pool.wait_ge(S["xs_zero"], 16 * BATCH * PAIRS // 2)
            pool.wait_ge(S["rows_done"], 1)
            def send(g, use, par):
                if use is not None:
                    pool.wait_ge(S[f"sent{par}"], 16 * TOP_K * use)
                h_tile = ht[:, :, :].rearrange("p t n -> p (t n)")[:, bass.ds(g * EMB, EMB)]
                g_.tensor_tensor(h_send[:, par, :].rearrange("p (k n) -> p k n", k=KE), h_tile.rearrange("p (k n) -> p k n", k=KE),
                                 ones[:, None, :].broadcast_to([P, KE, P]), ALU.mult).then_inc(S["row_at"], 1)
                row_numbers(g, par)
                pool.wait_ge(S["row_at"], 3 * g + 2)
                pass_by().then_inc(S["row_at"], 1)
                for k in range(TOP_K):
                    g_.indirect_dma_start(grouped_rows, bass.IndirectOffsetOnAxis(row_at[:, par, k:k + 1], 0),
                                          h_send[:, par, :], None).then_inc(S[f"sent{par}"], 16)

            send(0, None, 0)
            send(1, None, 1)
            with pool.Fori(1, GTILES // 2) as n:
                send(2 * n, n, 0)
                send(2 * n + 1, n, 1)

            def load_rows(n, h):
                pool.wait_ge(S["x_turned"], START["x_turned"] + DEEP * n + 2 * h - 2)
                pool.dma_start(x_rows[:, 2 * h:2 * h + 2, :], tile_pair(grouped_rows, n, h)).then_inc(S[f"x_in{h}"], 16)

            def take(n, r, more=True):
                pool.wait_ge(S["w_hi"], DEEP * n + r + 1)
                w = slice(0, W1_COLS)
                low(ew_lo[:, r, w], ew[:, r, w], ew_hi[:, r, w]).then_inc(S["w_lo"], 1)
                if more and r % 2 == 0:
                    load_rows(n + 1, r // 2)

            pool.wait_ge(S["sent0"], 8 * GTILES * TOP_K)
            pool.wait_ge(S["sent1"], 8 * GTILES * TOP_K)
            load_rows(0, 0)
            load_rows(0, 1)
            with pool.Fori(0, ETILES // DEEP - 1) as n:
                for r in range(DEEP):
                    take(n, r)
            for r in range(DEEP):
                take(ETILES // DEEP - 1, r, more=False)

            pool.wait_ge(S["row_out0"], START["row_out0"] + 16 * ETILES // DEEP)
            pool.wait_ge(S["row_out1"], START["row_out1"] + 16 * ETILES // DEEP)
            with pool.Fori(0, BATCH) as b:
                for t in range(TILES):
                    g = b * TILES + t
                    pool.wait_ge(S["acc_chain"], START["acc_chain"] + TOP_K * (g - 1))
                    row_numbers(g, t % 2)
                    pool.wait_ge(S["row_at"], 3 * GTILES + 2 * g + 1)
                    pass_by().then_inc(S["row_at"], 1)
                    for k in range(TOP_K):
                        g_.indirect_dma_start(got[:, t % 2, k, :], None, outputs,
                                              bass.IndirectOffsetOnAxis(row_at[:, t % 2, k:k + 1], 0))\
                            .then_inc(S[f"got{t % 2}"], 16)


def kernel(L0_attn_input_states, L0_attn_mask, L0_attn_W_in, L0_attn_conv_w, L0_attn_conv_b, L0_attn_dt_bias,
           L0_attn_A_log, L0_attn_D, L0_attn_norm_w, L0_attn_W_out, L0_ffn_gate_w, L0_ffn_experts_w1,
           L0_ffn_experts_w2, L0_ffn_shared_gate_up, L0_ffn_shared_down, L0_c, L0_wmod):
    import concourse.bacc as bacc
    from concourse.bass_utils import run_bass_kernel_spmd

    def rows(a):
        return a.reshape(-1, P, a.shape[1]).transpose(1, 0, 2)

    x, w_in = np.asarray(L0_attn_input_states), np.asarray(L0_attn_W_in)
    w_gate, w_hid = (w_in[n * INTER:(n + 1) * INTER].reshape(PAIRS, P, KE, P).transpose(0, 3, 2, 1)
                     .reshape(PAIRS, P, KE * P) for n in range(2))
    w_out = np.asarray(L0_attn_W_out).T.reshape(PAIRS, P, EMB)
    conv = np.concatenate([L0_attn_conv_w, np.asarray(L0_attn_conv_b)[:, None]], 1)
    scalars = np.concatenate([np.asarray(L0_attn_norm_w).reshape(PAIRS, P, 1),
                              np.repeat(L0_attn_D, HEAD_DIM).reshape(PAIRS, P, 1),
                              conv[:INTER].reshape(PAIRS, P, TAPS + 1)], 2)
    bc = w_in[2 * INTER:2 * INTER + 2 * STATE].reshape(2, P, KE, P).transpose(3, 0, 2, 1)
    w1 = np.asarray(L0_ffn_experts_w1).reshape(EXPERTS, EXP_INNER, KE, P).transpose(0, 3, 2, 1).reshape(EXPERTS, P, -1)
    w2 = np.asarray(L0_ffn_experts_w2).transpose(0, 2, 1).reshape(EXPERTS, 2, IHALF, EMB).transpose(0, 2, 1, 3)
    w2 = np.pad(w2.reshape(EXPERTS, IHALF, -1), ((0, 0), (0, P - IHALF), (0, 0)))
    down = np.zeros((SH_CHUNKS * P, EMB), np.float32)
    down[:SHARED_INNER] = np.asarray(L0_ffn_shared_down).T
    arrays = {
        "x_t": rows(x.reshape(TOKENS, EMB).T),
        "in_w": np.concatenate([w_gate, w_hid], 2),
        "out_w": w_out,
        "scalars": scalars.transpose(1, 0, 2),
        "bc_w": bc,
        "bc_conv": conv[INTER:].reshape(2, P, TAPS + 1).transpose(1, 0, 2),
        "dt_w": rows(np.pad(w_in[2 * INTER + 2 * STATE:].T, ((0, 0), (0, P - HEADS)))),
        "dt_bias": np.pad(np.asarray(L0_attn_dt_bias), (0, P - HEADS))[:, None],
        "a_log": np.asarray(L0_attn_A_log),
        "c_t": rows(np.asarray(L0_c).T),
        "mod_w": rows(np.asarray(L0_wmod)),
        "gate_w": rows(np.asarray(L0_ffn_gate_w).T),
        "shared_w": rows(np.asarray(L0_ffn_shared_gate_up).T),
        "shared_d": rows(down),
        "expert_w": np.concatenate([w1, w2], 2),
        "const": constants(),
        "route_const": routing_constants(),
    }
    nc = bacc.Bacc("TRN2", target_bir_lowering=False, num_devices=1)
    arrays = {n: np.ascontiguousarray(a) for n, a in arrays.items()}
    args = [nc.dram_tensor(n, a.shape, F32, kind="ExternalInput").ap() for n, a in arrays.items()]
    out = nc.dram_tensor("out_t", (P, KE, TOKENS), F32, kind="ExternalOutput").ap()
    grouped = nc.dram_tensor("grouped", (EROWS * EMB,), F32).ap()
    outputs = nc.dram_tensor("outputs", (EROWS, EMB), F32).ap()
    program(nc, *args, grouped, outputs, out)
    got = run_bass_kernel_spmd(nc, [arrays], core_ids=[0]).results[0]["out_t"]
    return got.transpose(2, 1, 0).reshape(BATCH, SEQ, EMB)
```
